# Optimizing a Trainium2 kernel written in Bass

```python
import numpy as np
import jax
import jax.numpy as jnp

def _softmax(x, axis=-1):
    return jax.nn.softmax(x, axis=axis)

def _gelu(x):
    return jax.nn.gelu(x, approximate=True)

def _silu(x):
    return jax.nn.silu(x)

def _sigmoid(x):
    return jax.nn.sigmoid(x)

def _layernorm(x, axis=-1, eps=1e-05):
    m = jnp.mean(x, axis=axis, keepdims=True)
    v = jnp.var(x, axis=axis, keepdims=True)
    return (x - m) / jnp.sqrt(v + eps)

def _scatter_add(tgt, idx, src, axis=0):
    return tgt.at[idx].add(src)

def _segment_sum(src, seg, n):
    return jax.ops.segment_sum(src, seg, n)
kernel_name = 'mk_sandwich_d1_jaxref_r4_61a4e9'

def setup_inputs(seed: int=0):
    np.random.seed(seed)
    _w = jnp.asarray

    def _L0_attn_setup():
        import jax, jax.numpy as jnp
        import numpy as np
        from jax import lax
        D_MODEL, D_CONV, EXPAND = (256, 4, 2)
        D_INNER = D_MODEL * EXPAND
        B, N = (4, 512)
        key = jax.random.key(seed)
        ks = jax.random.split(key, 10)
        s = 0.02
        return {'x': jax.random.normal(ks[0], (B, N, D_MODEL), jnp.float32), 'W_in': jax.random.normal(ks[1], (D_MODEL, 2 * D_INNER), jnp.float32) * s, 'b_in': jnp.zeros((2 * D_INNER,), jnp.float32), 'conv_w': jax.random.normal(ks[2], (D_INNER, 1, D_CONV), jnp.float32) * 0.2, 'conv_b': jnp.zeros((D_INNER,), jnp.float32), 'W_bc': jax.random.normal(ks[3], (D_INNER, 2 * D_INNER), jnp.float32) * s, 'b_bc': jnp.zeros((2 * D_INNER,), jnp.float32), 'log_decay': jnp.zeros((D_INNER,), jnp.float32), 'W_out': jax.random.normal(ks[4], (D_INNER, D_MODEL), jnp.float32) * s, 'b_out': jnp.zeros((D_MODEL,), jnp.float32)}
    _L0_attn_in = _L0_attn_setup()

    def _L0_ffn_setup():
        import jax, jax.numpy as jnp
        import numpy as np
        B, S, D, H, F = (4, 1024, 256, 16, 1024)
        CAP = 0.125
        ROPE_BASE = 10000.0

        def rmsnorm(x, g):
            return x * jax.lax.rsqrt(jnp.mean(x * x, -1, keepdims=True) + 1e-06) * g

        def rope(t, pos):
            hd = t.shape[-1]
            inv = 1.0 / ROPE_BASE ** (jnp.arange(0, hd, 2, dtype=jnp.float32) / hd)
            f = pos[:, None, :, None].astype(jnp.float32) * inv
            emb = jnp.concatenate([f, f], axis=-1)
            cos, sin = (jnp.cos(emb), jnp.sin(emb))
            rot = jnp.concatenate([-t[..., hd // 2:], t[..., :hd // 2]], axis=-1)
            return t * cos + rot * sin
        key = jax.random.key(seed)
        ks = jax.random.split(key, 9)
        scale = 0.02
        x = jax.random.normal(ks[0], (B, S, D), jnp.float32)
        causal = jnp.where(jnp.tril(jnp.ones((S, S), bool)), 0.0, -1000000000.0).astype(jnp.float32)
        attention_mask = jnp.broadcast_to(causal[None, None], (B, 1, S, S))
        position_ids = jnp.broadcast_to(jnp.arange(S, dtype=jnp.int32), (B, S))
        return {'x': x, 'attention_mask': attention_mask, 'position_ids': position_ids, 'router_w': jax.random.normal(ks[1], (D, 1), jnp.float32) * scale, 'router_b': jnp.zeros((1,), jnp.float32), 'wq': jax.random.normal(ks[2], (D, D), jnp.float32) * scale, 'wk': jax.random.normal(ks[3], (D, D), jnp.float32) * scale, 'wv': jax.random.normal(ks[4], (D, D), jnp.float32) * scale, 'wo': jax.random.normal(ks[5], (D, D), jnp.float32) * scale, 'w1': jax.random.normal(ks[6], (D, F), jnp.float32) * scale, 'w2': jax.random.normal(ks[7], (F, D), jnp.float32) * scale, 'ln1': jnp.ones((D,), jnp.float32), 'ln2': jnp.ones((D,), jnp.float32)}
    _L0_ffn_in = _L0_ffn_setup()
    _d = {'L0_attn_x': _L0_attn_in['x'], 'L0_attn_W_in': _L0_attn_in['W_in'], 'L0_attn_b_in': _L0_attn_in['b_in'], 'L0_attn_conv_w': _L0_attn_in['conv_w'], 'L0_attn_conv_b': _L0_attn_in['conv_b'], 'L0_attn_W_bc': _L0_attn_in['W_bc'], 'L0_attn_b_bc': _L0_attn_in['b_bc'], 'L0_attn_log_decay': _L0_attn_in['log_decay'], 'L0_attn_W_out': _L0_attn_in['W_out'], 'L0_attn_b_out': _L0_attn_in['b_out'], 'L0_ffn_attention_mask': _L0_ffn_in['attention_mask'], 'L0_ffn_position_ids': _L0_ffn_in['position_ids'], 'L0_ffn_router_w': _L0_ffn_in['router_w'], 'L0_ffn_router_b': _L0_ffn_in['router_b'], 'L0_ffn_wq': _L0_ffn_in['wq'], 'L0_ffn_wk': _L0_ffn_in['wk'], 'L0_ffn_wv': _L0_ffn_in['wv'], 'L0_ffn_wo': _L0_ffn_in['wo'], 'L0_ffn_w1': _L0_ffn_in['w1'], 'L0_ffn_w2': _L0_ffn_in['w2'], 'L0_ffn_ln1': _L0_ffn_in['ln1'], 'L0_ffn_ln2': _L0_ffn_in['ln2']}
    _x0 = _d['L0_attn_x']
    _d['L0_attn_x'] = jax.random.normal(jax.random.fold_in(jax.random.key(seed), 1), (8, 512, 256), dtype=_x0.dtype)
    del _x0
    return _d

def reference(L0_attn_x, L0_attn_W_in, L0_attn_b_in, L0_attn_conv_w, L0_attn_conv_b, L0_attn_W_bc, L0_attn_b_bc, L0_attn_log_decay, L0_attn_W_out, L0_attn_b_out, L0_ffn_attention_mask, L0_ffn_position_ids, L0_ffn_router_w, L0_ffn_router_b, L0_ffn_wq, L0_ffn_wk, L0_ffn_wv, L0_ffn_wo, L0_ffn_w1, L0_ffn_w2, L0_ffn_ln1, L0_ffn_ln2):

    def _L0_attn_ref(x, W_in, b_in, conv_w, conv_b, W_bc, b_bc, log_decay, W_out, b_out):
        import jax, jax.numpy as jnp
        import numpy as np
        from jax import lax
        D_MODEL, D_CONV, EXPAND = (256, 4, 2)
        D_INNER = D_MODEL * EXPAND
        B, N = (4, 512)
        Bsz, Nlen, _ = x.shape
        d_inner = conv_w.shape[0]
        d_conv = conv_w.shape[-1]
        ug = x @ W_in + b_in
        u, gate = jnp.split(ug, 2, axis=-1)
        u_t = jnp.transpose(u, (0, 2, 1))
        u_conv = lax.conv_general_dilated(u_t, conv_w, window_strides=(1,), padding=[(d_conv - 1, 0)], dimension_numbers=('NCH', 'OIH', 'NCH'), feature_group_count=d_inner)
        u_conv = u_conv + conv_b[None, :, None]
        u_conv = jnp.transpose(u_conv, (0, 2, 1))
        u_conv = jax.nn.silu(u_conv)
        bc = u_conv @ W_bc + b_bc
        b, c = jnp.split(bc, 2, axis=-1)
        a = jnp.exp(-jax.nn.softplus(log_decay)).astype(x.dtype)

        def step(state, bc_t):
            b_t, c_t = bc_t
            state = state * a + b_t
            return (state, state * c_t)
        xs = (jnp.moveaxis(b, 1, 0), jnp.moveaxis(c, 1, 0))
        init = jnp.zeros((Bsz, d_inner), x.dtype)
        _, ys = lax.scan(step, init, xs)
        y = jnp.moveaxis(ys, 0, 1)
        y = y * jax.nn.sigmoid(gate)
        return y @ W_out + b_out

    def _L0_ffn_ref(x, attention_mask, position_ids, router_w, router_b, wq, wk, wv, wo, w1, w2, ln1, ln2):
        import jax, jax.numpy as jnp
        import numpy as np
        B, S, D, H, F = (4, 1024, 256, 16, 1024)
        CAP = 0.125
        ROPE_BASE = 10000.0

        def rmsnorm(x, g):
            return x * jax.lax.rsqrt(jnp.mean(x * x, -1, keepdims=True) + 1e-06) * g

        def rope(t, pos):
            hd = t.shape[-1]
            inv = 1.0 / ROPE_BASE ** (jnp.arange(0, hd, 2, dtype=jnp.float32) / hd)
            f = pos[:, None, :, None].astype(jnp.float32) * inv
            emb = jnp.concatenate([f, f], axis=-1)
            cos, sin = (jnp.cos(emb), jnp.sin(emb))
            rot = jnp.concatenate([-t[..., hd // 2:], t[..., :hd // 2]], axis=-1)
            return t * cos + rot * sin
        b, s, d = x.shape
        hd = d // H
        weights = (x @ router_w)[..., 0] + router_b[0]
        k = int(CAP * s)
        topv, topi = jax.lax.top_k(weights, k)
        thr = topv[:, -1]
        sel_mask = (weights > thr[:, None]).astype(x.dtype)
        kc = k - 1
        sel_idx = jnp.sort(topi[:, :kc], axis=1)
        bidx = jnp.arange(b)[:, None]
        x_sel = x[bidx, sel_idx]
        pos_sel = position_ids[bidx, sel_idx]
        w_sel = weights[bidx, sel_idx]
        m = attention_mask[:, 0]
        m_sel = m[bidx[:, :, None], sel_idx[:, :, None], sel_idx[:, None, :]]
        hn = rmsnorm(x_sel, ln1)

        def heads(t):
            return t.reshape(b, kc, H, hd).transpose(0, 2, 1, 3)
        q = rope(heads(hn @ wq), pos_sel)
        kk = rope(heads(hn @ wk), pos_sel)
        v = heads(hn @ wv)
        sc = jnp.einsum('bhqd,bhkd->bhqk', q, kk) / np.sqrt(hd).astype(np.float32)
        sc = sc + m_sel[:, None]
        a = jax.nn.softmax(sc, axis=-1)
        o = jnp.einsum('bhqk,bhkd->bhqd', a, v).transpose(0, 2, 1, 3).reshape(b, kc, d) @ wo
        x1 = x_sel + o
        x2 = x1 + jax.nn.gelu(rmsnorm(x1, ln2) @ w1) @ w2
        proc = x2 * w_sel[..., None]
        out = jnp.zeros_like(x).at[bidx, sel_idx].set(proc)
        return out + x * (1.0 - sel_mask)[..., None]
    x = L0_attn_x
    x = x + _layernorm(_L0_attn_ref(_layernorm(x, axis=-1), L0_attn_W_in, L0_attn_b_in, L0_attn_conv_w, L0_attn_conv_b, L0_attn_W_bc, L0_attn_b_bc, L0_attn_log_decay, L0_attn_W_out, L0_attn_b_out), axis=-1)
    x = x + _layernorm(_L0_ffn_ref(_layernorm(x, axis=-1), L0_ffn_attention_mask, L0_ffn_position_ids, L0_ffn_router_w, L0_ffn_router_b, L0_ffn_wq, L0_ffn_wk, L0_ffn_wv, L0_ffn_wo, L0_ffn_w1, L0_ffn_w2, L0_ffn_ln1, L0_ffn_ln2), axis=-1)
    return x

_drawn_inputs = setup_inputs


def setup_inputs(seed=0):
    import zlib

    import numpy as np

    out = dict(_drawn_inputs(seed))
    spreads = {'L0_attn_b_in': (0.0, 0.8),
     'L0_attn_conv_b': (0.0, 0.672),
     'L0_attn_b_bc': (0.0, 0.1),
     'L0_attn_log_decay': (0.0, 0.8),
     'L0_attn_b_out': (0.0, 0.1),
     'L0_ffn_ln1': (1.0, 0.6),
     'L0_ffn_ln2': (1.0, 0.6)}
    factors = {'L0_attn_W_in': 4.132,
     'L0_attn_conv_w': 4.21,
     'L0_attn_W_bc': 2.932,
     'L0_ffn_router_w': 3.19,
     'L0_ffn_wq': 8.0,
     'L0_ffn_wk': 8.0,
     'L0_ffn_wv': 4.85,
     'L0_ffn_wo': 5.066,
     'L0_ffn_w1': 3.573,
     'L0_ffn_w2': 3.52}
    for name, (base, spread) in spreads.items():
        noise = np.random.default_rng([zlib.crc32(name.encode()), seed]).standard_normal(out[name].shape)
        drawn = base * np.exp(spread * noise) if base else spread * noise
        out[name] = jnp.asarray(drawn.astype(out[name].dtype))
    for name, factor in factors.items():
        out[name] = (out[name] * factor).astype(out[name].dtype)
    return out
```

```python
from contextlib import ExitStack

import numpy as np
import concourse.bass as bass
from concourse import mybir

P = 128
NB, NT, D = 8, 512, 256
DI, TAPS = 512, 4
H, HD, F = 16, 16, 1024
NP_ROWS, S_TAB = 4, 1024
SLOTS = int(0.125 * NT)
KC = SLOTS - 1
TT = NT // P
KD, KI, KF = D // P, DI // P, F // P
PAIRS = NB // 2
HP = H // 2
VW = HD + 1

F32 = mybir.dt.float32
F32R = mybir.dt.float32r
BF16 = mybir.dt.bfloat16
I32 = mybir.dt.int32
U32 = mybir.dt.uint32
ALU = mybir.AluOpType
ACT = mybir.ActivationFunctionType
AX = mybir.AxisListType

C_W, C_UNSEL, C_COS, C_SIN, C_MROW, C_OROW = D, D + 1, D + 2, D + 10, D + 18, D + 19
PAY = D + 20
TCW = PAY - C_COS
HALF = HD // 2

K_ID, K_TRI, K_IOTA, K_INV, K_MROW, K_OROW, K_HEAD, K_SEL = 0, 128, 640, 704, 712, 744, 776, 784
K_ALL = 785
R_BIN, R_BBC, R_CB, R_LD, R_LN1, R_LN2, R_ALL = 0, 8, 16, 20, 24, 26, 28

TWO_PI = 2.0 * np.pi
PI_A = 6.28125
PI_B = float(np.float32(np.round((TWO_PI - PI_A) * 2**16) / 2**16))
PI_C = float(np.float32(np.round((TWO_PI - PI_A - PI_B) * 2**25) / 2**25))
PI_D = float(np.float32(TWO_PI - PI_A - PI_B - PI_C))
MAGIC = 1.5 * 2.0**23


def shape_constants():
    c = np.zeros((P, K_ALL), np.float32)
    c[:, K_ID:K_ID + P] = np.eye(P)
    c[:, K_TRI:K_TRI + NT] = np.arange(NT)[None] >= np.arange(P)[:, None]
    c[:, K_IOTA:K_IOTA + SLOTS] = np.arange(SLOTS)
    c[:, K_INV:K_INV + HALF] = np.float32(1.0) / np.float32(10000.0) ** (np.arange(0, HD, 2, dtype=np.float32) / np.float32(HD))
    for b in range(NB):
        for i in range(TT):
            tok = P * i + np.arange(P)
            c[:, K_MROW + TT * b + i] = 2 * (min(b, NP_ROWS - 1) * S_TAB + tok)
            c[:, K_OROW + TT * b + i] = b * NT + tok
    c[:, K_HEAD:K_HEAD + 8] = (np.arange(P)[:, None] // HD) == np.arange(8)
    c[:, K_SEL] = (np.arange(P) % SLOTS) < KC
    return c


class Signal:

    def __init__(self, sem, events):
        self.sem, self.n, self.index = sem, len(events), {e: k + 1 for k, e in enumerate(events)}

    def at(self, rep, event=None):
        return rep * self.n + (self.index[event] if event is not None else self.n)


def began(rep):
    return not isinstance(rep, int) or rep >= 0


def build(nc, x, W_in, b_in, conv_w, conv_b, W_bc, b_bc, log_decay, W_out, b_out, mask, pos, router_w,
          router_b, wq, wk, wv, wo, w1, w2, ln1, ln2, consts, out):
    ctx = ExitStack()
    with ctx:
        def sb(name, shape, dt=F32):
            return ctx.enter_context(nc.sbuf_tensor(name, [P] + list(shape), dt))

        def semaphore(name):
            return ctx.enter_context(nc.semaphore(name))

        def signal(name, events):
            return Signal(semaphore(name), events)

        WinH, WinL = sb("WinH", [KD, 2 * DI], F32R), sb("WinL", [KD, 2 * DI], F32R)
        WbcH, WbcL = sb("WbcH", [KI, 2 * DI], F32R), sb("WbcL", [KI, 2 * DI], F32R)
        WoutH, WoutL = sb("WoutH", [KI, D], F32R), sb("WoutL", [KI, D], F32R)
        Wqkv, Wo = sb("Wqkv", [KD, 3 * D]), sb("Wo", [KD, D])
        W1, W2 = sb("W1", [KD, F]), sb("W2", [KF, D])
        K = sb("K", [K_ALL])
        ident = K[:, K_ID:K_ID + P]
        cols = sb("cols", [R_ALL])
        convw = sb("convw", [KI, TAPS])
        rw, bout, rb = sb("rw", [D]), sb("bout", [D]), sb("rb", [1])
        decay, hbin, vbias = sb("decay", [KI]), sb("hbin", [KI]), sb("vbias", [KI])
        tokc = sb("tokc", [NB, TT, TCW])

        X = sb("X", [2, TT, D])
        LNH, LNL = sb("LNH", [KD, NT], F32R), sb("LNL", [KD, NT], F32R)
        U = sb("U", [2, TAPS - 1 + NT])
        V = sb("V", [2, NT])
        S = sb("S", [2, NT])
        SH, SL = sb("SH", [KI, NT], F32R), sb("SL", [KI, NT], F32R)
        G = sb("G", [KI, NT])
        Y = sb("Y", [2, NT])
        rows = Y[:, 0, 0:P]
        posi = Y[:, 0, P:2 * P].bitcast(I32)
        posf = Y[:, 0, 2 * P:3 * P]
        YH, YL = sb("YH", [KI, NT], F32R), sb("YL", [KI, NT], F32R)
        A = sb("A", [TT, D])
        HB = sb("HB", [TT, D])
        XR, junk = HB, HB[:, 0:2, :].rearrange("p i d -> p (i d)")
        pay = sb("pay", [2, TT, PAY])
        onehot = sb("onehot", [2, TT, SLOTS])
        tpos = sb("tpos", [NB * TT])
        stats, mv, ve, rs = sb("stats", [4, TT, 6]), sb("mv", [4, TT, 2]), sb("ve", [4, TT]), sb("rs", [4, TT])
        half = sb("half", [TT])
        nge, tie, rank = sb("nge", [TT]), sb("tie", [TT]), sb("rank", [TT])

        big = sb("big", [7168])
        used = [0]

        def carve(n):
            used[0] += n
            assert used[0] <= 7168
            return big[:, used[0] - n:used[0]]

        GS, MR, HS, HN = carve(PAY), carve(NT), carve(D), carve(D)
        HT = carve(D).rearrange("p (k n) -> p k n", k=KD)
        MT = carve(NT).rearrange("p (k n) -> p k n", k=TT)
        QK, RT = carve(2 * D), carve(2 * D)
        QT = carve(D).rearrange("p (k n) -> p k n", k=KD)
        KB0, SC, AT_ = carve(1024), carve(1024), carve(1024)
        VB = carve(2 * HP * 2 * VW).rearrange("p (q h e) -> p q h e", q=2, h=HP)
        MS = carve(SLOTS)
        KB = [KB0, AT_]
        AT = AT_.rearrange("p (h n) -> p h n", h=HP)
        HTT = AT_[:, 0:2 * D].rearrange("p (k q n) -> p k q n", k=KD, q=2)
        GE = KB0.rearrange("p (k n) -> p k n", k=KF)
        X1S, FS, OS = QK[:, 0:D], QK[:, D:2 * D], RT[:, 0:D]
        rawin = big[:, 0:2048].rearrange("p (k n) -> p k n", k=KD)
        rawbc = big[:, 2048:6144].rearrange("p (k n) -> p k n", k=KI)
        rawout = big[:, 6144:7168].rearrange("p (k n) -> p k n", k=KI)
        idx = sb("idx", [2], U32)
        bst, bmv, bve, brs, bss, bws = (sb("bst", [6]), sb("bmv", [2]), sb("bve", [1]), sb("brs", [1]),
                                        sb("bss", [1]), sb("bws", [1]))
        spare = sb("spare", [2])
        mx, rden = sb("mx", [H]), sb("rden", [H])
        bhalf = half[:, 0:1]
        ang = A[:, 0, :].rearrange("p (r f) -> p r f", f=HALF)
        trn = A[:, 1, :].rearrange("p (r f) -> p r f", f=HALF)
        red = A[:, 2, :].rearrange("p (r f) -> p r f", f=HALF)

        bank = [ctx.enter_context(nc.psum_tensor(f"bank{i}", [P, 512], F32)) for i in range(8)]
        TURN, B5, B6, B7 = bank[4], bank[5], bank[6], bank[7]

        s_k, s_vec, s_win, s_wbc, s_wout, s_wb = (semaphore(n) for n in (
            "consts_in", "vectors_in", "win_in", "wbc_in", "wout_in", "wb_in"))
        x_in, xr_in, out_stored, mask_in, scattered = (semaphore(n) for n in (
            "x_in", "xr_in", "out_stored", "mask_in", "scattered"))
        set_pe = signal("set_pe", ["vectors", "positions"])
        set_act = signal("set_act", ["win", "edecay", "hbin", "wbc", "wout", "sin", "cos"])
        set_dve = signal("set_dve", ["half", "pos", "cols", "pad", "win", "ed1", "decay", "vb1", "vbias", "wbc", "wout",
                                     "tokpos", "rows"] + [f"ang{i}" for i in range(17)]
                         + ["ln1a", "ln1b", "ln2a", "ln2b", "zero", "one0", "one1", "sczero"])
        T4, C4 = range(TT), range(KI)
        pre = signal("norm_x", [f"{k}{i}" for k in ("st", "ag") for i in T4] + ["ve"] + [f"ln{i}" for i in T4])
        roots = signal("roots", ["x"])
        roots_post = signal("roots_post", ["a", "x1", "h"])
        turned = signal("turned", ["t0", "t1"])
        ln_hi, ln_lo = signal("ln_hi", ["k0", "k1"]), signal("ln_lo", ["k0", "k1"])
        win = signal("win", [f"u{c}" for c in C4] + [f"g{c}" for c in C4])
        u_out = signal("u_out", [f"{k}{c}" for c in C4 for k in "uv"])
        g_out = signal("g_out", [f"g{c}" for c in C4])
        conv = signal("conv", [f"{c}{j}" for c in C4 for j in range(TAPS - 1)])
        tanh_v, silu = signal("tanh_v", [f"{c}" for c in C4]), signal("silu", [f"{c}" for c in C4])
        s_hi, s_lo = signal("s_hi", [f"{c}" for c in C4]), signal("s_lo", [f"{c}" for c in C4])
        wbc = signal("wbc", [f"{k}{c}" for c in C4 for k in "bc"])
        b_out_ = signal("b_out", [f"{c}" for c in C4])
        ssm = signal("ssm", [f"{k}{c}" for c in C4 for k in ("scan", "c", "y")])
        y_hi, y_lo = signal("y_hi", [f"{c}" for c in C4]), signal("y_lo", [f"{c}" for c in C4])
        wout = signal("wout", [f"{i}" for i in T4])
        post = signal("post", [f"a{i}" for i in T4] + [f"{k}{i}" for k in ("as", "aa") for i in T4] + ["ave"]
                      + [f"n{i}" for i in T4] + [f"{k}{i}" for k in ("xs", "xg") for i in T4] + ["xve"]
                      + [f"h{i}" for i in T4] + [f"w{i}" for i in T4] + ["wb"]
                      + [f"{k}{i}" for k in ("hs", "hg") for i in T4] + ["hve"] + [f"z{i}" for i in T4])
        x1_out = signal("x1_out", ["tokc", "x1", "out"])
        wrow = signal("wrow", [f"{i}" for i in T4])
        ranked = signal("ranked", [f"{k}{i}" for i in T4 for k in ("nge", "tie")] + ["rank", "unsel"]
                        + [f"hot{i}" for i in T4])
        bpe = signal("slots_pe", ["gather", "hnT", "maskT", "qk", "v", "mask", "qkT", "s0", "s1", "at0", "at1", "pv",
                                  "oT", "wo", "hn2T", "w1a", "w1b", "w2"])
        bact = signal("slots_act", ["gs", "hnT", "hnTT0", "hnTT1", "v00", "v01", "v10", "v11", "ms", "qT", "exp", "at0", "oT", "hn2T",
                                    "ge0", "ge1"])
        bdve = signal("slots_dve", ["idx", "st", "ag", "ve", "hs", "ss", "ssve", "hn", "mt", "r1", "r2", "r3", "q1",
                                    "q2", "kb0", "kb1", "sc0", "sc1", "max", "sub", "at1", "rden", "on", "x1s",
                                    "ss2", "ss2ve", "hn2", "x2", "ws", "ho", "f", "fst", "fag", "fve", "fn", "os"])
        bpool = signal("slots_roots", ["h", "hn", "hn2", "f"])

        x_rows = x.rearrange("b (i p) d -> b p i d", p=P)
        out_rows = out.rearrange("b (i p) d -> b p i d", p=P)
        mask_rows = mask.rearrange("b o s (h c) -> (b o s h) c", c=NT)
        out_flat = out.rearrange("b n d -> (b n) d")
        block = ctx.enter_context(nc.Block())

        ROW = [("into", 0), ("into", 1), ("tanh", 0), ("into", 2), ("hi", 0), ("tanh", 1), ("into", 3), ("hi", 1),
               ("tanh", 2), ("into", 4), ("hi", 2), ("tanh", 3), ("into", 5), ("hi", 3), ("into", 6), ("into", 7),
               ("pre", 0), ("out_of", 0), ("post_a", 0), ("b", 0), ("c", 0), ("turn", 0), ("post_n", 0), ("b", 1),
               ("yhi", 0), ("c", 1), ("turn", 1), ("post_x", 0), ("b", 2), ("yhi", 1), ("c", 2), ("post_h", 0),
               ("b", 3), ("yhi", 2), ("spread", 0), ("c", 3), ("yhi", 3), ("post_z", 0), ("rank", 0)]
        SLOT_STEPS = {("into", 0): (1,), ("into", 4): (2,), ("into", 6): (3,), ("out_of", 0): (4,), ("b", 0): (5,),
                      ("b", 1): (6,), ("c", 1): (7,), ("b", 2): (8,), ("c", 2): (9,), ("b", 3): (10,),
                      ("c", 3): (11,), ("rank", 0): (12, 13)}
        NEXT, BEFORE = ("pre", "turn"), ("out_of", "post_a", "post_n", "post_x", "post_h", "spread", "post_z", "rank")

        def run_row(do, t, q, r=None, first=False, last=False):
            for step in ROW:
                name, k = step
                if name in BEFORE:
                    if not first:
                        do(name, t - 1, 1 - q, k)
                elif name in NEXT:
                    if not last:
                        do(name, t + 1, 1 - q, k)
                else:
                    do(name, t, q, k)
                if r is not None:
                    for n in SLOT_STEPS.get(step, ()):
                        do("slots", r, 0, n)

        def run_all(eng, do):
            do("pre", 0, 0, 0)
            do("turn", 0, 0, 0)
            do("turn", 0, 0, 1)
            run_row(do, 0, 0, first=True)
            run_row(do, 1, 1)
            with eng.Fori(1, PAIRS - 1) as p:
                run_row(do, p * 2, 0)
                run_row(do, p * 2 + 1, 1, r=p - 1)
            run_row(do, NB - 2, 0)
            run_row(do, NB - 1, 1, r=PAIRS - 2, last=True)
            for name in BEFORE:
                do(name, NB - 1, 1, 0)
            for n in range(1, 14):
                do("slots", PAIRS - 1, 0, n)

        def is_row(t, n):
            return isinstance(t, int) and t == n

        @block.sync
        def _(sp):
            sp.dma_start(X[:, 0], x_rows[0]).then_inc(x_in, 16)
            sp.dma_start(K[:, :], consts).then_inc(s_k, 16)
            sp.dma_start(rawin, W_in.rearrange("(k p) n -> p k n", p=P)).then_inc(s_win, 16)
            for v, r, n in ((b_in, R_BIN, 8), (b_bc, R_BBC, 8), (conv_b, R_CB, 4), (log_decay, R_LD, 4),
                            (ln1, R_LN1, 2), (ln2, R_LN2, 2)):
                sp.dma_start(rows[r:r + n, :], v.rearrange("(r p) -> r p", p=P)).then_inc(s_vec, 16)
            sp.dma_start(posi[0:16, :], pos[:, 0:NT].rearrange("b (i p) -> b i p", p=P)).then_inc(s_vec, 16)
            sp.dma_start(convw[:, :, :], conv_w.rearrange("(c p) o j -> p c (o j)", p=P)).then_inc(s_vec, 16)
            sp.dma_start(rw[:, :], router_w.rearrange("d o -> o d").to_broadcast([P, D])).then_inc(s_vec, 16)
            sp.dma_start(bout[:, :], b_out.rearrange("(o d) -> o d", o=1).to_broadcast([P, D])).then_inc(s_vec, 16)
            sp.dma_start(rb[:, :], router_b.rearrange("(o d) -> o d", o=1).to_broadcast([P, 1])).then_inc(s_vec, 16)
            sp.dma_start(rawbc, W_bc.rearrange("(k p) n -> p k n", p=P)).then_inc(s_wbc, 16)
            sp.dma_start(rawout, W_out.rearrange("(k p) n -> p k n", p=P)).then_inc(s_wout, 16)
            sp.dma_start(X[:, 1], x_rows[1]).then_inc(x_in, 16)
            for j, w in enumerate((wq, wk, wv)):
                sp.dma_start(Wqkv[:, :, j * D:(j + 1) * D], w.rearrange("(k p) n -> p k n", p=P)).then_inc(s_wb, 16)
            sp.dma_start(Wo[:, :, :], wo.rearrange("(k p) n -> p k n", p=P)).then_inc(s_wb, 16)
            sp.dma_start(W1[:, :, :], w1.rearrange("(k p) n -> p k n", p=P)).then_inc(s_wb, 16)
            sp.dma_start(W2[:, :, :], w2.rearrange("(k p) n -> p k n", p=P)).then_inc(s_wb, 16)

            def residual(t):
                if began(t - 1):
                    sp.wait_ge(ranked.sem, ranked.at(t - 1))
                sp.dma_start(XR[:, :, :], x_rows[t]).then_inc(xr_in, 16)

            def next_x(t, q):
                if began(t - 2):
                    sp.wait_ge(turned.sem, turned.at(t - 2))
                sp.dma_start(X[:, q], x_rows[t]).then_inc(x_in, 16)

            def store(t):
                sp.wait_ge(x1_out.sem, x1_out.at(t, "out"))
                sp.dma_start(out_rows[t], A[:, :, :]).then_inc(out_stored, 16)

            residual(0)
            next_x(2, 0)
            store(0)
            residual(1)
            with sp.Fori(1, PAIRS - 1) as p:
                next_x(p * 2 + 1, 1)
                store(p * 2 - 1)
                residual(p * 2)
                next_x(p * 2 + 2, 0)
                store(p * 2)
                residual(p * 2 + 1)
            next_x(NB - 1, 1)
            store(NB - 3)
            residual(NB - 2)
            store(NB - 2)
            residual(NB - 1)
            store(NB - 1)
            sp.wait_ge(out_stored, 16 * NB)
            sp.wait_ge(scattered, 16 * PAIRS)

        @block.tensor
        def _(pe):
            def split_product(o, wh, wl, ah, al, n_k, w_cols, a_cols, done, weights_move):
                n = 0
                for k in range(n_k):
                    for w, a in ((wh, ah), (wh, al), (wl, ah)):
                        ws, as_ = w[:, k, w_cols], a[:, k, a_cols]
                        l, r = (as_, ws) if weights_move else (ws, as_)
                        mm = pe.matmul(o, l, r, start=(n == 0), stop=(n == 3 * n_k - 1))
                        n += 1
                mm.then_inc(done, 1)

            pe.wait_ge(s_k, 16)
            pe.wait_ge(s_vec, 16 * 11)
            pe.transpose(TURN[:, 0:R_ALL], rows[0:R_ALL, :], ident[0:R_ALL, 0:R_ALL]).then_inc(set_pe.sem, 1)
            pe.wait_ge(set_dve.sem, set_dve.at(0, "pos"))
            pe.transpose(TURN[:, 32:48], posf[0:16, :], ident[0:16, 0:16]).then_inc(set_pe.sem, 1)

            def turn(t, q, k):
                if k == 0:
                    pe.wait_ge(pre.sem, pre.at(t))
                    if is_row(t, 0):
                        pe.wait_ge(set_dve.sem, set_dve.at(0, "tokpos"))
                    if not is_row(t, 1):
                        if began(t - 3):
                            pe.wait_ge(ranked.sem, ranked.at(t - 3, "tie3"))
                    if began(t - 1):
                        pe.wait_ge(ln_lo.sem, ln_lo.at(t - 1))
                else:
                    pe.wait_ge(ln_hi.sem, ln_hi.at(t, "k0"))
                    pe.wait_ge(ln_lo.sem, ln_lo.at(t, "k0"))
                for i in T4:
                    mm = pe.transpose(TURN[:, i * P:(i + 1) * P], X[:, q, i, k * P:(k + 1) * P], ident)
                mm.then_inc(turned.sem, 1)

            def into(t, m):
                if m == 0:
                    pe.wait_ge(ln_hi.sem, ln_hi.at(t))
                    pe.wait_ge(ln_lo.sem, ln_lo.at(t))
                    if is_row(t, 0):
                        pe.wait_ge(set_dve.sem, set_dve.at(0, "win"))
                c = m % 4
                if m < 4:
                    if c % 2 == 0:
                        if began(t - 1):
                            pe.wait_ge(b_out_.sem, b_out_.at(t - 1, f"{2 + c // 2}"))
                    else:
                        if began(t - 1):
                            pe.wait_ge(ssm.sem, ssm.at(t - 1, f"c{2 + c // 2}"))
                else:
                    pe.wait_ge(u_out.sem, u_out.at(t, f"v{c}"))
                cols_ = slice((m * P), (m + 1) * P)
                split_product(bank[c][:, :], WinH, WinL, LNH, LNL, KD, cols_, slice(0, NT), win.sem, False)

            def out_of(t):
                pe.wait_ge(y_lo.sem, y_lo.at(t))
                for i in T4:
                    if i % 2 == 0:
                        if not is_row(t, NB - 1):
                            pe.wait_ge(g_out.sem, g_out.at(t + 1, f"g{i // 2}"))
                        else:
                            pe.wait_ge(ssm.sem, ssm.at(t, "c3"))
                            pe.wait_ge(b_out_.sem, b_out_.at(t))
                    split_product(bank[i // 2][:, (i % 2) * D:(i % 2 + 1) * D], WoutH, WoutL, YH, YL, KI,
                                  slice(0, D), slice(i * P, (i + 1) * P), wout.sem, True)

            def bc(t, c, j):
                if c == 0 and j == 0:
                    pe.wait_ge(s_hi.sem, s_hi.at(t))
                    pe.wait_ge(s_lo.sem, s_lo.at(t))
                    if is_row(t, 0):
                        pe.wait_ge(set_dve.sem, set_dve.at(0, "wbc"))
                b = 2 * (c % 2) + j
                if c == 0 and not is_row(t, 0):
                    if began(t - 1):
                        pe.wait_ge(post.sem, post.at(t - 1, "a3" if j else "a1"))
                elif c < 2:
                    pe.wait_ge(g_out.sem, g_out.at(t, f"g{b}"))
                elif j == 0:
                    pe.wait_ge(b_out_.sem, b_out_.at(t, f"{c - 2}"))
                else:
                    pe.wait_ge(ssm.sem, ssm.at(t, f"c{c - 2}"))
                m = 4 * j + c
                split_product(bank[b][:, :], WbcH, WbcL, SH, SL, KI, slice(m * P, (m + 1) * P),
                              slice(0, NT), wbc.sem, False)

            def spread(t, q):
                pe.wait_ge(post.sem, post.at(t, "wb"))
                if is_row(t, NB - 1) or is_row(t, NB - 2):
                    if began(t - 1):
                        pe.wait_ge(ranked.sem, ranked.at(t - 1))
                else:
                    pe.wait_ge(ln_lo.sem, ln_lo.at(t + 2))
                for i in T4:
                    pe.transpose(TURN[:, i * P:(i + 1) * P],
                                 pay[:, q, i, C_W:C_W + 1].to_broadcast([P, P]), ident).then_inc(wrow.sem, 1)

            half_rows = [slice(0, 64), slice(64, 128)]

            def b1(r):
                pe.wait_ge(x1_out.sem, x1_out.at(r * 2 + 1, "x1"))
                pe.wait_ge(ranked.sem, ranked.at(r * 2 + 1))
                for q in range(2):
                    for i in T4:
                        mm = pe.matmul(B5[half_rows[q], 0:PAY], onehot[:, q, i, :], pay[:, q, i, :],
                                       start=(i == 0), stop=(i == TT - 1))
                mm.then_inc(bpe.sem, 1)

            def b2(r):
                pe.wait_ge(bdve.sem, bdve.at(r, "hn"))
                for k in range(KD):
                    mm = pe.transpose(B6[:, k * P:(k + 1) * P], HN[:, k * P:(k + 1) * P], ident)
                mm.then_inc(bpe.sem, 1)
                pe.wait_ge(mask_in, r * 16 + 16)
                for k in T4:
                    mm = pe.transpose(B7[:, k * P:(k + 1) * P], MR[:, k * P:(k + 1) * P], ident)
                mm.then_inc(bpe.sem, 1)

            def b3(r):
                pe.wait_ge(bact.sem, bact.at(r, "hnTT1"))
                for k in range(KD):
                    mm = pe.matmul(B5[:, :], HT[:, k, :], Wqkv[:, k, 0:2 * D], start=(k == 0), stop=(k == KD - 1))
                mm.then_inc(bpe.sem, 1)
                for q in range(2):
                    for k in range(KD):
                        mm = pe.matmul(B6[:, q * D:(q + 1) * D], HTT[:, k, q, :], Wqkv[:, k, 2 * D:3 * D],
                                       start=(k == 0), stop=(k == KD - 1))
                mm.then_inc(bpe.sem, 1)
                pe.wait_ge(bdve.sem, bdve.at(r, "mt"))
                for q in range(2):
                    for k in T4:
                        mm = pe.matmul(B7[half_rows[q], 0:SLOTS], MT[:, k, half_rows[q]], onehot[:, q, k, :],
                                       start=(k == 0), stop=(k == TT - 1))
                mm.then_inc(bpe.sem, 1)

            def b4(r):
                pe.wait_ge(bdve.sem, bdve.at(r, "q2"))
                for k in range(4):
                    mm = pe.transpose(B5[:, k * P:(k + 1) * P], QK[:, k * P:(k + 1) * P], ident)
                mm.then_inc(bpe.sem, 1)

            def b5(r):
                pe.wait_ge(bact.sem, bact.at(r, "qT"))
                for g in range(2):
                    pe.wait_ge(bdve.sem, bdve.at(r, f"kb{g}"))
                    if g == 0:
                        pe.wait_ge(bact.sem, bact.at(r, "v11"))
                    else:
                        pe.wait_ge(bact.sem, bact.at(r, "ms"))
                    for q in range(2):
                        kb = KB[g].rearrange("p (q n) -> p q n", q=2)
                        mm = pe.matmul(bank[6 + g][half_rows[q], :], QT[:, g, half_rows[q]], kb[:, q, :],
                                       start=True, stop=True)
                    mm.then_inc(bpe.sem, 1)

            def b6(r):
                pe.wait_ge(bact.sem, bact.at(r, "exp"))
                for g in range(2):
                    for k in range(4):
                        hp = 4 * g + k
                        mm = pe.transpose(bank[6 + g][:, k * P:(k + 1) * P], SC[:, hp * P:(hp + 1) * P], ident)
                    mm.then_inc(bpe.sem, 1)

            def b7(r):
                pe.wait_ge(bact.sem, bact.at(r, "at0"))
                pe.wait_ge(bdve.sem, bdve.at(r, "at1"))
                for q in range(2):
                    for hp in range(HP):
                        mm = pe.matmul(B5[half_rows[q], hp * 2 * VW:(hp + 1) * 2 * VW], AT[:, hp, half_rows[q]],
                                       VB[:, q, hp, :], start=True, stop=True)
                mm.then_inc(bpe.sem, 1)

            def b8(r):
                pe.wait_ge(bdve.sem, bdve.at(r, "on"))
                for k in range(KD):
                    mm = pe.transpose(B6[:, k * P:(k + 1) * P], HN[:, k * P:(k + 1) * P], ident)
                mm.then_inc(bpe.sem, 1)

            def b9(r):
                pe.wait_ge(bact.sem, bact.at(r, "oT"))
                for k in range(KD):
                    mm = pe.matmul(B5[:, 0:D], HT[:, k, :], Wo[:, k, :], start=(k == 0), stop=(k == KD - 1))
                mm.then_inc(bpe.sem, 1)

            def b10(r):
                pe.wait_ge(bdve.sem, bdve.at(r, "hn2"))
                for k in range(KD):
                    mm = pe.transpose(B6[:, k * P:(k + 1) * P], HN[:, k * P:(k + 1) * P], ident)
                mm.then_inc(bpe.sem, 1)

            def b11(r):
                pe.wait_ge(bact.sem, bact.at(r, "hn2T"))
                for m in range(KF):
                    for k in range(KD):
                        mm = pe.matmul(bank[6 + m // 4][:, (m % 4) * P:(m % 4 + 1) * P], W1[:, k, m * P:(m + 1) * P],
                                       HT[:, k, :], start=(k == 0), stop=(k == KD - 1))
                    if m % 4 == 3:
                        mm.then_inc(bpe.sem, 1)

            def b12(r):
                pe.wait_ge(bact.sem, bact.at(r, "ge1"))
                for m in range(KF):
                    mm = pe.matmul(B5[:, 0:D], GE[:, m, :], W2[:, m, :], start=(m == 0), stop=(m == KF - 1))
                mm.then_inc(bpe.sem, 1)

            B = [b1, b2, b3, b4, b5, b6, b7, b8, b9, b10, b11, b12]

            def do(name, t, q, k):
                if name == "turn":
                    turn(t, q, k)
                elif name == "into":
                    into(t, k)
                elif name == "out_of":
                    out_of(t)
                elif name in "bc":
                    bc(t, k, "bc".index(name))
                elif name == "spread":
                    spread(t, q)
                elif name == "slots" and k <= len(B):
                    B[k - 1](t)

            run_all(pe, do)

        @block.scalar
        def _(act):
            act.wait_ge(s_win, 16)
            act.copy(WinH[:, :, :], rawin).then_inc(set_act.sem, 1)
            act.wait_ge(set_dve.sem, set_dve.at(0, "cols"))
            act.activation(decay[:, :], cols[:, R_LD:R_LD + KI], ACT.Exp).then_inc(set_act.sem, 1)
            act.mul(hbin[:, :], cols[:, R_BIN + KI:R_BIN + 2 * KI], 0.5).then_inc(set_act.sem, 1)
            act.wait_ge(s_wbc, 16)
            act.mul(WbcH[:, :, :], rawbc, 0.5).then_inc(set_act.sem, 1)
            act.wait_ge(s_wout, 16)
            act.mul(WoutH[:, :, :], rawout, 0.5).then_inc(set_act.sem, 1)
            flat = tokc[:, :, :, :].rearrange("p b i c -> p (b i) c")

            def trig():
                act.wait_ge(set_dve.sem, set_dve.at(0, "ang16"))
                act.activation(flat[:, :, HALF:2 * HALF], ang, ACT.Sin).then_inc(set_act.sem, 1)
                act.activation(flat[:, :, 0:HALF], red, ACT.Sin).then_inc(set_act.sem, 1)

            def turn(t, k):
                act.wait_ge(turned.sem, turned.at(t, f"t{k}"))
                if began(t - 1):
                    act.wait_ge(win.sem, win.at(t - 1))
                act.copy(LNH[:, k, :], TURN[:, :]).then_inc(ln_hi.sem, 1)

            def u(t, c):
                act.wait_ge(win.sem, win.at(t, f"u{c}"))
                if c < 2:
                    if began(t - 1):
                        act.wait_ge(conv.sem, conv.at(t - 1, f"{c + 2}2"))
                    if began(t - 1):
                        act.wait_ge(silu.sem, silu.at(t - 1, f"{c + 2}"))
                else:
                    act.wait_ge(conv.sem, conv.at(t, f"{c - 2}2"))
                    act.wait_ge(silu.sem, silu.at(t, f"{c - 2}"))
                if is_row(t, 0) and c == 0:
                    act.wait_ge(set_dve.sem, set_dve.at(0, "vbias"))
                act.activation(U[:, c % 2, TAPS - 1:], bank[c][:, :], ACT.Identity,
                               bias=cols[:, R_BIN + c:R_BIN + c + 1]).then_inc(u_out.sem, 1)
                act.activation(V[:, c % 2, :], bank[c][:, :], ACT.Identity, bias=vbias[:, c:c + 1],
                               scale=convw[:, c, TAPS - 1:TAPS]).then_inc(u_out.sem, 1)

            def tanhv(t, c):
                act.wait_ge(conv.sem, conv.at(t, f"{c}2"))
                if c >= 2:
                    act.wait_ge(s_lo.sem, s_lo.at(t, f"{c - 2}"))
                else:
                    if began(t - 1):
                        act.wait_ge(s_lo.sem, s_lo.at(t - 1, f"{c + 2}"))
                act.activation(S[:, c % 2, :], V[:, c % 2, :], ACT.Tanh, scale=0.5).then_inc(tanh_v.sem, 1)

            def shi(t, c):
                act.wait_ge(silu.sem, silu.at(t, f"{c}"))
                if began(t - 1):
                    act.wait_ge(wbc.sem, wbc.at(t - 1))
                act.copy(SH[:, c, :], S[:, c % 2, :]).then_inc(s_hi.sem, 1)

            def gate(t, c):
                act.wait_ge(win.sem, win.at(t, f"g{c}"))
                if began(t - 1):
                    act.wait_ge(ssm.sem, ssm.at(t - 1, f"y{c}"))
                act.activation(G[:, c, :], bank[c][:, :], ACT.Tanh, bias=hbin[:, c:c + 1],
                               scale=0.5).then_inc(g_out.sem, 1)

            def bout_(t, c):
                act.wait_ge(wbc.sem, wbc.at(t, f"b{c}"))
                if c >= 2:
                    act.wait_ge(y_lo.sem, y_lo.at(t, f"{c - 2}"))
                else:
                    if began(t - 1):
                        act.wait_ge(y_lo.sem, y_lo.at(t - 1, f"{c + 2}"))
                act.activation(Y[:, c % 2, :], bank[2 * (c % 2)][:, :], ACT.Identity,
                               bias=cols[:, R_BBC + c:R_BBC + c + 1]).then_inc(b_out_.sem, 1)

            def yhi(t, c):
                act.wait_ge(ssm.sem, ssm.at(t, f"y{c}"))
                if began(t - 1):
                    act.wait_ge(wout.sem, wout.at(t - 1))
                act.copy(YH[:, c, :], Y[:, c % 2, :]).then_inc(y_hi.sem, 1)

            def b1(r):
                act.wait_ge(bpe.sem, bpe.at(r, "gather"))
                act.copy(GS, B5[:, 0:PAY]).then_inc(bact.sem, 1)

            def b2(r):
                act.wait_ge(bpe.sem, bpe.at(r, "hnT"))
                act.copy(HT, B6[:, 0:D].rearrange("p (k n) -> p k n", k=KD)).then_inc(bact.sem, 1)

                for k in range(KD):
                    act.copy(HTT[:, k, :, :].rearrange("p q (e n) -> p q e n", e=2),
                             B6[:, k * P:(k + 1) * P].rearrange("p (q n) -> p q n", q=2).unsqueeze(2)
                             .to_broadcast([P, 2, 2, SLOTS])).then_inc(bact.sem, 1)

            def b3(r):
                act.wait_ge(bpe.sem, bpe.at(r, "v"))
                for q in range(2):
                    v = B6[:, q * D:(q + 1) * D].rearrange("p (h e d) -> p h e d", h=HP, e=2)
                    act.copy(VB[0:64, q, :, 0:HD], v[0:64, :, 0, :]).then_inc(bact.sem, 1)
                    act.copy(VB[64:128, q, :, VW:VW + HD], v[64:128, :, 1, :]).then_inc(bact.sem, 1)
                act.wait_ge(bpe.sem, bpe.at(r, "mask"))
                act.copy(MS, B7[:, 0:SLOTS]).then_inc(bact.sem, 1)

            def b4(r):
                act.wait_ge(bpe.sem, bpe.at(r, "qkT"))
                act.copy(QT, B5[:, 0:D].rearrange("p (k n) -> p k n", k=KD)).then_inc(bact.sem, 1)

            def b5(r):
                act.wait_ge(bdve.sem, bdve.at(r, "sub"))
                sc = SC.rearrange("p (h k) -> p h k", h=H)[:, :, 0:KC]
                act.activation(sc, sc, ACT.Exp).then_inc(bact.sem, 1)

            def b6(r):
                act.wait_ge(bpe.sem, bpe.at(r, "at0"))
                act.copy(AT[:, 0:4, :], B6[:, :].rearrange("p (h n) -> p h n", h=4)).then_inc(bact.sem, 1)

            def b7(r):
                act.wait_ge(bpe.sem, bpe.at(r, "oT"))
                act.copy(HT, B6[:, 0:D].rearrange("p (k n) -> p k n", k=KD)).then_inc(bact.sem, 1)

            def b8(r):
                act.wait_ge(bpe.sem, bpe.at(r, "hn2T"))
                act.copy(HT, B6[:, 0:D].rearrange("p (k n) -> p k n", k=KD)).then_inc(bact.sem, 1)

            def b9(r):
                for g in range(2):
                    act.wait_ge(bpe.sem, bpe.at(r, "w1a" if g == 0 else "w1b"))
                    act.activation(GE[:, 4 * g:4 * g + 4, :], bank[6 + g][:, :].rearrange("p (h n) -> p h n", h=4),
                                   ACT.Gelu_apprx_tanh).then_inc(bact.sem, 1)

            AT_STEP = {1: b1, 2: b2, 3: b3, 4: b4, 5: b5, 6: b6, 8: b7, 10: b8, 11: b9}

            def do(name, t, q, k):
                if name == "turn":
                    turn(t, k)
                    if is_row(t, 0) and k == 1:
                        trig()
                elif name == "into":
                    (u if k < 4 else gate)(t, k % 4)
                elif name == "tanh":
                    tanhv(t, k)
                elif name == "hi":
                    shi(t, k)
                elif name == "b":
                    bout_(t, k)
                elif name == "yhi":
                    yhi(t, k)
                elif name == "slots" and k in AT_STEP:
                    AT_STEP[k](t)

            run_all(act, do)

        @block.gpsimd
        def _(pool):
            def root(which, sig, rep, event, done):
                pool.wait_ge(sig.sem, sig.at(rep, event))
                pool.tensor_tensor(rs[:, which, :], ve[:, which, :], half[:, :], ALU.pow).then_inc(done.sem, 1)

            def slo(t, c):
                pool.wait_ge(s_hi.sem, s_hi.at(t, f"{c}"))
                pool.tensor_tensor(SL[:, c, :], S[:, c % 2, :], SH[:, c, :].bitcast(F32), ALU.subtract).then_inc(s_lo.sem, 1)

            def ylo(t, c):
                pool.wait_ge(y_hi.sem, y_hi.at(t, f"{c}"))
                pool.tensor_tensor(YL[:, c, :], Y[:, c % 2, :], YH[:, c, :].bitcast(F32), ALU.subtract).then_inc(y_lo.sem, 1)

            def post_a(t, q):
                if q == 0 and not is_row(t, 0):
                    if began((t // 2 if isinstance(t, int) else pair[0]) - 1):
                        pool.wait_ge(bpe.sem, bpe.at((t // 2 if isinstance(t, int) else pair[0]) - 1, "mask"))
                if is_row(t, 0):
                    pool.wait_ge(set_act.sem, set_act.at(0, "cos"))
                    pool.wait_ge(set_dve.sem, set_dve.at(0, "rows"))
                pool.tensor_copy(pay[:, q, :, C_COS:PAY], tokc[:, t, :, :]).then_inc(x1_out.sem, 1)
                root(1, post, t, "ave", roots_post)

            def post_n(t, q):
                pool.wait_ge(post.sem, post.at(t, "n3"))
                pool.wait_ge(xr_in, t * 16 + 16)
                pool.tensor_tensor(pay[:, q, :, 0:D], A[:, :, :], XR[:, :, :], ALU.add).then_inc(x1_out.sem, 1)

            def post_z(t, q):
                pool.wait_ge(post.sem, post.at(t, "z3"))
                pool.tensor_tensor(A[:, :, :], A[:, :, :], pay[:, q, :, 0:D], ALU.add).then_inc(x1_out.sem, 1)

            pair = [None]

            def broot(r, event):
                pool.wait_ge(bdve.sem, bdve.at(r, event))
                pool.tensor_tensor(brs[:, :], bve[:, :], bhalf, ALU.pow).then_inc(bpool.sem, 1)

            def b1(r):
                broot(r, "ve")
                pool.indirect_dma_start(MR, None, mask_rows,
                                        bass.IndirectOffsetOnAxis(ap=idx[:, 0:1], axis=0)).then_inc(mask_in, 16)
                broot(r, "ssve")

            def b13(r):
                broot(r, "fve")
                pool.wait_ge(bdve.sem, bdve.at(r, "os"))
                pool.wait_ge(out_stored, (r * 2 + 1) * 16 + 16)
                pool.tensor_tensor(spare[:, 1:2], bhalf, bhalf, ALU.mult)
                pool.indirect_dma_start(out_flat, bass.IndirectOffsetOnAxis(ap=idx[:, 1:2], axis=0),
                                        OS, None).then_inc(scattered, 16)
                pool.wait_ge(scattered, r * 16 + 16)

            def do(name, t, q, k):
                if name == "pre":
                    root(0, pre, t, "ve", roots)
                elif name == "hi":
                    slo(t, k)
                elif name == "yhi":
                    ylo(t, k)
                elif name == "post_a":
                    post_a(t, q)
                elif name == "post_n":
                    post_n(t, q)
                elif name == "post_x":
                    root(2, post, t, "xve", roots_post)
                elif name == "post_h":
                    root(3, post, t, "hve", roots_post)
                elif name == "post_z":
                    post_z(t, q)
                elif name == "slots":
                    if k == 1:
                        pair[0] = t + 1
                        b1(t)
                    elif k == 9:
                        broot(t, "ss2ve")
                    elif k == 13:
                        b13(t)

            pool.wait_ge(set_dve.sem, set_dve.at(0, "half"))
            run_all(pool, do)

        @block.vector
        def _(dve):
            n_set = [0]

            def setup(ins):
                n_set[0] += 1
                ins.then_inc(set_dve.sem, 1)
                dve.wait_ge(set_dve.sem, n_set[0])

            setup(dve.memset(half[:, :], -0.5))
            dve.wait_ge(s_vec, 16 * 11)
            setup(dve.tensor_copy(posf[0:16, :], posi[0:16, :]))

            def setup_rest():
                dve.wait_ge(set_pe.sem, set_pe.at(0))
                setup(dve.tensor_copy(cols[:, :], TURN[:, 0:R_ALL]))
                setup(dve.memset(U[:, :, 0:TAPS - 1], 0.0))
                dve.wait_ge(set_act.sem, set_act.at(0, "win"))
                setup(dve.tensor_tensor(WinL[:, :, :], rawin, WinH[:, :, :].bitcast(F32), ALU.subtract))
                dve.wait_ge(set_act.sem, set_act.at(0, "edecay"))
                setup(dve.tensor_scalar(decay[:, :], decay[:, :], 1.0, None, ALU.add))
                setup(dve.reciprocal(decay[:, :], decay[:, :]))
                setup(dve.tensor_tensor(vbias[:, :], cols[:, R_BIN:R_BIN + KI], convw[:, :, TAPS - 1], ALU.mult))
                setup(dve.tensor_tensor(vbias[:, :], vbias[:, :], cols[:, R_CB:R_CB + KI], ALU.add))
                dve.wait_ge(set_act.sem, set_act.at(0, "wbc"))
                setup(dve.scalar_tensor_tensor(WbcL[:, :, :].rearrange("p k n -> p (k n)"),
                                               big[:, 2048:6144], 0.5,
                                               WbcH[:, :, :].rearrange("p k n -> p (k n)").bitcast(F32),
                                               ALU.mult, ALU.subtract))
                dve.wait_ge(set_act.sem, set_act.at(0, "wout"))
                setup(dve.scalar_tensor_tensor(WoutL[:, :, :].rearrange("p k n -> p (k n)"),
                                               big[:, 6144:7168], 0.5,
                                               WoutH[:, :, :].rearrange("p k n -> p (k n)").bitcast(F32),
                                               ALU.mult, ALU.subtract))
                setup(dve.tensor_copy(tpos[:, 0:NP_ROWS * TT], TURN[:, 32:48]))

            def setup_tokens():
                last_row = tpos[:, (NP_ROWS - 1) * TT:NP_ROWS * TT].unsqueeze(1)
                rest = tpos[:, NP_ROWS * TT:].rearrange("p (b i) -> p b i", i=TT)
                setup(dve.tensor_copy(rest, last_row.to_broadcast([P, NB - NP_ROWS, TT])))
                pb = tpos[:, :].unsqueeze(2).to_broadcast([P, NB * TT, HALF])
                fb = K[:, K_INV:K_INV + HALF].unsqueeze(1).to_broadcast([P, NB * TT, HALF])
                setup(dve.tensor_tensor(ang, pb, fb, ALU.mult))
                for shift, dst in ((0.25, red), (0.0, ang)):
                    setup(dve.tensor_scalar(trn, ang, 1.0 / TWO_PI, shift, ALU.mult, ALU.add))
                    setup(dve.tensor_scalar(trn, trn, MAGIC, None, ALU.add))
                    setup(dve.tensor_scalar(trn, trn, MAGIC, None, ALU.subtract))
                    src = ang
                    for part in (PI_A, PI_B, PI_C, PI_D):
                        setup(dve.scalar_tensor_tensor(dst, trn, -part, src, ALU.mult, ALU.add))
                        src = dst
                setup(dve.tensor_scalar(red, red, float(np.pi / 2), None, ALU.add))
                setup(dve.tensor_copy(tokc[:, :, :, C_MROW - C_COS],
                                      K[:, K_MROW:K_MROW + NB * TT].rearrange("p (b i) -> p b i", i=TT)))
                setup(dve.tensor_copy(tokc[:, :, :, C_OROW - C_COS],
                                      K[:, K_OROW:K_OROW + NB * TT].rearrange("p (b i) -> p b i", i=TT)))
                dve.wait_ge(s_wb, 16 * 6)
                for k in range(KD):
                    setup(dve.tensor_scalar(Wqkv[:, k, :], Wqkv[:, k, :], cols[:, R_LN1 + k:R_LN1 + k + 1], None, ALU.mult))
                for k in range(KD):
                    setup(dve.tensor_scalar(W1[:, k, :], W1[:, k, :], cols[:, R_LN2 + k:R_LN2 + k + 1], None, ALU.mult))
                setup(dve.memset(VB, 0.0))
                setup(dve.memset(VB[0:64, :, :, HD:HD + 1], 1.0))
                setup(dve.memset(VB[64:128, :, :, VW + HD:VW + HD + 1], 1.0))
                setup(dve.memset(SC, 0.0))

            def carry():
                dve.memset(spare[:, 0:1], 0.0)

            def statistics(which, sig, t, tag, src, eps, name):
                for i in T4:
                    dve.bn_stats(stats[:, which, i, :], src(i)).then_inc(sig.sem, 1)
                dve.wait_ge(sig.sem, sig.at(t, f"{tag[0]}3"))
                carry()
                for i in T4:
                    dve.bn_aggr(mv[:, which, i, :], stats[:, which, i, :]).then_inc(sig.sem, 1)
                dve.wait_ge(sig.sem, sig.at(t, f"{tag[1]}3"))
                dve.tensor_scalar(ve[:, which, :], mv[:, which, :, 1], eps, None, ALU.add).then_inc(sig.sem, 1)

            def normalise(which, sig, dst, src):
                for i in T4:
                    dve.tensor_scalar(dst(i), src(i), mv[:, which, i, 0:1], rs[:, which, i:i + 1],
                                      ALU.subtract, ALU.mult).then_inc(sig.sem, 1)

            def norm_x(t, q):
                dve.wait_ge(x_in, t * 16 + 16)
                statistics(0, pre, t, ("st", "ag"), lambda i: X[:, q, i, :], 1e-5, "ve")
                dve.wait_ge(roots.sem, roots.at(t))
                normalise(0, pre, lambda i: X[:, q, i, :], lambda i: X[:, q, i, :])

            def turn(t, k):
                dve.wait_ge(ln_hi.sem, ln_hi.at(t, f"k{k}"))
                dve.tensor_tensor(LNL[:, k, :], TURN[:, :], LNH[:, k, :].bitcast(F32), ALU.subtract).then_inc(ln_lo.sem, 1)

            def convolve(t, c):
                for j in range(TAPS - 1):
                    if j == 0:
                        dve.wait_ge(u_out.sem, u_out.at(t, f"v{c}"))
                    else:
                        dve.wait_ge(conv.sem, conv.at(t, f"{c}{j - 1}"))
                    dve.scalar_tensor_tensor(V[:, c % 2, :], U[:, c % 2, j:j + NT], convw[:, c, j:j + 1],
                                             V[:, c % 2, :], ALU.mult, ALU.add).then_inc(conv.sem, 1)

            def silu_(t, c):
                dve.wait_ge(tanh_v.sem, tanh_v.at(t, f"{c}"))
                dve.scalar_tensor_tensor(S[:, c % 2, :], S[:, c % 2, :], 1.0, V[:, c % 2, :],
                                         ALU.add, ALU.mult).then_inc(silu.sem, 1)

            def scan(t, c):
                dve.wait_ge(b_out_.sem, b_out_.at(t, f"{c}"))
                dve.tensor_tensor_scan(Y[:, c % 2, :], decay[:, c:c + 1].to_broadcast([P, NT]), Y[:, c % 2, :], 0.0,
                                       ALU.mult, ALU.add).then_inc(ssm.sem, 1)

            def c_and_gate(t, c):
                dve.wait_ge(wbc.sem, wbc.at(t, f"c{c}"))
                dve.wait_ge(ssm.sem, ssm.at(t, f"scan{c}"))
                dve.scalar_tensor_tensor(Y[:, c % 2, :], bank[2 * (c % 2) + 1][:, :],
                                         cols[:, R_BBC + KI + c:R_BBC + KI + c + 1], Y[:, c % 2, :],
                                         ALU.add, ALU.mult).then_inc(ssm.sem, 1)
                dve.wait_ge(g_out.sem, g_out.at(t, f"g{c}"))
                dve.wait_ge(ssm.sem, ssm.at(t, f"c{c}"))
                dve.scalar_tensor_tensor(Y[:, c % 2, :], G[:, c, :], 1.0, Y[:, c % 2, :],
                                         ALU.add, ALU.mult).then_inc(ssm.sem, 1)

            def post_a(t):
                if is_row(t, 0):
                    dve.wait_ge(set_act.sem, set_act.at(0, "cos"))
                if began(t - 1):
                    dve.wait_ge(out_stored, (t - 1) * 16 + 16)
                for i in T4:
                    if i % 2 == 0:
                        dve.wait_ge(wout.sem, wout.at(t, f"{i + 1}"))
                    dve.tensor_tensor(A[:, i, :], bank[i // 2][:, (i % 2) * D:(i % 2 + 1) * D], bout[:, :],
                                      ALU.add).then_inc(post.sem, 1)
                dve.wait_ge(post.sem, post.at(t, "a3"))
                statistics(1, post, t, ("as", "aa"), lambda i: A[:, i, :], 1e-5, "ave")

            def post_n(t):
                dve.wait_ge(roots_post.sem, roots_post.at(t, "a"))
                normalise(1, post, lambda i: A[:, i, :], lambda i: A[:, i, :])

            def post_x(t, q):
                dve.wait_ge(x1_out.sem, x1_out.at(t, "x1"))
                statistics(2, post, t, ("xs", "xg"), lambda i: pay[:, q, i, 0:D], 1e-5, "xve")

            def post_h(t, q):
                dve.wait_ge(roots_post.sem, roots_post.at(t, "x1"))
                normalise(2, post, lambda i: HB[:, i, :], lambda i: pay[:, q, i, 0:D])
                for i in T4:
                    dve.wait_ge(post.sem, post.at(t, f"h{i}"))
                    dve.tensor_tensor_reduce(out=A[:, i, :], in0=HB[:, i, :], in1=rw[:, :], scale=1.0, scalar=0.0,
                                             op0=ALU.mult, op1=ALU.add, accum_out=rank[:, i:i + 1]).then_inc(post.sem, 1)
                dve.wait_ge(post.sem, post.at(t, "w3"))
                dve.tensor_scalar(pay[:, q, :, C_W], rank[:, :], rb[:, 0:1], None, ALU.add).then_inc(post.sem, 1)
                statistics(3, post, t, ("hs", "hg"), lambda i: HB[:, i, :], 1e-5, "hve")

            def post_z(t):
                dve.wait_ge(roots_post.sem, roots_post.at(t, "h"))
                normalise(3, post, lambda i: A[:, i, :], lambda i: HB[:, i, :])

            def rank_(t, q):
                w = lambda i: pay[:, q, i, C_W:C_W + 1]
                dve.wait_ge(wrow.sem, wrow.at(t))
                dve.wait_ge(post.sem, post.at(t))
                for i in T4:
                    if i:
                        dve.wait_ge(ranked.sem, ranked.at(t, f"tie{i - 1}"))
                    dve.tensor_scalar(junk[:, :], TURN[:, :], w(i), None, ALU.is_ge, ALU.add,
                                      accum_out=nge[:, i:i + 1]).then_inc(ranked.sem, 1)
                    dve.wait_ge(ranked.sem, ranked.at(t, f"nge{i}"))
                    n = NT - P * i
                    dve.scalar_tensor_tensor(junk[:, 0:n], TURN[:, P * i:NT], w(i), K[:, K_TRI:K_TRI + n],
                                             ALU.is_equal, ALU.mult, accum_out=tie[:, i:i + 1]).then_inc(ranked.sem, 1)
                dve.wait_ge(ranked.sem, ranked.at(t, "tie3"))
                dve.tensor_tensor(rank[:, :], nge[:, :], tie[:, :], ALU.subtract).then_inc(ranked.sem, 1)
                dve.tensor_scalar(pay[:, q, :, C_UNSEL], nge[:, :], float(KC), None, ALU.is_gt).then_inc(ranked.sem, 1)
                dve.wait_ge(ranked.sem, ranked.at(t, "rank"))
                for i in T4:
                    dve.tensor_scalar(onehot[:, q, i, :], K[:, K_IOTA:K_IOTA + SLOTS], rank[:, i:i + 1], None,
                                      ALU.is_equal).then_inc(ranked.sem, 1)

            def link(ins, r, event):
                ins.then_inc(bdve.sem, 1)
                dve.wait_ge(bdve.sem, bdve.at(r, event))

            def b1(r):
                dve.wait_ge(bact.sem, bact.at(r, "gs"))
                link(dve.tensor_copy(idx[:, :], GS[:, C_MROW:C_OROW + 1]), r, "idx")
                dve.bn_stats(bst[:, :], GS[:, 0:D]).then_inc(bdve.sem, 1)
                dve.wait_ge(bdve.sem, bdve.at(r, "st"))
                carry()
                link(dve.bn_aggr(bmv[:, :], bst[:, :]), r, "ag")
                link(dve.tensor_scalar(bve[:, :], bmv[:, 1:2], 1e-5, None, ALU.add), r, "ve")
                dve.wait_ge(bpool.sem, bpool.at(r, "h"))
                link(dve.tensor_scalar(HS, GS[:, 0:D], bmv[:, 0:1], brs[:, 0:1], ALU.subtract, ALU.mult), r, "hs")
                rms(r, HS, "ss", "hn")

            def rms(r, src, ss, hn):
                link(dve.tensor_tensor_reduce(out=HN, in0=src, in1=src, scale=1.0, scalar=0.0, op0=ALU.mult,
                                              op1=ALU.add, accum_out=bss[:, :]), r, ss)
                link(dve.tensor_scalar(bve[:, :], bss[:, :], 1.0 / D, 1e-6, ALU.mult, ALU.add), r, ss + "ve")
                dve.wait_ge(bpool.sem, bpool.at(r, hn))
                link(dve.tensor_scalar(HN, src, brs[:, 0:1], None, ALU.mult), r, hn)

            def b2(r):
                dve.wait_ge(bpe.sem, bpe.at(r, "maskT"))
                link(dve.tensor_copy(MT, B7[:, :].rearrange("p (k n) -> p k n", k=TT)), r, "mt")

            def b3(r):
                dve.wait_ge(bpe.sem, bpe.at(r, "qk"))
                x4 = B5[:, :].rearrange("p (h e f) -> p h e f", e=2, f=HALF)
                o4 = QK.rearrange("p (h e f) -> p h e f", e=2, f=HALF)
                r4 = RT.rearrange("p (h e f) -> p h e f", e=2, f=HALF)
                cos = GS[:, C_COS:C_COS + HALF]
                sin = GS[:, C_SIN:C_SIN + HALF].unsqueeze(1).to_broadcast([P, 2 * H, HALF])
                cos4 = cos.unsqueeze(1).unsqueeze(1).to_broadcast([P, 2 * H, 2, HALF])
                link(dve.tensor_tensor(o4, x4, cos4, ALU.mult), r, "r1")
                link(dve.tensor_tensor(r4[:, :, 0, :], x4[:, :, 1, :], sin, ALU.mult), r, "r2")
                link(dve.tensor_tensor(r4[:, :, 1, :], x4[:, :, 0, :], sin, ALU.mult), r, "r3")
                link(dve.tensor_tensor(o4[:, :, 0, :], o4[:, :, 0, :], r4[:, :, 0, :], ALU.subtract), r, "q1")
                link(dve.tensor_tensor(o4[:, :, 1, :], o4[:, :, 1, :], r4[:, :, 1, :], ALU.add), r, "q2")

            def b4(r):
                dve.wait_ge(bpe.sem, bpe.at(r, "qkT"))
                dve.wait_ge(bact.sem, bact.at(r, "qT"))
                head = K[:, K_HEAD:K_HEAD + 8].unsqueeze(1).unsqueeze(3).to_broadcast([P, 2, 8, SLOTS])
                for g in range(2):
                    kt = B5[:, (2 + g) * P:(3 + g) * P].rearrange("p (q n) -> p q n", q=2).unsqueeze(2) \
                        .to_broadcast([P, 2, 8, SLOTS])
                    dve.tensor_tensor(KB[g].rearrange("p (q h n) -> p q h n", q=2, h=8), kt, head,
                                      ALU.mult).then_inc(bdve.sem, 1)

            def b5(r):
                sc = SC.rearrange("p (h k) -> p h k", h=H)[:, :, 0:KC]
                dve.wait_ge(bact.sem, bact.at(r, "ms"))
                for g in range(2):
                    dve.wait_ge(bpe.sem, bpe.at(r, f"s{g}"))
                    s = bank[6 + g][:, :].rearrange("p (h k) -> p h k", h=8)[:, :, 0:KC]
                    m = MS[:, 0:KC].unsqueeze(1).to_broadcast([P, 8, KC])
                    dve.scalar_tensor_tensor(sc[:, 8 * g:8 * g + 8, :], s, HD ** -0.5, m, ALU.mult,
                                             ALU.add).then_inc(bdve.sem, 1)
                dve.wait_ge(bdve.sem, bdve.at(r, "sc1"))
                link(dve.tensor_reduce(mx[:, :], sc, AX.X, ALU.max), r, "max")
                link(dve.tensor_tensor(sc, sc, mx[:, :].unsqueeze(2).to_broadcast([P, H, KC]), ALU.subtract), r, "sub")

            def b6(r):
                dve.wait_ge(bpe.sem, bpe.at(r, "at1"))
                dve.tensor_copy(AT[:, 4:8, :], B7[:, :].rearrange("p (h n) -> p h n", h=4)).then_inc(bdve.sem, 1)

            def b7(r):
                dve.wait_ge(bpe.sem, bpe.at(r, "pv"))
                o = B5[:, 0:H * VW].rearrange("p (h e) -> p h e", e=VW)
                link(dve.reciprocal(rden[:, :], o[:, :, HD]), r, "rden")
                link(dve.tensor_tensor(HN.rearrange("p (h e) -> p h e", e=HD), o[:, :, 0:HD],
                                       rden[:, :].unsqueeze(2).to_broadcast([P, H, HD]), ALU.mult), r, "on")

            def b9(r):
                dve.wait_ge(bpe.sem, bpe.at(r, "wo"))
                link(dve.tensor_tensor(X1S, B5[:, 0:D], HS, ALU.add), r, "x1s")
                rms(r, X1S, "ss2", "hn2")

            def b12(r):
                dve.wait_ge(bpe.sem, bpe.at(r, "w2"))
                link(dve.tensor_tensor(X1S, B5[:, 0:D], X1S, ALU.add), r, "x2")
                link(dve.tensor_tensor(bws[:, :], GS[:, C_W:C_W + 1], K[:, K_SEL:K_SEL + 1], ALU.mult), r, "ws")
                link(dve.tensor_scalar(FS, HS, GS[:, C_UNSEL:C_UNSEL + 1], None, ALU.mult), r, "ho")
                link(dve.scalar_tensor_tensor(FS, X1S, bws[:, 0:1], FS, ALU.mult, ALU.add), r, "f")
                dve.bn_stats(bst[:, :], FS).then_inc(bdve.sem, 1)
                dve.wait_ge(bdve.sem, bdve.at(r, "fst"))
                carry()
                link(dve.bn_aggr(bmv[:, :], bst[:, :]), r, "fag")
                link(dve.tensor_scalar(bve[:, :], bmv[:, 1:2], 1e-5, None, ALU.add), r, "fve")

            def b13(r):
                dve.wait_ge(bpool.sem, bpool.at(r, "f"))
                link(dve.tensor_scalar(FS, FS, bmv[:, 0:1], brs[:, 0:1], ALU.subtract, ALU.mult), r, "fn")
                dve.tensor_tensor(OS, FS, GS[:, 0:D], ALU.add).then_inc(bdve.sem, 1)

            AT_STEP = {1: b1, 2: b2, 3: b3, 4: b4, 5: b5, 6: b6, 7: b7, 9: b9, 12: b12, 13: b13}
            pair = [None]

            def do(name, t, q, k):
                if name == "pre":
                    if is_row(t, 0):
                        norm_x(t, q)
                        setup_rest()
                    else:
                        norm_x(t, q)
                elif name == "turn":
                    turn(t, k)
                    if is_row(t, 0) and k == 1:
                        setup_tokens()
                elif name == "into" and k < 4:
                    convolve(t, k)
                elif name == "tanh":
                    silu_(t, k)
                elif name == "b":
                    scan(t, k)
                elif name == "c":
                    c_and_gate(t, k)
                elif name == "post_a":
                    post_a(t)
                elif name == "post_n":
                    post_n(t)
                elif name == "post_x":
                    post_x(t, q)
                elif name == "post_h":
                    post_h(t, q)
                elif name == "post_z":
                    post_z(t)
                elif name == "rank":
                    rank_(t, q)
                elif name == "slots" and k in AT_STEP:
                    AT_STEP[k](t)

            run_all(dve, do)



_INS = ["L0_attn_x", "L0_attn_W_in", "L0_attn_b_in", "L0_attn_conv_w", "L0_attn_conv_b", "L0_attn_W_bc",
        "L0_attn_b_bc", "L0_attn_log_decay", "L0_attn_W_out", "L0_attn_b_out", "L0_ffn_attention_mask",
        "L0_ffn_position_ids", "L0_ffn_router_w", "L0_ffn_router_b", "L0_ffn_wq", "L0_ffn_wk", "L0_ffn_wv",
        "L0_ffn_wo", "L0_ffn_w1", "L0_ffn_w2", "L0_ffn_ln1", "L0_ffn_ln2"]


def kernel(**inputs):
    import concourse.bacc as bacc
    from concourse.bass_utils import run_bass_kernel_spmd

    nc = bacc.Bacc("TRN2", target_bir_lowering=False, num_devices=1)
    arrays = {f"in_{n}_dram": np.ascontiguousarray(inputs[n]) for n in _INS}
    arrays["in_shape_constants_dram"] = shape_constants()
    args = [nc.dram_tensor(n, a.shape, mybir.dt.from_np(a.dtype), kind="ExternalInput").ap()
            for n, a in arrays.items()]
    out = nc.dram_tensor("out_0_dram", (NB, NT, D), F32, kind="ExternalOutput").ap()
    build(nc, *args, out)
    r = run_bass_kernel_spmd(nc, [arrays], core_ids=[0])
    return r.results[0]["out_0_dram"]
```

```python
from contextlib import ExitStack

import numpy as np
import concourse.bass as bass
from concourse import mybir

P = 128
NB, NT, D = 8, 512, 256
DI, TAPS = 512, 4
H, HD, F = 16, 16, 1024
NP_ROWS, S_TAB = 4, 1024
SLOTS = int(0.125 * NT)
KC = SLOTS - 1
TT = NT // P
KD, KI, KF = D // P, DI // P, F // P
PAIRS = NB // 2
HP = H // 2
VW = HD + 1

F32 = mybir.dt.float32
F32R = mybir.dt.float32r
BF16 = mybir.dt.bfloat16
I32 = mybir.dt.int32
U32 = mybir.dt.uint32
ALU = mybir.AluOpType
ACT = mybir.ActivationFunctionType
AX = mybir.AxisListType

C_W, C_UNSEL, C_R, C_MR, C_R2, C_COS, C_SIN, C_MROW, C_OROW = (D + n for n in (0, 1, 2, 3, 4, 5, 13, 21, 22))
PAY = D + 23
TCW = PAY - C_COS
HALF = HD // 2

K_ID, K_TRI, K_IOTA, K_INV, K_MROW, K_OROW, K_HEAD, K_SEL = 0, 128, 640, 704, 712, 744, 776, 784
K_ALL = 785
R_BIN, R_BBC, R_CB, R_LD, R_LN1, R_LN2, R_ALL = 0, 8, 16, 20, 24, 26, 28

TWO_PI = 2.0 * np.pi
PI_A = 6.28125
PI_B = float(np.float32(np.round((TWO_PI - PI_A) * 2**16) / 2**16))
PI_C = float(np.float32(np.round((TWO_PI - PI_A - PI_B) * 2**25) / 2**25))
PI_D = float(np.float32(TWO_PI - PI_A - PI_B - PI_C))
MAGIC = 1.5 * 2.0**23


def shape_constants():
    c = np.zeros((P, K_ALL), np.float32)
    c[:, K_ID:K_ID + P] = np.eye(P)
    c[:, K_TRI:K_TRI + NT] = np.arange(NT)[None] >= np.arange(P)[:, None]
    c[:, K_IOTA:K_IOTA + SLOTS] = np.arange(SLOTS)
    c[:, K_INV:K_INV + HALF] = np.float32(1.0) / np.float32(10000.0) ** (np.arange(0, HD, 2, dtype=np.float32) / np.float32(HD))
    for b in range(NB):
        for i in range(TT):
            tok = P * i + np.arange(P)
            c[:, K_MROW + TT * b + i] = 2 * (min(b, NP_ROWS - 1) * S_TAB + tok)
            c[:, K_OROW + TT * b + i] = b * NT + tok
    c[:, K_HEAD:K_HEAD + 8] = (np.arange(P)[:, None] // HD) == np.arange(8)
    c[:, K_SEL] = (np.arange(P) % SLOTS) < KC
    return c


class Signal:

    def __init__(self, sem, events):
        self.sem, self.n, self.index = sem, len(events), {e: k + 1 for k, e in enumerate(events)}

    def at(self, rep, event=None):
        return rep * self.n + (self.index[event] if event is not None else self.n)


def began(rep):
    return not isinstance(rep, int) or rep >= 0


def build(nc, x, W_in, b_in, conv_w, conv_b, W_bc, b_bc, log_decay, W_out, b_out, mask, pos, router_w,
          router_b, wq, wk, wv, wo, w1, w2, ln1, ln2, consts, out):
    ctx = ExitStack()
    with ctx:
        def sb(name, shape, dt=F32):
            return ctx.enter_context(nc.sbuf_tensor(name, [P] + list(shape), dt))

        def semaphore(name):
            return ctx.enter_context(nc.semaphore(name))

        def signal(name, events):
            return Signal(semaphore(name), events)

        WinH, WinL = sb("WinH", [KD, 2 * DI], F32R), sb("WinL", [KD, 2 * DI], F32R)
        WbcH, WbcL = sb("WbcH", [KI, 2 * DI], F32R), sb("WbcL", [KI, 2 * DI], F32R)
        WoutH, WoutL = sb("WoutH", [KI, D], F32R), sb("WoutL", [KI, D], F32R)
        Wqkv, Wo = sb("Wqkv", [KD, 3 * D]), sb("Wo", [KD, D])
        W1, W2 = sb("W1", [KD, F]), sb("W2", [KF, D])
        K = sb("K", [K_ALL])
        ident = K[:, K_ID:K_ID + P]
        cols = sb("cols", [R_ALL])
        convw = sb("convw", [KI, TAPS])
        rw, bout, rb = sb("rw", [D]), sb("bout", [D]), sb("rb", [1])
        decay, hbin, vbias = sb("decay", [KI]), sb("hbin", [KI]), sb("vbias", [KI])
        tokc = sb("tokc", [NB, TT, TCW])

        X = sb("X", [2, TT, D])
        LNH, LNL = sb("LNH", [KD, NT], F32R), sb("LNL", [KD, NT], F32R)
        U = sb("U", [2, TAPS - 1 + NT])
        V = sb("V", [2, NT])
        S = sb("S", [2, NT])
        SH, SL = sb("SH", [KI, NT], F32R), sb("SL", [KI, NT], F32R)
        G = sb("G", [KI, NT])
        Y = sb("Y", [2, NT])
        rows = Y[:, 0, 0:P]
        posi = Y[:, 0, P:2 * P].bitcast(I32)
        posf = Y[:, 0, 2 * P:3 * P]
        YH, YL = sb("YH", [KI, NT], F32R), sb("YL", [KI, NT], F32R)
        A = sb("A", [TT, D])
        HB = sb("HB", [TT, D])
        XR, junk = HB, HB[:, 0:2, :].rearrange("p i d -> p (i d)")
        pay = sb("pay", [2, TT, PAY])
        onehot = sb("onehot", [2, TT, SLOTS])
        tpos = sb("tpos", [NB * TT])
        stats, mv, ve, rs = sb("stats", [3, TT, 6]), sb("mv", [3, TT, 2]), sb("ve", [5, TT]), sb("rs", [4, TT])
        neg, negr = sb("neg", [3, TT]), sb("negr", [2, TT])
        half = sb("half", [TT])
        nge, tie, rank = sb("nge", [TT]), sb("tie", [TT]), sb("rank", [TT])

        big = sb("big", [7168])
        used = [0]

        def carve(n):
            used[0] += n
            assert used[0] <= 7168
            return big[:, used[0] - n:used[0]]

        GS, MR, HS, HN = carve(PAY), carve(NT), carve(D), carve(D)
        HT = carve(D).rearrange("p (k n) -> p k n", k=KD)
        MT = carve(NT).rearrange("p (k n) -> p k n", k=TT)
        QK, RT = carve(2 * D), carve(2 * D)
        QT = carve(D).rearrange("p (k n) -> p k n", k=KD)
        KB0, SC, AT_ = carve(1024), carve(1024), carve(1024)
        VB = carve(2 * HP * 2 * VW).rearrange("p (q h e) -> p q h e", q=2, h=HP)
        MS = carve(SLOTS)
        KB = [KB0, AT_]
        AT = AT_.rearrange("p (h n) -> p h n", h=HP)
        HTT = AT_[:, 0:2 * D].rearrange("p (k q n) -> p k q n", k=KD, q=2)
        GE = KB0.rearrange("p (k n) -> p k n", k=KF)
        X1S, FS, OS = QK[:, 0:D], QK[:, D:2 * D], RT[:, 0:D]
        rawin = big[:, 0:2048].rearrange("p (k n) -> p k n", k=KD)
        rawbc = big[:, 2048:6144].rearrange("p (k n) -> p k n", k=KI)
        rawout = big[:, 6144:7168].rearrange("p (k n) -> p k n", k=KI)
        idx = sb("idx", [2, 2], U32)
        bst, bmv, bve, brs, bss, bws = (sb("bst", [6]), sb("bmv", [2]), sb("bve", [1]), sb("brs", [1]),
                                        sb("bss", [1]), sb("bws", [1]))
        spare = sb("spare", [3])
        mx, rden = sb("mx", [H]), sb("rden", [H])
        bhalf = half[:, 0:1]
        ang = A[:, 0, :].rearrange("p (r f) -> p r f", f=HALF)
        trn = A[:, 1, :].rearrange("p (r f) -> p r f", f=HALF)
        red = A[:, 2, :].rearrange("p (r f) -> p r f", f=HALF)

        bank = [ctx.enter_context(nc.psum_tensor(f"bank{i}", [P, 512], F32)) for i in range(8)]
        TURN, B5, B6, B7 = bank[4], bank[5], bank[6], bank[7]

        s_ident, s_k, s_vec, s_win, s_wbc, s_wout, s_wb = (semaphore(n) for n in (
            "identity_in", "consts_in", "vectors_in", "win_in", "wbc_in", "wout_in", "wb_in"))
        x_in, xr_in, out_stored, mask_in, scattered = (semaphore(n) for n in (
            "x_in", "xr_in", "out_stored", "mask_in", "scattered"))
        set_pe = signal("set_pe", ["vectors", "positions"])
        set_act = signal("set_act", ["win", "edecay", "hbin", "wbc", "wout", "sin", "cos"])
        set_pool = signal("set_pool", ["wbc"])
        set_dve = signal("set_dve", ["half", "winh", "win", "pos", "cols", "tokpos", "pad", "vb1", "vbias", "wbch", "wbcl", "ed1", "decay",
                                     "wout", "rows"] + [f"ang{i}" for i in range(17)]
                         + ["ln1a", "ln1b", "ln2a", "ln2b", "zero", "one0", "one1", "sczero"])
        T4, C4 = range(TT), range(KI)
        pre = signal("norm_x", [f"{k}{i}" for k in ("st", "ag") for i in T4] + ["ve", "neg"])
        roots = signal("roots", ["x", "mx"])
        x_norm = signal("x_norm", [f"{i}" for i in T4])
        roots_post = signal("roots_post", ["a", "ma", "x1", "mx1", "h", "rms"])
        turned = signal("turned", ["t0", "t1"])
        ln_hi, ln_lo = signal("ln_hi", ["k0", "k1"]), signal("ln_lo", ["k0", "k1"])
        win = signal("win", ["u0", "u1", "g0", "u2", "g1", "u3", "g2", "g3"])
        u_out = signal("u_out", [f"{k}{c}" for c in C4 for k in "uv"])
        g_out = signal("g_out", [f"g{c}" for c in C4])
        conv = signal("conv", [f"{c}{j}" for c in C4 for j in range(TAPS - 1)])
        s_hi, s_lo = signal("s_hi", [f"{k}{c}" for c in C4 for k in ("", "r")]), signal("s_lo", [f"r{c}" for c in C4])
        wbc = signal("wbc", [f"{k}{c}" for c in C4 for k in "bc"])
        b_out_ = signal("b_out", [f"{c}" for c in C4])
        ssm = signal("ssm", [f"{k}{c}" for c in C4 for k in ("scan", "c", "y")])
        y_hi, y_lo = signal("y_hi", [f"{c}" for c in C4]), signal("y_lo", [f"{c}" for c in C4])
        wout = signal("wout", [f"{i}" for i in T4])
        post = signal("post", [f"a{i}" for i in T4] + [f"{k}{i}" for k in ("as", "aa") for i in T4] + ["ave", "aneg"]
                      + [f"{k}{i}" for k in ("xs", "xg") for i in T4] + ["xve", "xneg"] + ["v1", "v2", "hve", "rve"]
                      + [f"w{i}" for i in T4] + ["wb"])
        scaled = signal("scaled", [f"{k}{i}" for k in "nhz" for i in T4])
        x1_out = signal("x1_out", ["tokc"] + [f"{k}{i}" for k in ("x1", "out") for i in T4])
        wrow = signal("wrow", [f"{i}" for i in T4])
        ranked = signal("ranked", [f"{k}{i}" for i in T4 for k in ("nge", "tie")] + ["rank", "unsel"]
                        + [f"hot{i}" for i in T4])
        bpe = signal("slots_pe", ["gather", "hnT", "maskT", "qk", "v", "mask", "qkT", "s0", "s1", "at0", "at1", "pv",
                                  "oT", "wo", "hn2T", "w1a", "w1b", "w2"])
        bact = signal("slots_act", ["gs", "hnT", "hnTT0", "hnTT1", "v00", "v01", "v10", "v11", "ms", "qT", "exp0", "exp1", "at0", "oT", "hn2T",
                                    "ge0", "ge1"])
        bdve = signal("slots_dve", ["idx", "hs", "hn", "mt", "r1", "r2", "r3", "q1",
                                    "q2", "kb0", "kb1", "sc0", "max0", "sub0", "sc1", "max1", "sub1", "at1", "rden", "on", "x1s",
                                    "ss2", "ss2ve", "hn2", "x2", "ws", "ho", "f", "fst", "fag", "fve", "fn", "os"])
        bpool = signal("slots_roots", ["hn2", "f"])

        x_rows = x.rearrange("b (i p) d -> b p i d", p=P)
        out_rows = out.rearrange("b (i p) d -> b p i d", p=P)
        mask_rows = mask.rearrange("b o s (h c) -> (b o s h) c", c=NT)
        out_flat = out.rearrange("b n d -> (b n) d")
        block = ctx.enter_context(nc.Block())

        INTO = [("u", 0), ("u", 1), ("g", 0), ("u", 2), ("g", 1), ("u", 3), ("g", 2), ("g", 3)]

        def into_bank(c, q, which):
            n = INTO.index((which, c))
            return 2 * ((n // 2 + q) % 2) + n % 2

        def out_pair(q):
            return 1 - q

        def b_pair(c, q):
            return (c + 1 + q) % 2

        ROW = [("u", 0), ("u", 1), ("g", 0), ("silu", 0), ("u", 2), ("g", 1), ("silu", 1), ("u", 3), ("g", 2),
               ("silu", 2), ("g", 3), ("out_of", 0), ("silu", 3), ("pre_n", 0), ("pre_s", 0), ("post_a", 0),
               ("b", 0), ("c", 0), ("turn", 0), ("post_n", 0), ("post_x", 0), ("b", 1), ("yhi", 0),
               ("post_h", 0), ("turn", 1), ("c", 1), ("b", 2), ("rank", 0), ("post_z", 0), ("spread", 0),
               ("c", 2), ("yhi", 1), ("rank", 1), ("b", 3), ("yhi", 2), ("rank", 2), ("c", 3), ("rank", 3),
               ("rank", 4), ("yhi", 3)]
        SLOT_STEPS = {1: {("u", 1): (1,), ("g", 3): (2,), ("post_n", 0): (3,), ("post_x", 0): (4,),
                          ("turn", 1): (5,), ("yhi", 1): (6,), ("b", 3): (7,), ("rank", 3): (8,)},
                      0: {("u", 0): (9,), ("silu", 1): (10,), ("g", 3): (11,), ("post_n", 0): (12, 13),
                          ("turn", 1): (14,)}}
        TAIL = [("slots", 9), ("out_of", 0), ("slots", 10), ("slots", 11), ("spread", 0), ("post_a", 0),
                ("post_n", 0), ("post_x", 0), ("post_h", 0), ("post_z", 0), ("rank", 0), ("rank", 1),
                ("rank", 2), ("slots", 12), ("rank", 3), ("rank", 4), ("slots", 13)]
        NEXT = ("pre_s", "pre_n", "turn")
        BEFORE = ("out_of", "post_a", "post_n", "post_x", "post_h", "post_z", "spread", "rank")

        def run_row(do, t, q, r=None, first=False, last=False):
            for step in ROW:
                name, k = step
                if name in BEFORE:
                    if not first:
                        do(name, t - 1, 1 - q, k)
                elif name in NEXT:
                    if not last:
                        do(name, t + 1, 1 - q, k)
                else:
                    do(name, t, q, k)
                if r is not None:
                    for n in SLOT_STEPS[q].get(step, ()):
                        do("slots", r, 0, n)

        def run_all(eng, do):
            do("pre_s", 0, 0, 0)
            do("pre_n", 0, 0, 0)
            do("turn", 0, 0, 0)
            do("turn", 0, 0, 1)
            run_row(do, 0, 0, first=True)
            run_row(do, 1, 1)
            run_row(do, 2, 0)
            with eng.Fori(1, PAIRS - 1) as p:
                run_row(do, p * 2 + 1, 1, r=p - 1)
                run_row(do, p * 2 + 2, 0, r=p - 1)
            run_row(do, NB - 1, 1, r=PAIRS - 2, last=True)
            for step in TAIL:
                if step[0] == "slots":
                    do("slots", PAIRS - 2, 0, step[1])
                else:
                    do(step[0], NB - 1, 1, step[1])
            for n in (1, 2):
                do("slots", PAIRS - 1, 0, n)
            do("slots", PAIRS - 2, 0, 14)
            for n in range(3, 14):
                do("slots", PAIRS - 1, 0, n)

        def idx_of(r, which):
            last = 1 if isinstance(r, int) and r == PAIRS - 1 else 0
            return idx[:, last, which:which + 1] if which is not None else idx[:, last, :]

        def is_row(t, n):
            return isinstance(t, int) and t == n

        @block.sync
        def _(sp):
            sp.dma_start(X[:, 0], x_rows[0]).then_inc(x_in, 16)
            sp.dma_start(ident, consts[:, K_ID:K_ID + P]).then_inc(s_ident, 16)
            sp.dma_start(rawin, W_in.rearrange("(k p) n -> p k n", p=P)).then_inc(s_win, 16)
            for v, r, n in ((b_in, R_BIN, 8), (b_bc, R_BBC, 8), (conv_b, R_CB, 4), (log_decay, R_LD, 4),
                            (ln1, R_LN1, 2), (ln2, R_LN2, 2)):
                sp.dma_start(rows[r:r + n, :], v.rearrange("(r p) -> r p", p=P)).then_inc(s_vec, 16)
            sp.dma_start(posi[0:16, :], pos[:, 0:NT].rearrange("b (i p) -> b i p", p=P)).then_inc(s_vec, 16)
            sp.dma_start(convw[:, :, :], conv_w.rearrange("(c p) o j -> p c (o j)", p=P)).then_inc(s_vec, 16)
            sp.dma_start(rw[:, :], router_w.rearrange("d o -> o d").to_broadcast([P, D])).then_inc(s_vec, 16)
            sp.dma_start(bout[:, :], b_out.rearrange("(o d) -> o d", o=1).to_broadcast([P, D])).then_inc(s_vec, 16)
            sp.dma_start(rb[:, :], router_b.rearrange("(o d) -> o d", o=1).to_broadcast([P, 1])).then_inc(s_vec, 16)
            sp.dma_start(K[:, P:], consts[:, P:]).then_inc(s_k, 16)
            sp.dma_start(rawbc, W_bc.rearrange("(k p) n -> p k n", p=P)).then_inc(s_wbc, 16)
            sp.dma_start(rawout, W_out.rearrange("(k p) n -> p k n", p=P)).then_inc(s_wout, 16)
            sp.wait_ge(pre.sem, pre.at(0, "st0"))
            sp.dma_start(X[:, 1], x_rows[1]).then_inc(x_in, 16)
            for j, w in enumerate((wq, wk, wv)):
                sp.dma_start(Wqkv[:, :, j * D:(j + 1) * D], w.rearrange("(k p) n -> p k n", p=P)).then_inc(s_wb, 16)
            sp.dma_start(Wo[:, :, :], wo.rearrange("(k p) n -> p k n", p=P)).then_inc(s_wb, 16)
            sp.dma_start(W1[:, :, :], w1.rearrange("(k p) n -> p k n", p=P)).then_inc(s_wb, 16)
            sp.dma_start(W2[:, :, :], w2.rearrange("(k p) n -> p k n", p=P)).then_inc(s_wb, 16)

            def residual(t):
                if began(t - 1):
                    sp.wait_ge(ranked.sem, ranked.at(t - 1))
                sp.dma_start(XR[:, :, :], x_rows[t]).then_inc(xr_in, 16)

            def next_x(t, q):
                if began(t - 2):
                    sp.wait_ge(turned.sem, turned.at(t - 2))
                sp.wait_ge(pre.sem, pre.at(t - 1, "st0"))
                sp.dma_start(X[:, q], x_rows[t]).then_inc(x_in, 16)

            def store(t):
                sp.wait_ge(x1_out.sem, x1_out.at(t))
                sp.dma_start(out_rows[t], A[:, :, :]).then_inc(out_stored, 16)

            residual(0)
            next_x(2, 0)
            store(0)
            residual(1)
            with sp.Fori(1, PAIRS - 1) as p:
                next_x(p * 2 + 1, 1)
                store(p * 2 - 1)
                residual(p * 2)
                next_x(p * 2 + 2, 0)
                store(p * 2)
                residual(p * 2 + 1)
            next_x(NB - 1, 1)
            store(NB - 3)
            residual(NB - 2)
            store(NB - 2)
            residual(NB - 1)
            store(NB - 1)
            sp.wait_ge(out_stored, 16 * NB)
            sp.wait_ge(scattered, 16 * PAIRS)

        @block.tensor
        def _(pe):
            def split_product(o, wh, wl, ah, al, n_k, w_cols, a_cols, done, weights_move, parts=None, t=None):
                n = 0
                for k in range(n_k):
                    if parts is not None:
                        hi, lo, event = parts
                        pe.wait_ge(hi.sem, hi.at(t, f"{event}{k}"))
                        pe.wait_ge(lo.sem, lo.at(t, f"{event}{k}"))
                    for w, a in ((wh, ah), (wh, al), (wl, ah)):
                        ws, as_ = w[:, k, w_cols], a[:, k, a_cols]
                        l, r = (as_, ws) if weights_move else (ws, as_)
                        mm = pe.matmul(o, l, r, start=(n == 0), stop=(n == 3 * n_k - 1))
                        n += 1
                mm.then_inc(done, 1)

            def turn_vectors():
                pe.wait_ge(s_vec, 16 * 11)
                pe.transpose(B5[:, 0:R_ALL], rows[0:R_ALL, :], ident[0:R_ALL, 0:R_ALL]).then_inc(set_pe.sem, 1)
                pe.wait_ge(set_dve.sem, set_dve.at(0, "pos"))
                pe.transpose(B5[:, 32:48], posf[0:16, :], ident[0:16, 0:16]).then_inc(set_pe.sem, 1)

            def turn(t, q, k):
                if k == 0:
                    pe.wait_ge(x_norm.sem, x_norm.at(t))
                    if is_row(t, 0):
                        pe.wait_ge(s_ident, 16)
                    if not is_row(t, 1):
                        if began(t - 3):
                            pe.wait_ge(ranked.sem, ranked.at(t - 3, "tie3"))
                    if began(t - 1):
                        pe.wait_ge(ln_lo.sem, ln_lo.at(t - 1))
                else:
                    pe.wait_ge(ln_hi.sem, ln_hi.at(t, "k0"))
                    pe.wait_ge(ln_lo.sem, ln_lo.at(t, "k0"))
                for i in T4:
                    mm = pe.transpose(TURN[:, i * P:(i + 1) * P], X[:, q, i, k * P:(k + 1) * P], ident)
                mm.then_inc(turned.sem, 1)

            def into(t, q, c, j):
                if c == 0 and j == 0 and is_row(t, 0):
                    pe.wait_ge(set_dve.sem, set_dve.at(0, "win"))
                n = INTO.index(("ug"[j], c))
                if n < 4:
                    if began(t - 1):
                        if n % 2 == 0:
                            pe.wait_ge(b_out_.sem, b_out_.at(t - 1, f"{2 + n // 2}"))
                        else:
                            pe.wait_ge(ssm.sem, ssm.at(t - 1, f"c{2 + n // 2}"))
                else:
                    before, c_before = INTO[n - 4]
                    if before == "u":
                        pe.wait_ge(u_out.sem, u_out.at(t, f"v{c_before}"))
                    else:
                        pe.wait_ge(g_out.sem, g_out.at(t, f"g{c_before}"))
                b = into_bank(c, q, "ug"[j])
                m = 4 * j + c
                split_product(bank[b][:, :], WinH, WinL, LNH, LNL, KD, slice(m * P, (m + 1) * P),
                              slice(0, NT), win.sem, False, (ln_hi, ln_lo, "k") if c == 0 and j == 0 else None, t)

            def out_of(t, q):
                b = 2 * out_pair(q)
                for i in T4:
                    if i % 2 == 0:
                        if is_row(t, NB - 1):
                            pe.wait_ge(ssm.sem, ssm.at(t, "c2"))
                        elif i == 0:
                            pe.wait_ge(g_out.sem, g_out.at(t + 1, "g1"))
                        else:
                            pe.wait_ge(u_out.sem, u_out.at(t + 1, "v3"))
                    split_product(bank[b + i // 2][:, (i % 2) * D:(i % 2 + 1) * D], WoutH, WoutL, YH, YL, KI,
                                  slice(0, D), slice(i * P, (i + 1) * P), wout.sem, True,
                                  (y_hi, y_lo, "") if i == 0 else None, t)

            def bc(t, q, c, j):
                if c == 0 and j == 0:
                    if is_row(t, 0):
                        pe.wait_ge(set_pool.sem, set_pool.at(0, "wbc"))
                        pe.wait_ge(set_dve.sem, set_dve.at(0, "wbcl"))
                if c == 0:
                    pe.wait_ge(g_out.sem, g_out.at(t, "g3" if j else "g2"))
                elif c == 1:
                    if began(t - 1):
                        pe.wait_ge(post.sem, post.at(t - 1, "a3" if j else "a1"))
                elif j == 0:
                    pe.wait_ge(b_out_.sem, b_out_.at(t, f"{c - 2}"))
                else:
                    pe.wait_ge(ssm.sem, ssm.at(t, f"c{c - 2}"))
                m = 4 * j + c
                split_product(bank[2 * b_pair(c, q) + j][:, :], WbcH, WbcL, SH, SL, KI, slice(m * P, (m + 1) * P),
                              slice(0, NT), wbc.sem, False, (s_hi, s_lo, "r") if c == 0 and j == 0 else None, t)

            def spread(t, q):
                pe.wait_ge(post.sem, post.at(t, "wb"))
                if is_row(t, NB - 1) or is_row(t, NB - 2):
                    if began(t - 1):
                        pe.wait_ge(ranked.sem, ranked.at(t - 1))
                else:
                    pe.wait_ge(ln_lo.sem, ln_lo.at(t + 2))
                for i in T4:
                    pe.transpose(TURN[:, i * P:(i + 1) * P],
                                 pay[:, q, i, C_W:C_W + 1].to_broadcast([P, P]), ident).then_inc(wrow.sem, 1)

            half_rows = [slice(0, 64), slice(64, 128)]

            def b1(r):
                for q in range(2):
                    pe.wait_ge(x1_out.sem, x1_out.at(r * 2 + q, "x13"))
                    pe.wait_ge(roots_post.sem, roots_post.at(r * 2 + q))
                    pe.wait_ge(ranked.sem, ranked.at(r * 2 + q))
                    for i in T4:
                        mm = pe.matmul(B5[half_rows[q], 0:PAY], onehot[:, q, i, :], pay[:, q, i, :],
                                       start=(i == 0), stop=(i == TT - 1))
                mm.then_inc(bpe.sem, 1)

            def b2(r):
                pe.wait_ge(bdve.sem, bdve.at(r, "hn"))
                for k in range(KD):
                    mm = pe.transpose(B6[:, k * P:(k + 1) * P], HN[:, k * P:(k + 1) * P], ident)
                mm.then_inc(bpe.sem, 1)

            def b3(r):
                pe.wait_ge(mask_in, r * 16 + 16)
                for k in T4:
                    mm = pe.transpose(B7[:, k * P:(k + 1) * P], MR[:, k * P:(k + 1) * P], ident)
                mm.then_inc(bpe.sem, 1)
                pe.wait_ge(bact.sem, bact.at(r, "hnT"))
                for k in range(KD):
                    mm = pe.matmul(B5[:, :], HT[:, k, :], Wqkv[:, k, 0:2 * D], start=(k == 0), stop=(k == KD - 1))
                mm.then_inc(bpe.sem, 1)
                pe.wait_ge(bact.sem, bact.at(r, "hnTT1"))
                for q in range(2):
                    for k in range(KD):
                        mm = pe.matmul(B6[:, q * D:(q + 1) * D], HTT[:, k, q, :], Wqkv[:, k, 2 * D:3 * D],
                                       start=(k == 0), stop=(k == KD - 1))
                mm.then_inc(bpe.sem, 1)
                pe.wait_ge(bdve.sem, bdve.at(r, "mt"))
                for q in range(2):
                    for k in T4:
                        mm = pe.matmul(B7[half_rows[q], 0:SLOTS], MT[:, k, half_rows[q]], onehot[:, q, k, :],
                                       start=(k == 0), stop=(k == TT - 1))
                mm.then_inc(bpe.sem, 1)

            def b4(r):
                pe.wait_ge(bdve.sem, bdve.at(r, "q2"))
                for k in range(4):
                    mm = pe.transpose(B5[:, k * P:(k + 1) * P], QK[:, k * P:(k + 1) * P], ident)
                mm.then_inc(bpe.sem, 1)

            def b5(r):
                pe.wait_ge(bact.sem, bact.at(r, "qT"))
                for g in range(2):
                    pe.wait_ge(bdve.sem, bdve.at(r, f"kb{g}"))
                    if g == 0:
                        pe.wait_ge(bact.sem, bact.at(r, "v11"))
                    else:
                        pe.wait_ge(bact.sem, bact.at(r, "ms"))
                    for q in range(2):
                        kb = KB[g].rearrange("p (q n) -> p q n", q=2)
                        mm = pe.matmul(bank[6 + g][half_rows[q], :], QT[:, g, half_rows[q]], kb[:, q, :],
                                       start=True, stop=True)
                    mm.then_inc(bpe.sem, 1)

            def b6(r):
                for g in range(2):
                    pe.wait_ge(bact.sem, bact.at(r, f"exp{g}"))
                    for k in range(4):
                        hp = 4 * g + k
                        mm = pe.transpose(bank[6 + g][:, k * P:(k + 1) * P], SC[:, hp * P:(hp + 1) * P], ident)
                    mm.then_inc(bpe.sem, 1)

            def b7(r):
                for g in range(2):
                    if g == 0:
                        pe.wait_ge(bact.sem, bact.at(r, "at0"))
                    else:
                        pe.wait_ge(bdve.sem, bdve.at(r, "at1"))
                    for q, hp in ((q, 4 * g + k) for q in range(2) for k in range(4)):
                        mm = pe.matmul(B5[half_rows[q], hp * 2 * VW:(hp + 1) * 2 * VW], AT[:, hp, half_rows[q]],
                                       VB[:, q, hp, :], start=True, stop=True)
                mm.then_inc(bpe.sem, 1)

            def b8(r):
                pe.wait_ge(bdve.sem, bdve.at(r, "on"))
                for k in range(KD):
                    mm = pe.transpose(B6[:, k * P:(k + 1) * P], HN[:, k * P:(k + 1) * P], ident)
                mm.then_inc(bpe.sem, 1)

            def b9(r):
                pe.wait_ge(bact.sem, bact.at(r, "oT"))
                for k in range(KD):
                    mm = pe.matmul(B5[:, 0:D], HT[:, k, :], Wo[:, k, :], start=(k == 0), stop=(k == KD - 1))
                mm.then_inc(bpe.sem, 1)

            def b10(r):
                pe.wait_ge(bdve.sem, bdve.at(r, "hn2"))
                for k in range(KD):
                    mm = pe.transpose(B6[:, k * P:(k + 1) * P], HN[:, k * P:(k + 1) * P], ident)
                mm.then_inc(bpe.sem, 1)

            def b11(r):
                pe.wait_ge(bact.sem, bact.at(r, "hn2T"))
                for m in range(KF):
                    for k in range(KD):
                        mm = pe.matmul(bank[6 + m // 4][:, (m % 4) * P:(m % 4 + 1) * P], W1[:, k, m * P:(m + 1) * P],
                                       HT[:, k, :], start=(k == 0), stop=(k == KD - 1))
                    if m % 4 == 3:
                        mm.then_inc(bpe.sem, 1)

            def b12(r):
                for m in range(KF):
                    if m % 4 == 0:
                        pe.wait_ge(bact.sem, bact.at(r, f"ge{m // 4}"))
                    mm = pe.matmul(B5[:, 0:D], GE[:, m, :], W2[:, m, :], start=(m == 0), stop=(m == KF - 1))
                mm.then_inc(bpe.sem, 1)

            def b13(r):
                pe.wait_ge(bdve.sem, bdve.at(r, "x2"))

            B = [b1, b2, b3, b4, b5, b6, b7, b8, b9, b10, b11, b12, b13]

            def do(name, t, q, k):
                if name == "turn":
                    turn(t, q, k)
                    if is_row(t, 0) and k == 1:
                        turn_vectors()
                elif name in "ug":
                    into(t, q, k, "ug".index(name))
                elif name == "out_of":
                    out_of(t, q)
                elif name in "bc":
                    bc(t, q, k, "bc".index(name))
                elif name == "spread":
                    spread(t, q)
                elif name == "slots" and k <= len(B):
                    B[k - 1](t)

            run_all(pe, do)

        @block.scalar
        def _(act):
            act.wait_ge(s_win, 16)
            act.copy(WinH[:, 0, :], rawin[:, 0, :]).then_inc(set_act.sem, 1)
            flat = tokc[:, :, :, :].rearrange("p b i c -> p (b i) c")

            def setup_more():
                act.wait_ge(set_dve.sem, set_dve.at(0, "cols"))
                act.activation(decay[:, :], cols[:, R_LD:R_LD + KI], ACT.Exp).then_inc(set_act.sem, 1)
                act.mul(hbin[:, :], cols[:, R_BIN + KI:R_BIN + 2 * KI], 0.5).then_inc(set_act.sem, 1)
                act.wait_ge(s_wbc, 16)
                act.copy(WbcH[:, 0:2, :], rawbc[:, 0:2, :]).then_inc(set_act.sem, 1)

            def setup_wout():
                act.wait_ge(s_wout, 16)
                act.mul(WoutH[:, :, :], rawout, 0.5).then_inc(set_act.sem, 1)

            def trig():
                act.wait_ge(set_dve.sem, set_dve.at(0, "ang16"))
                act.activation(flat[:, :, HALF:2 * HALF], ang, ACT.Sin).then_inc(set_act.sem, 1)
                act.activation(flat[:, :, 0:HALF], red, ACT.Sin).then_inc(set_act.sem, 1)

            def scale_tiles(root, mean_root, dst, src, done):
                for i in T4:
                    act.activation(dst(i), src(i), ACT.Identity, bias=mean_root(i),
                                   scale=root(i)).then_inc(done.sem, 1)

            def pre_n(t, q):
                act.wait_ge(roots.sem, roots.at(t))
                scale_tiles(lambda i: rs[:, 0, i:i + 1], lambda i: negr[:, 0, i:i + 1],
                            lambda i: X[:, q, i, :], lambda i: X[:, q, i, :], x_norm)

            def post_n(t):
                act.wait_ge(roots_post.sem, roots_post.at(t, "ma"))
                scale_tiles(lambda i: rs[:, 1, i:i + 1], lambda i: negr[:, 1, i:i + 1],
                            lambda i: A[:, i, :], lambda i: A[:, i, :], scaled)

            def post_h(t, q):
                act.wait_ge(roots_post.sem, roots_post.at(t, "mx1"))
                scale_tiles(lambda i: pay[:, q, i, C_R:C_R + 1], lambda i: pay[:, q, i, C_MR:C_MR + 1],
                            lambda i: HB[:, i, :], lambda i: pay[:, q, i, 0:D], scaled)

            def post_z(t):
                act.wait_ge(roots_post.sem, roots_post.at(t, "h"))
                act.wait_ge(scaled.sem, scaled.at(t, "h3"))
                act.wait_ge(post.sem, post.at(t, "w3"))
                for i in T4:
                    act.activation(A[:, i, :], HB[:, i, :], ACT.Copy, scale=rs[:, 3, i:i + 1]).then_inc(scaled.sem, 1)

            def turn(t, k):
                act.wait_ge(turned.sem, turned.at(t, f"t{k}"))
                if began(t - 1):
                    act.wait_ge(win.sem, win.at(t - 1))
                act.copy(LNH[:, k, :], TURN[:, :]).then_inc(ln_hi.sem, 1)

            def u(t, q, c):
                act.wait_ge(win.sem, win.at(t, f"u{c}"))
                if c < 2:
                    if began(t - 1):
                        act.wait_ge(s_hi.sem, s_hi.at(t - 1, f"r{c + 2}"))
                else:
                    act.wait_ge(s_hi.sem, s_hi.at(t, f"r{c - 2}"))
                if is_row(t, 0) and c == 0:
                    act.wait_ge(set_dve.sem, set_dve.at(0, "vbias"))
                act.activation(U[:, c % 2, TAPS - 1:], bank[into_bank(c, q, "u")][:, :], ACT.Identity,
                               bias=cols[:, R_BIN + c:R_BIN + c + 1]).then_inc(u_out.sem, 1)
                act.activation(V[:, c % 2, :], bank[into_bank(c, q, "u")][:, :], ACT.Identity, bias=vbias[:, c:c + 1],
                               scale=convw[:, c, TAPS - 1:TAPS]).then_inc(u_out.sem, 1)

            def silu(t, c):
                act.wait_ge(conv.sem, conv.at(t, f"{c}2"))
                if c >= 2:
                    act.wait_ge(s_lo.sem, s_lo.at(t, f"r{c - 2}"))
                elif began(t - 1):
                    act.wait_ge(s_lo.sem, s_lo.at(t - 1, f"r{c + 2}"))
                act.activation(S[:, c % 2, :], V[:, c % 2, :], ACT.Silu).then_inc(s_hi.sem, 1)
                if began(t - 1):
                    act.wait_ge(wbc.sem, wbc.at(t - 1))
                act.activation(SH[:, c, :], V[:, c % 2, :], ACT.Silu).then_inc(s_hi.sem, 1)

            def gate(t, q, c):
                act.wait_ge(win.sem, win.at(t, f"g{c}"))
                if is_row(t, 0) and c == 0:
                    act.wait_ge(set_act.sem, set_act.at(0, "hbin"))
                if began(t - 1):
                    act.wait_ge(ssm.sem, ssm.at(t - 1, f"y{c}"))
                act.activation(G[:, c, :], bank[into_bank(c, q, "g")][:, :], ACT.Tanh, bias=hbin[:, c:c + 1],
                               scale=0.5).then_inc(g_out.sem, 1)

            def bout_(t, q, c):
                act.wait_ge(wbc.sem, wbc.at(t, f"b{c}"))
                if c >= 2:
                    act.wait_ge(y_lo.sem, y_lo.at(t, f"{c - 2}"))
                else:
                    if began(t - 1):
                        act.wait_ge(y_lo.sem, y_lo.at(t - 1, f"{c + 2}"))
                act.activation(Y[:, c % 2, :], bank[2 * b_pair(c, q)][:, :], ACT.Identity,
                               bias=cols[:, R_BBC + c:R_BBC + c + 1]).then_inc(b_out_.sem, 1)

            def yhi(t, c):
                act.wait_ge(ssm.sem, ssm.at(t, f"y{c}"))
                if began(t - 1):
                    act.wait_ge(wout.sem, wout.at(t - 1))
                act.copy(YH[:, c, :], Y[:, c % 2, :]).then_inc(y_hi.sem, 1)

            def b1(r):
                act.wait_ge(bpe.sem, bpe.at(r, "gather"))
                act.copy(GS, B5[:, 0:PAY]).then_inc(bact.sem, 1)

            def b2(r):
                act.wait_ge(bpe.sem, bpe.at(r, "hnT"))
                act.copy(HT, B6[:, 0:D].rearrange("p (k n) -> p k n", k=KD)).then_inc(bact.sem, 1)

                for k in range(KD):
                    act.copy(HTT[:, k, :, :].rearrange("p q (e n) -> p q e n", e=2),
                             B6[:, k * P:(k + 1) * P].rearrange("p (q n) -> p q n", q=2).unsqueeze(2)
                             .to_broadcast([P, 2, 2, SLOTS])).then_inc(bact.sem, 1)

            def b3(r):
                act.wait_ge(bpe.sem, bpe.at(r, "v"))
                for q in range(2):
                    v = B6[:, q * D:(q + 1) * D].rearrange("p (h e d) -> p h e d", h=HP, e=2)
                    act.copy(VB[0:64, q, :, 0:HD], v[0:64, :, 0, :]).then_inc(bact.sem, 1)
                    act.copy(VB[64:128, q, :, VW:VW + HD], v[64:128, :, 1, :]).then_inc(bact.sem, 1)
                act.wait_ge(bpe.sem, bpe.at(r, "mask"))
                act.copy(MS, B7[:, 0:SLOTS]).then_inc(bact.sem, 1)

            def b4(r):
                act.wait_ge(bpe.sem, bpe.at(r, "qkT"))
                act.copy(QT, B5[:, 0:D].rearrange("p (k n) -> p k n", k=KD)).then_inc(bact.sem, 1)

            def b5(r):
                sc = SC.rearrange("p (h k) -> p h k", h=H)
                for g in range(2):
                    act.wait_ge(bdve.sem, bdve.at(r, f"sub{g}"))
                    sg = sc[:, 8 * g:8 * g + 8, 0:KC]
                    act.activation(sg, sg, ACT.Exp).then_inc(bact.sem, 1)

            def b6(r):
                act.wait_ge(bpe.sem, bpe.at(r, "at0"))
                act.copy(AT[:, 0:4, :], B6[:, :].rearrange("p (h n) -> p h n", h=4)).then_inc(bact.sem, 1)

            def b7(r):
                act.wait_ge(bpe.sem, bpe.at(r, "oT"))
                act.copy(HT, B6[:, 0:D].rearrange("p (k n) -> p k n", k=KD)).then_inc(bact.sem, 1)

            def b8(r):
                act.wait_ge(bpe.sem, bpe.at(r, "hn2T"))
                act.copy(HT, B6[:, 0:D].rearrange("p (k n) -> p k n", k=KD)).then_inc(bact.sem, 1)

            def b9(r):
                for g in range(2):
                    act.wait_ge(bpe.sem, bpe.at(r, "w1a" if g == 0 else "w1b"))
                    act.activation(GE[:, 4 * g:4 * g + 4, :], bank[6 + g][:, :].rearrange("p (h n) -> p h n", h=4),
                                   ACT.Gelu_apprx_tanh).then_inc(bact.sem, 1)

            def b13(r):
                act.wait_ge(bdve.sem, bdve.at(r))

            AT_STEP = {1: b1, 2: b2, 3: b3, 4: b4, 5: b5, 6: b6, 8: b7, 10: b8, 11: b9, 13: b13}

            def do(name, t, q, k):
                if name == "turn":
                    turn(t, k)
                    if is_row(t, 0) and k == 1:
                        setup_more()
                elif name == "u":
                    u(t, q, k)
                elif name == "g":
                    gate(t, q, k)
                elif name == "silu":
                    silu(t, k)
                    if is_row(t, 0) and k == 3:
                        setup_wout()
                elif name == "pre_n":
                    pre_n(t, q)
                elif name == "post_n":
                    post_n(t)
                elif name == "post_h":
                    post_h(t, q)
                elif name == "post_z":
                    post_z(t)
                elif name == "b":
                    bout_(t, q, k)
                elif name == "yhi":
                    yhi(t, k)
                    if is_row(t, 0) and k == 3:
                        trig()
                elif name == "slots" and k in AT_STEP:
                    AT_STEP[k](t)

            run_all(act, do)

        @block.gpsimd
        def _(pool):
            def root(out_, var, sig, rep, event, done, mean=None):
                pool.wait_ge(sig.sem, sig.at(rep, event))
                pool.tensor_tensor(out_, var, half[:, :], ALU.pow).then_inc(done.sem, 1)
                if mean is not None:
                    pool.wait_ge(done.sem, done.at(rep, mean[0]))
                    pool.tensor_tensor(mean[1], mean[2], out_, ALU.mult).then_inc(done.sem, 1)

            def setup_pool():
                pool.wait_ge(set_act.sem, set_act.at(0, "wbc"))
                pool.tensor_tensor(WbcL[:, 0:2, :], rawbc[:, 0:2, :], WbcH[:, 0:2, :].bitcast(F32),
                                   ALU.subtract).then_inc(set_pool.sem, 1)

            def slo(t, c):
                pool.wait_ge(s_hi.sem, s_hi.at(t, f"r{c}"))
                pool.tensor_tensor(SL[:, c, :], S[:, c % 2, :], SH[:, c, :].bitcast(F32), ALU.subtract).then_inc(s_lo.sem, 1)

            def ylo(t, c):
                pool.wait_ge(y_hi.sem, y_hi.at(t, f"{c}"))
                pool.tensor_tensor(YL[:, c, :], Y[:, c % 2, :], YH[:, c, :].bitcast(F32), ALU.subtract).then_inc(y_lo.sem, 1)

            def post_a(t, q):
                if q == 0 and not is_row(t, 0):
                    if began((t // 2 if isinstance(t, int) else pair[0]) - 1):
                        pool.wait_ge(bpe.sem, bpe.at((t // 2 if isinstance(t, int) else pair[0]) - 1, "gather"))
                if is_row(t, 0):
                    pool.wait_ge(set_act.sem, set_act.at(0, "cos"))
                    pool.wait_ge(set_dve.sem, set_dve.at(0, "rows"))
                pool.tensor_copy(pay[:, q, :, C_COS:PAY], tokc[:, t, :, :]).then_inc(x1_out.sem, 1)
                root(rs[:, 1, :], ve[:, 1, :], post, t, "aneg", roots_post, mean=("a", negr[:, 1, :], neg[:, 1, :]))

            def post_n(t, q):
                pool.wait_ge(xr_in, t * 16 + 16)
                for i in T4:
                    pool.wait_ge(scaled.sem, scaled.at(t, f"n{i}"))
                    pool.tensor_tensor(pay[:, q, i, 0:D], A[:, i, :], XR[:, i, :], ALU.add).then_inc(x1_out.sem, 1)

            def post_z(t, q):
                for i in T4:
                    pool.wait_ge(scaled.sem, scaled.at(t, f"z{i}"))
                    pool.tensor_tensor(A[:, i, :], A[:, i, :], pay[:, q, i, 0:D], ALU.add).then_inc(x1_out.sem, 1)

            pair = [None]

            def broot(r, event):
                pool.wait_ge(bdve.sem, bdve.at(r, event))
                pool.tensor_tensor(brs[:, :], bve[:, :], bhalf, ALU.pow).then_inc(bpool.sem, 1)

            def b1(r):
                pool.wait_ge(bdve.sem, bdve.at(r, "idx"))
                pool.tensor_tensor(spare[:, 2:3], bhalf, bhalf, ALU.mult)
                pool.indirect_dma_start(MR, None, mask_rows,
                                        bass.IndirectOffsetOnAxis(ap=idx_of(r, 0), axis=0)).then_inc(mask_in, 16)

            def b13(r):
                broot(r, "fve")
                pool.wait_ge(bdve.sem, bdve.at(r, "os"))
                pool.wait_ge(out_stored, (r * 2 + 1) * 16 + 16)
                pool.tensor_tensor(spare[:, 1:2], bhalf, bhalf, ALU.mult)
                pool.indirect_dma_start(out_flat, bass.IndirectOffsetOnAxis(ap=idx_of(r, 1), axis=0),
                                        OS, None).then_inc(scattered, 16)

            def do(name, t, q, k):
                if name == "pre_s":
                    root(rs[:, 0, :], ve[:, 0, :], pre, t, "neg", roots, mean=("x", negr[:, 0, :], neg[:, 0, :]))
                elif name == "turn" and k == 1 and is_row(t, 0):
                    setup_pool()
                elif name == "silu":
                    slo(t, k)
                elif name == "yhi":
                    ylo(t, k)
                elif name == "post_a":
                    post_a(t, q)
                elif name == "post_n":
                    post_n(t, q)
                elif name == "post_x":
                    root(pay[:, q, :, C_R], ve[:, 2, :], post, t, "xneg", roots_post,
                         mean=("x1", pay[:, q, :, C_MR], neg[:, 2, :]))
                    root(rs[:, 3, :], ve[:, 3, :], post, t, "hve", roots_post)
                    root(pay[:, q, :, C_R2], ve[:, 4, :], post, t, "rve", roots_post)
                elif name == "post_z":
                    post_z(t, q)
                elif name == "slots":
                    if k == 1:
                        pair[0] = t + 1
                        b1(t)
                    elif k == 9:
                        broot(t, "ss2ve")
                    elif k == 13:
                        b13(t)

            pool.wait_ge(set_dve.sem, set_dve.at(0, "half"))
            run_all(pool, do)

        @block.vector
        def _(dve):
            n_set = [0]

            def setup(ins):
                n_set[0] += 1
                ins.then_inc(set_dve.sem, 1)
                dve.wait_ge(set_dve.sem, n_set[0])

            setup(dve.memset(half[:, :], -0.5))

            def setup_win():
                dve.wait_ge(s_win, 16)
                setup(dve.tensor_copy(WinH[:, 1, :], rawin[:, 1, :]))
                dve.wait_ge(set_act.sem, set_act.at(0, "win"))
                setup(dve.tensor_tensor(WinL[:, :, :], rawin, WinH[:, :, :].bitcast(F32), ALU.subtract))
                dve.wait_ge(s_vec, 16 * 11)
                setup(dve.tensor_copy(posf[0:16, :], posi[0:16, :]))

            def setup_first():
                dve.wait_ge(set_pe.sem, set_pe.at(0))
                setup(dve.tensor_copy(cols[:, :], B5[:, 0:R_ALL]))
                setup(dve.tensor_copy(tpos[:, 0:NP_ROWS * TT], B5[:, 32:48]))
                setup(dve.memset(U[:, :, 0:TAPS - 1], 0.0))
                setup(dve.tensor_tensor(vbias[:, :], cols[:, R_BIN:R_BIN + KI], convw[:, :, TAPS - 1], ALU.mult))
                setup(dve.tensor_tensor(vbias[:, :], vbias[:, :], cols[:, R_CB:R_CB + KI], ALU.add))
                dve.wait_ge(s_wbc, 16)
                setup(dve.tensor_copy(WbcH[:, 2:, :], rawbc[:, 2:, :]))
                setup(dve.tensor_tensor(WbcL[:, 2:, :], rawbc[:, 2:, :], WbcH[:, 2:, :].bitcast(F32), ALU.subtract))

            def setup_more():
                dve.wait_ge(set_act.sem, set_act.at(0, "edecay"))
                setup(dve.tensor_scalar(decay[:, :], decay[:, :], 1.0, None, ALU.add))
                setup(dve.reciprocal(decay[:, :], decay[:, :]))
                dve.wait_ge(set_act.sem, set_act.at(0, "wout"))
                setup(dve.scalar_tensor_tensor(WoutL[:, :, :].rearrange("p k n -> p (k n)"),
                                               big[:, 6144:7168], 0.5,
                                               WoutH[:, :, :].rearrange("p k n -> p (k n)").bitcast(F32),
                                               ALU.mult, ALU.subtract))

            def setup_tokens():
                last_row = tpos[:, (NP_ROWS - 1) * TT:NP_ROWS * TT].unsqueeze(1)
                rest = tpos[:, NP_ROWS * TT:].rearrange("p (b i) -> p b i", i=TT)
                setup(dve.tensor_copy(rest, last_row.to_broadcast([P, NB - NP_ROWS, TT])))
                pb = tpos[:, :].unsqueeze(2).to_broadcast([P, NB * TT, HALF])
                fb = K[:, K_INV:K_INV + HALF].unsqueeze(1).to_broadcast([P, NB * TT, HALF])
                setup(dve.tensor_tensor(ang, pb, fb, ALU.mult))
                for shift, dst in ((0.25, red), (0.0, ang)):
                    setup(dve.tensor_scalar(trn, ang, 1.0 / TWO_PI, shift, ALU.mult, ALU.add))
                    setup(dve.tensor_scalar(trn, trn, MAGIC, None, ALU.add))
                    setup(dve.tensor_scalar(trn, trn, MAGIC, None, ALU.subtract))
                    src = ang
                    for part in (PI_A, PI_B, PI_C, PI_D):
                        setup(dve.scalar_tensor_tensor(dst, trn, -part, src, ALU.mult, ALU.add))
                        src = dst
                setup(dve.tensor_scalar(red, red, float(np.pi / 2), None, ALU.add))
                setup(dve.tensor_copy(tokc[:, :, :, C_MROW - C_COS],
                                      K[:, K_MROW:K_MROW + NB * TT].rearrange("p (b i) -> p b i", i=TT)))
                setup(dve.tensor_copy(tokc[:, :, :, C_OROW - C_COS],
                                      K[:, K_OROW:K_OROW + NB * TT].rearrange("p (b i) -> p b i", i=TT)))

            def setup_slots():
                dve.wait_ge(s_wb, 16 * 6)
                for k in range(KD):
                    setup(dve.tensor_scalar(Wqkv[:, k, :], Wqkv[:, k, :], cols[:, R_LN1 + k:R_LN1 + k + 1], None, ALU.mult))
                for k in range(KD):
                    setup(dve.tensor_scalar(W1[:, k, :], W1[:, k, :], cols[:, R_LN2 + k:R_LN2 + k + 1], None, ALU.mult))
                dve.wait_ge(set_pool.sem, set_pool.at(0))
                setup(dve.memset(VB, 0.0))
                setup(dve.memset(VB[0:64, :, :, HD:HD + 1], 1.0))
                setup(dve.memset(VB[64:128, :, :, VW + HD:VW + HD + 1], 1.0))
                setup(dve.memset(SC, 0.0))

            def carry():
                dve.memset(spare[:, 0:1], 0.0)

            def statistics(which, sig, t, tag, src, eps, name, x1=False):
                for i in T4:
                    if x1:
                        dve.wait_ge(x1_out.sem, x1_out.at(t, f"x1{i}"))
                    dve.bn_stats(stats[:, which, i, :], src(i)).then_inc(sig.sem, 1)
                dve.wait_ge(sig.sem, sig.at(t, f"{tag[0]}3"))
                carry()
                for i in T4:
                    dve.bn_aggr(mv[:, which, i, :], stats[:, which, i, :]).then_inc(sig.sem, 1)
                dve.wait_ge(sig.sem, sig.at(t, f"{tag[1]}3"))
                dve.tensor_scalar(ve[:, which, :], mv[:, which, :, 1], eps, None, ALU.add).then_inc(sig.sem, 1)
                dve.tensor_scalar(neg[:, which, :], mv[:, which, :, 0], -1.0, None, ALU.mult).then_inc(sig.sem, 1)

            def pre_s(t, q):
                dve.wait_ge(x_in, t * 16 + 16)
                statistics(0, pre, t, ("st", "ag"), lambda i: X[:, q, i, :], 1e-5, "ve")

            def turn(t, k):
                dve.wait_ge(ln_hi.sem, ln_hi.at(t, f"k{k}"))
                dve.tensor_tensor(LNL[:, k, :], TURN[:, :], LNH[:, k, :].bitcast(F32), ALU.subtract).then_inc(ln_lo.sem, 1)

            def convolve(t, c):
                for j in range(TAPS - 1):
                    if j == 0:
                        dve.wait_ge(u_out.sem, u_out.at(t, f"v{c}"))
                    else:
                        dve.wait_ge(conv.sem, conv.at(t, f"{c}{j - 1}"))
                    dve.scalar_tensor_tensor(V[:, c % 2, :], U[:, c % 2, j:j + NT], convw[:, c, j:j + 1],
                                             V[:, c % 2, :], ALU.mult, ALU.add).then_inc(conv.sem, 1)

            def scan(t, c):
                dve.wait_ge(b_out_.sem, b_out_.at(t, f"{c}"))
                dve.tensor_tensor_scan(Y[:, c % 2, :], decay[:, c:c + 1].to_broadcast([P, NT]), Y[:, c % 2, :], 0.0,
                                       ALU.mult, ALU.add).then_inc(ssm.sem, 1)

            def c_and_gate(t, q, c):
                dve.wait_ge(wbc.sem, wbc.at(t, f"c{c}"))
                dve.wait_ge(ssm.sem, ssm.at(t, f"scan{c}"))
                dve.scalar_tensor_tensor(Y[:, c % 2, :], bank[2 * b_pair(c, q) + 1][:, :],
                                         cols[:, R_BBC + KI + c:R_BBC + KI + c + 1], Y[:, c % 2, :],
                                         ALU.add, ALU.mult).then_inc(ssm.sem, 1)
                dve.wait_ge(g_out.sem, g_out.at(t, f"g{c}"))
                dve.wait_ge(ssm.sem, ssm.at(t, f"c{c}"))
                dve.scalar_tensor_tensor(Y[:, c % 2, :], G[:, c, :], 1.0, Y[:, c % 2, :],
                                         ALU.add, ALU.mult).then_inc(ssm.sem, 1)

            def post_a(t, q):
                if is_row(t, 0):
                    dve.wait_ge(set_act.sem, set_act.at(0, "cos"))
                if began(t - 1):
                    dve.wait_ge(out_stored, (t - 1) * 16 + 16)
                for i in T4:
                    if i % 2 == 0:
                        dve.wait_ge(wout.sem, wout.at(t, f"{i + 1}"))
                    dve.tensor_tensor(A[:, i, :], bank[2 * out_pair(q) + i // 2][:, (i % 2) * D:(i % 2 + 1) * D], bout[:, :],
                                      ALU.add).then_inc(post.sem, 1)
                dve.wait_ge(post.sem, post.at(t, "a3"))
                statistics(1, post, t, ("as", "aa"), lambda i: A[:, i, :], 1e-5, "ave")

            def post_x(t, q):
                statistics(2, post, t, ("xs", "xg"), lambda i: pay[:, q, i, 0:D], 1e-5, "xve", x1=True)
                dve.wait_ge(roots_post.sem, roots_post.at(t, "x1"))
                dve.tensor_tensor(ve[:, 4, :], mv[:, 2, :, 1], pay[:, q, :, C_R], ALU.mult).then_inc(post.sem, 1)
                dve.wait_ge(post.sem, post.at(t, "v1"))
                dve.tensor_tensor(ve[:, 4, :], ve[:, 4, :], pay[:, q, :, C_R], ALU.mult).then_inc(post.sem, 1)
                dve.wait_ge(post.sem, post.at(t, "v2"))
                dve.tensor_scalar(ve[:, 3, :], ve[:, 4, :], 1e-5, None, ALU.add).then_inc(post.sem, 1)
                dve.wait_ge(post.sem, post.at(t, "hve"))
                dve.tensor_scalar(ve[:, 4, :], ve[:, 4, :], 1e-6, None, ALU.add).then_inc(post.sem, 1)

            def post_h(t, q):
                for i in T4:
                    dve.wait_ge(scaled.sem, scaled.at(t, f"h{i}"))
                    dve.tensor_tensor_reduce(out=A[:, i, :], in0=HB[:, i, :], in1=rw[:, :], scale=1.0, scalar=0.0,
                                             op0=ALU.mult, op1=ALU.add, accum_out=rank[:, i:i + 1]).then_inc(post.sem, 1)
                dve.wait_ge(post.sem, post.at(t, "w3"))
                dve.tensor_scalar(pay[:, q, :, C_W], rank[:, :], rb[:, 0:1], None, ALU.add).then_inc(post.sem, 1)

            def rank_(t, q, i):
                w = pay[:, q, i, C_W:C_W + 1] if i < TT else None
                if i == 0:
                    dve.wait_ge(wrow.sem, wrow.at(t))
                    dve.wait_ge(scaled.sem, scaled.at(t))
                if i > 0:
                    dve.wait_ge(ranked.sem, ranked.at(t, f"tie{i - 1}"))
                if i < TT:
                    dve.tensor_scalar(junk[:, :], TURN[:, :], w, None, ALU.is_ge, ALU.add,
                                      accum_out=nge[:, i:i + 1]).then_inc(ranked.sem, 1)
                    dve.wait_ge(ranked.sem, ranked.at(t, f"nge{i}"))
                    n = NT - P * i
                    dve.scalar_tensor_tensor(junk[:, 0:n], TURN[:, P * i:NT], w, K[:, K_TRI:K_TRI + n],
                                             ALU.is_equal, ALU.mult, accum_out=tie[:, i:i + 1]).then_inc(ranked.sem, 1)
                    return
                dve.tensor_tensor(rank[:, :], nge[:, :], tie[:, :], ALU.subtract).then_inc(ranked.sem, 1)
                dve.tensor_scalar(pay[:, q, :, C_UNSEL], nge[:, :], float(KC), None, ALU.is_gt).then_inc(ranked.sem, 1)
                dve.wait_ge(ranked.sem, ranked.at(t, "rank"))
                for k in T4:
                    dve.tensor_scalar(onehot[:, q, k, :], K[:, K_IOTA:K_IOTA + SLOTS], rank[:, k:k + 1], None,
                                      ALU.is_equal).then_inc(ranked.sem, 1)

            def link(ins, r, event):
                ins.then_inc(bdve.sem, 1)
                dve.wait_ge(bdve.sem, bdve.at(r, event))

            def b1(r):
                dve.wait_ge(bact.sem, bact.at(r, "gs"))
                link(dve.tensor_copy(idx_of(r, None), GS[:, C_MROW:C_OROW + 1]), r, "idx")
                link(dve.tensor_scalar(HS, GS[:, 0:D], GS[:, C_R:C_R + 1], GS[:, C_MR:C_MR + 1], ALU.mult, ALU.add), r, "hs")
                link(dve.tensor_scalar(HN, HS, GS[:, C_R2:C_R2 + 1], None, ALU.mult), r, "hn")

            def rms(r, src, ss, hn):
                link(dve.tensor_tensor_reduce(out=HN, in0=src, in1=src, scale=1.0, scalar=0.0, op0=ALU.mult,
                                              op1=ALU.add, accum_out=bss[:, :]), r, ss)
                link(dve.tensor_scalar(bve[:, :], bss[:, :], 1.0 / D, 1e-6, ALU.mult, ALU.add), r, ss + "ve")
                dve.wait_ge(bpool.sem, bpool.at(r, hn))
                link(dve.tensor_scalar(HN, src, brs[:, 0:1], None, ALU.mult), r, hn)

            def b3(r):
                dve.wait_ge(bpe.sem, bpe.at(r, "maskT"))
                link(dve.tensor_copy(MT, B7[:, :].rearrange("p (k n) -> p k n", k=TT)), r, "mt")
                dve.wait_ge(bpe.sem, bpe.at(r, "qk"))
                x4 = B5[:, :].rearrange("p (h e f) -> p h e f", e=2, f=HALF)
                o4 = QK.rearrange("p (h e f) -> p h e f", e=2, f=HALF)
                r4 = RT.rearrange("p (h e f) -> p h e f", e=2, f=HALF)
                cos = GS[:, C_COS:C_COS + HALF]
                sin = GS[:, C_SIN:C_SIN + HALF].unsqueeze(1).to_broadcast([P, 2 * H, HALF])
                cos4 = cos.unsqueeze(1).unsqueeze(1).to_broadcast([P, 2 * H, 2, HALF])
                link(dve.tensor_tensor(o4, x4, cos4, ALU.mult), r, "r1")
                link(dve.tensor_tensor(r4[:, :, 0, :], x4[:, :, 1, :], sin, ALU.mult), r, "r2")
                link(dve.tensor_tensor(r4[:, :, 1, :], x4[:, :, 0, :], sin, ALU.mult), r, "r3")
                link(dve.tensor_tensor(o4[:, :, 0, :], o4[:, :, 0, :], r4[:, :, 0, :], ALU.subtract), r, "q1")
                link(dve.tensor_tensor(o4[:, :, 1, :], o4[:, :, 1, :], r4[:, :, 1, :], ALU.add), r, "q2")

            def b4(r):
                dve.wait_ge(bpe.sem, bpe.at(r, "qkT"))
                dve.wait_ge(bact.sem, bact.at(r, "qT"))
                head = K[:, K_HEAD:K_HEAD + 8].unsqueeze(1).unsqueeze(3).to_broadcast([P, 2, 8, SLOTS])
                for g in range(2):
                    kt = B5[:, (2 + g) * P:(3 + g) * P].rearrange("p (q n) -> p q n", q=2).unsqueeze(2) \
                        .to_broadcast([P, 2, 8, SLOTS])
                    dve.tensor_tensor(KB[g].rearrange("p (q h n) -> p q h n", q=2, h=8), kt, head,
                                      ALU.mult).then_inc(bdve.sem, 1)

            def b5(r):
                dve.wait_ge(bact.sem, bact.at(r, "ms"))
                m = MS[:, 0:KC].unsqueeze(1).to_broadcast([P, 8, KC])
                for g in range(2):
                    sg = SC.rearrange("p (h k) -> p h k", h=H)[:, 8 * g:8 * g + 8, 0:KC]
                    mg = mx[:, 8 * g:8 * g + 8]
                    dve.wait_ge(bpe.sem, bpe.at(r, f"s{g}"))
                    s = bank[6 + g][:, :].rearrange("p (h k) -> p h k", h=8)[:, :, 0:KC]
                    link(dve.scalar_tensor_tensor(sg, s, HD ** -0.5, m, ALU.mult, ALU.add), r, f"sc{g}")
                    link(dve.tensor_reduce(mg, sg, AX.X, ALU.max), r, f"max{g}")
                    dve.tensor_tensor(sg, sg, mg.unsqueeze(2).to_broadcast([P, 8, KC]), ALU.subtract).then_inc(bdve.sem, 1)

            def b6(r):
                dve.wait_ge(bpe.sem, bpe.at(r, "at1"))
                dve.tensor_copy(AT[:, 4:8, :], B7[:, :].rearrange("p (h n) -> p h n", h=4)).then_inc(bdve.sem, 1)

            def b7(r):
                dve.wait_ge(bpe.sem, bpe.at(r, "pv"))
                o = B5[:, 0:H * VW].rearrange("p (h e) -> p h e", e=VW)
                link(dve.reciprocal(rden[:, :], o[:, :, HD]), r, "rden")
                link(dve.tensor_tensor(HN.rearrange("p (h e) -> p h e", e=HD), o[:, :, 0:HD],
                                       rden[:, :].unsqueeze(2).to_broadcast([P, H, HD]), ALU.mult), r, "on")

            def b9(r):
                dve.wait_ge(bpe.sem, bpe.at(r, "wo"))
                link(dve.tensor_tensor(X1S, B5[:, 0:D], HS, ALU.add), r, "x1s")
                rms(r, X1S, "ss2", "hn2")

            def b13(r):
                dve.wait_ge(bpe.sem, bpe.at(r, "w2"))
                link(dve.tensor_tensor(X1S, B5[:, 0:D], X1S, ALU.add), r, "x2")
                link(dve.tensor_tensor(bws[:, :], GS[:, C_W:C_W + 1], K[:, K_SEL:K_SEL + 1], ALU.mult), r, "ws")
                link(dve.tensor_scalar(FS, HS, GS[:, C_UNSEL:C_UNSEL + 1], None, ALU.mult), r, "ho")
                link(dve.scalar_tensor_tensor(FS, X1S, bws[:, 0:1], FS, ALU.mult, ALU.add), r, "f")
                dve.bn_stats(bst[:, :], FS).then_inc(bdve.sem, 1)
                dve.wait_ge(bdve.sem, bdve.at(r, "fst"))
                carry()
                link(dve.bn_aggr(bmv[:, :], bst[:, :]), r, "fag")
                link(dve.tensor_scalar(bve[:, :], bmv[:, 1:2], 1e-5, None, ALU.add), r, "fve")
                dve.wait_ge(bpool.sem, bpool.at(r, "f"))
                link(dve.tensor_scalar(FS, FS, bmv[:, 0:1], brs[:, 0:1], ALU.subtract, ALU.mult), r, "fn")
                dve.tensor_tensor(OS, FS, GS[:, 0:D], ALU.add).then_inc(bdve.sem, 1)

            def b14(r):
                dve.wait_ge(scattered, r * 16 + 16)

            AT_STEP = {1: b1, 3: b3, 4: b4, 5: b5, 6: b6, 7: b7, 9: b9, 13: b13, 14: b14}
            pair = [None]

            def do(name, t, q, k):
                if name == "pre_s":
                    pre_s(t, q)
                    if is_row(t, 0):
                        setup_win()
                elif name == "turn":
                    turn(t, k)
                    if is_row(t, 0) and k == 1:
                        setup_first()
                    if is_row(t, 1) and k == 1:
                        setup_tokens()
                elif name == "u":
                    convolve(t, k)
                elif name == "b":
                    if is_row(t, 0) and k == 0:
                        setup_more()
                    if is_row(t, 1) and k == 0:
                        setup_slots()
                    scan(t, k)
                elif name == "c":
                    c_and_gate(t, q, k)
                elif name == "post_a":
                    post_a(t, q)
                elif name == "post_x":
                    post_x(t, q)
                elif name == "post_h":
                    post_h(t, q)
                elif name == "rank":
                    rank_(t, q, k)
                elif name == "slots" and k in AT_STEP:
                    AT_STEP[k](t)

            run_all(dve, do)



_INS = ["L0_attn_x", "L0_attn_W_in", "L0_attn_b_in", "L0_attn_conv_w", "L0_attn_conv_b", "L0_attn_W_bc",
        "L0_attn_b_bc", "L0_attn_log_decay", "L0_attn_W_out", "L0_attn_b_out", "L0_ffn_attention_mask",
        "L0_ffn_position_ids", "L0_ffn_router_w", "L0_ffn_router_b", "L0_ffn_wq", "L0_ffn_wk", "L0_ffn_wv",
        "L0_ffn_wo", "L0_ffn_w1", "L0_ffn_w2", "L0_ffn_ln1", "L0_ffn_ln2"]


def kernel(**inputs):
    import concourse.bacc as bacc
    from concourse.bass_utils import run_bass_kernel_spmd

    nc = bacc.Bacc("TRN2", target_bir_lowering=False, num_devices=1)
    arrays = {f"in_{n}_dram": np.ascontiguousarray(inputs[n]) for n in _INS}
    arrays["in_shape_constants_dram"] = shape_constants()
    args = [nc.dram_tensor(n, a.shape, mybir.dt.from_np(a.dtype), kind="ExternalInput").ap()
            for n, a in arrays.items()]
    out = nc.dram_tensor("out_0_dram", (NB, NT, D), F32, kind="ExternalOutput").ap()
    build(nc, *args, out)
    r = run_bass_kernel_spmd(nc, [arrays], core_ids=[0])
    return r.results[0]["out_0_dram"]
```

```python
from contextlib import ExitStack

import numpy as np
import concourse.bass as bass
from concourse import mybir

P = 128
NB, NT, D = 8, 512, 256
DI, TAPS = 512, 4
H, HD, F = 16, 16, 1024
NP_ROWS, S_TAB = 4, 1024
SLOTS = int(0.125 * NT)
KC = SLOTS - 1
TT = NT // P
KD, KI, KF = D // P, DI // P, F // P
PAIRS = NB // 2
HP = H // 2
VW = HD + 1

F32 = mybir.dt.float32
F32R = mybir.dt.float32r
I32 = mybir.dt.int32
U32 = mybir.dt.uint32
ALU = mybir.AluOpType
ACT = mybir.ActivationFunctionType
AX = mybir.AxisListType

C_W, C_UNSEL, C_R, C_MR, C_R2, C_COS, C_SIN, C_MROW, C_OROW = (D + n for n in (0, 1, 2, 3, 4, 5, 13, 21, 22))
PAY = D + 23
TCW = PAY - C_COS
HALF = HD // 2

K_ID, K_TRI, K_IOTA, K_INV, K_MROW, K_OROW, K_HEAD, K_SEL = 0, 128, 640, 704, 712, 744, 776, 784
K_ALL = 785
R_BIN, R_BBC, R_CB, R_LD, R_LN1, R_LN2, R_ALL = 0, 8, 16, 20, 24, 26, 28

TWO_PI = 2.0 * np.pi
PI_A = 6.28125
PI_B = float(np.float32(np.round((TWO_PI - PI_A) * 2**16) / 2**16))
PI_C = float(np.float32(np.round((TWO_PI - PI_A - PI_B) * 2**25) / 2**25))
PI_D = float(np.float32(TWO_PI - PI_A - PI_B - PI_C))
MAGIC = 1.5 * 2.0**23


def shape_constants():
    c = np.zeros((P, K_ALL), np.float32)
    c[:, K_ID:K_ID + P] = np.eye(P)
    c[:, K_TRI:K_TRI + NT] = np.arange(NT)[None] >= np.arange(P)[:, None]
    c[:, K_IOTA:K_IOTA + SLOTS] = np.arange(SLOTS)
    c[:, K_INV:K_INV + HALF] = np.float32(1.0) / np.float32(10000.0) ** (np.arange(0, HD, 2, dtype=np.float32) / np.float32(HD))
    for b in range(NB):
        for i in range(TT):
            tok = P * i + np.arange(P)
            c[:, K_MROW + TT * b + i] = 2 * (min(b, NP_ROWS - 1) * S_TAB + tok)
            c[:, K_OROW + TT * b + i] = b * NT + tok
    c[:, K_HEAD:K_HEAD + 8] = (np.arange(P)[:, None] // HD) == np.arange(8)
    c[:, K_SEL] = (np.arange(P) % SLOTS) < KC
    return c


class Signal:

    def __init__(self, sem, events):
        self.sem, self.n, self.index = sem, len(events), {e: k + 1 for k, e in enumerate(events)}

    def at(self, rep, event=None):
        return rep * self.n + (self.index[event] if event is not None else self.n)


def began(rep):
    return not isinstance(rep, int) or rep >= 0


def build(nc, x, W_in, b_in, conv_w, conv_b, W_bc, b_bc, log_decay, W_out, b_out, mask, pos, router_w,
          router_b, wq, wk, wv, wo, w1, w2, ln1, ln2, consts, out):
    ctx = ExitStack()
    with ctx:
        def sb(name, shape, dt=F32):
            return ctx.enter_context(nc.sbuf_tensor(name, [P] + list(shape), dt))

        def semaphore(name):
            return ctx.enter_context(nc.semaphore(name))

        def signal(name, events):
            return Signal(semaphore(name), events)

        WinH, WinL = sb("WinH", [KD, 2 * DI], F32R), sb("WinL", [KD, 2 * DI], F32R)
        WbcH, WbcL = sb("WbcH", [KI, 2 * DI], F32R), sb("WbcL", [KI, 2 * DI], F32R)
        WoutH, WoutL = sb("WoutH", [KI, D], F32R), sb("WoutL", [KI, D], F32R)
        Wqkv, Wo = sb("Wqkv", [KD, 3 * D]), sb("Wo", [KD, D])
        W1, W2 = sb("W1", [KD, F]), sb("W2", [KF, D])
        K = sb("K", [K_ALL])
        ident = K[:, K_ID:K_ID + P]
        cols = sb("cols", [R_ALL])
        convw = sb("convw", [KI, TAPS])
        rw, bout, rb = sb("rw", [D]), sb("bout", [D]), sb("rb", [1])
        decay, hbin, vbias = sb("decay", [KI]), sb("hbin", [KI]), sb("vbias", [KI])
        tokc = sb("tokc", [NB, TT, TCW])

        X = sb("X", [2, TT, D])
        LNH, LNL = sb("LNH", [KD, NT], F32R), sb("LNL", [KD, NT], F32R)
        U = sb("U", [2, TAPS - 1 + NT])
        V = sb("V", [2, NT])
        S = sb("S", [2, NT])
        SH, SL = sb("SH", [KI, NT], F32R), sb("SL", [KI, NT], F32R)
        G = sb("G", [KI, NT])
        Y = sb("Y", [2, NT])
        rows = Y[:, 0, 0:P]
        posi = Y[:, 0, P:2 * P].bitcast(I32)
        posf = Y[:, 0, 2 * P:3 * P]
        YH, YL = sb("YH", [KI, NT], F32R), sb("YL", [KI, NT], F32R)
        A = sb("A", [TT, D])
        HB = sb("HB", [TT, D])
        XR = HB
        junk, junk_tie = (HB[:, k:k + 2, :].rearrange("p i d -> p (i d)") for k in (0, 2))
        pay = sb("pay", [2, TT, PAY])
        onehot = sb("onehot", [2, TT, SLOTS])
        tpos = sb("tpos", [NB * TT])
        stats, mv, ve, rs = sb("stats", [3, TT, 6]), sb("mv", [3, TT, 2]), sb("ve", [5, TT]), sb("rs", [4, TT])
        neg, negr = sb("neg", [3, TT]), sb("negr", [2, TT])
        half = sb("half", [TT])
        nge, tie, rank = sb("nge", [TT]), sb("tie", [TT]), sb("rank", [TT])

        big = sb("big", [7168])
        used = [0]

        def carve(n):
            used[0] += n
            assert used[0] <= 7168
            return big[:, used[0] - n:used[0]]

        GS, MR, HS, HN = carve(PAY), carve(NT), carve(D), carve(D)
        HT = carve(D).rearrange("p (k n) -> p k n", k=KD)
        MT = carve(NT).rearrange("p (k n) -> p k n", k=TT)
        QK, RT = carve(2 * D), carve(2 * D)
        QT = carve(D).rearrange("p (k n) -> p k n", k=KD)
        KB0, SC, AT_ = carve(1024), carve(1024), carve(1024)
        VB = carve(2 * HP * 2 * VW).rearrange("p (q h e) -> p q h e", q=2, h=HP)
        MS = carve(SLOTS)
        KB = [KB0, AT_]
        AT = AT_.rearrange("p (h n) -> p h n", h=HP)
        HTT = AT_[:, 0:2 * D].rearrange("p (k q n) -> p k q n", k=KD, q=2)
        GE = KB0.rearrange("p (k n) -> p k n", k=KF)
        X1S, FS, OS = QK[:, 0:D], QK[:, D:2 * D], RT[:, 0:D]
        rawin = big[:, 0:2048].rearrange("p (k n) -> p k n", k=KD)
        rawbc = big[:, 2048:6144].rearrange("p (k n) -> p k n", k=KI)
        rawout = big[:, 6144:7168].rearrange("p (k n) -> p k n", k=KI)
        idx = sb("idx", [2, 2], U32)
        bst, bmv, bve, brs, bss, bws = (sb("bst", [6]), sb("bmv", [2]), sb("bve", [1]), sb("brs", [1]),
                                        sb("bss", [1]), sb("bws", [1]))
        spare = sb("spare", [3])
        mx, rden = sb("mx", [H]), sb("rden", [H])
        bhalf = half[:, 0:1]
        ang = A[:, 0, :].rearrange("p (r f) -> p r f", f=HALF)
        trn = A[:, 1, :].rearrange("p (r f) -> p r f", f=HALF)
        red = A[:, 2, :].rearrange("p (r f) -> p r f", f=HALF)

        bank = [ctx.enter_context(nc.psum_tensor(f"bank{i}", [P, 512], F32)) for i in range(8)]
        TURN, B5, B6, B7 = bank[4], bank[5], bank[6], bank[7]

        s_ident, s_k, s_vec, s_win, s_wbc, s_wout, s_wb = (semaphore(n) for n in (
            "identity_in", "consts_in", "vectors_in", "win_in", "wbc_in", "wout_in", "wb_in"))
        x_in, xr_in, out_stored, mask_in, scattered = (semaphore(n) for n in (
            "x_in", "xr_in", "out_stored", "mask_in", "scattered"))
        set_pe = signal("set_pe", ["vectors", "positions"])
        set_act = signal("set_act", ["win", "edecay", "hbin", "wbc", "wout", "sin", "cos"])
        set_pool = signal("set_pool", ["wbc"])
        set_dve = signal("set_dve", ["half", "winh", "win", "pos", "cols", "tokpos", "pad", "vb1", "vbias", "wbch",
                                     "wbcl", "ed1", "decay", "wout", "rows"] + [f"ang{i}" for i in range(17)]
                         + ["ln1a", "ln1b", "ln2a", "ln2b", "zero", "one0", "one1", "sczero"])
        T4, C4 = range(TT), range(KI)
        pre = signal("norm_x", [f"{k}{i}" for k in ("st", "ag") for i in T4] + ["ve", "neg"])
        roots = signal("roots", ["x", "mx"])
        x_norm = signal("x_norm", [f"{i}" for i in T4])
        roots_post = signal("roots_post", ["a", "ma", "x1", "mx1", "h", "rms"])
        turned = signal("turned", ["t0", "t1"])
        ln_hi, ln_lo = signal("ln_hi", ["k0", "k1"]), signal("ln_lo", ["k0", "k1"])
        win = signal("win", ["u0", "u1", "g0", "u2", "g1", "u3", "g2", "g3"])
        u_out = signal("u_out", [f"{k}{c}" for c in C4 for k in "uv"])
        g_out = signal("g_out", [f"g{c}" for c in C4])
        conv = signal("conv", [f"{c}{j}" for c in C4 for j in range(TAPS - 1)])
        s_hi, s_lo = signal("s_hi", [f"{k}{c}" for c in C4 for k in ("", "r")]), signal("s_lo", [f"r{c}" for c in C4])
        wbc = signal("wbc", [f"{k}{c}" for c in C4 for k in "bc"])
        b_out_ = signal("b_out", [f"{c}" for c in C4])
        ssm = signal("ssm", [f"{k}{c}" for c in C4 for k in ("scan", "c", "y")])
        y_hi, y_lo = signal("y_hi", [f"{c}" for c in C4]), signal("y_lo", [f"{c}" for c in C4])
        wout = signal("wout", [f"{i}" for i in T4])
        post = signal("post", ["a0", "a1", "as0", "as1", "a2", "a3", "as2", "as3"]
                      + [f"aa{i}" for i in T4] + ["ave", "aneg"]
                      + [f"{k}{i}" for k in ("xs", "xg") for i in T4] + ["xve", "xneg"] + ["v1", "v2", "hve", "rve"]
                      + [f"w{i}" for i in T4] + ["wb"])
        scaled = signal("scaled", [f"{k}{i}" for k in "nhz" for i in T4])
        x1_out = signal("x1_out", ["tokc"] + [f"{k}{i}" for k in ("x1", "out") for i in T4])
        wrow = signal("wrow", [f"{i}" for i in T4])
        ranked = signal("ranked", [f"{k}{i}" for i in T4 for k in ("nge", "tie")] + ["rank", "unsel"]
                        + [f"hot{i}" for i in T4])
        bpe = signal("slots_pe", ["gather", "hnT", "qk", "v", "maskT", "qkT", "mask", "s0", "s1", "at0", "at1", "pv",
                                  "oT", "wo", "hn2T", "w1a", "w1b", "w2"])
        bact = signal("slots_act", ["gs", "hnT", "hnTT0", "hnTT1", "v00", "v01", "v10", "v11", "mt", "qT", "ms", "exp0",
                                    "exp1", "at0", "oT", "hn2T", "ge0", "ge1"])
        bdve = signal("slots_dve", ["hs", "idx", "hn", "r1", "r2", "r3", "q1", "q2", "kb00", "kb01", "kb10",
                                    "kb11", "sc0", "max0", "sc1", "sub0", "max1", "sub1", "at1", "rden", "on", "x1s",
                                    "ss2", "ss2ve", "hn2", "ws", "ho", "x2", "f", "fst", "fag", "fve", "fn", "os"])
        bpool = signal("slots_roots", ["hn2", "f"])

        x_rows = x.rearrange("b (i p) d -> b p i d", p=P)
        out_rows = out.rearrange("b (i p) d -> b p i d", p=P)
        mask_rows = mask.rearrange("b o s (h c) -> (b o s h) c", c=NT)
        out_flat = out.rearrange("b n d -> (b n) d")
        block = ctx.enter_context(nc.Block())

        def turn_bank(t, k):
            return B6 if is_row(t, 0) and k == 1 else TURN

        INTO = [("u", 0), ("u", 1), ("g", 0), ("u", 2), ("g", 1), ("u", 3), ("g", 2), ("g", 3)]

        def into_bank(c, q, which):
            n = INTO.index((which, c))
            return 2 * ((n // 2 + q) % 2) + n % 2

        def out_pair(q):
            return 1 - q

        def b_pair(c, q):
            return (c + 1 + q) % 2

        ROW = [("u", 0), ("u", 1), ("g", 0), ("silu", 0), ("u", 2), ("g", 1), ("silu", 1), ("u", 3), ("g", 2),
               ("g", 3), ("silu", 2), ("silu", 3), ("pre_s", 0), ("post_a", 0), ("out_of", 0), ("b", 0),
               ("pre_n", 0), ("c", 0), ("turn", 0), ("post_n", 0), ("post_x", 0), ("yhi", 0), ("b", 1),
               ("post_h", 0), ("turn", 1), ("c", 1), ("b", 2), ("c", 2), ("spread", 0), ("yhi", 1), ("rank", 0),
               ("post_z", 0), ("rank", 1), ("b", 3), ("rank", 2), ("c", 3), ("rank", 3), ("yhi", 2), ("yhi", 3),
               ("rank", 4)]
        SLOT_STEPS = {1: {("silu", 0): (1,), ("out_of", 0): (2,), ("post_n", 0): (3,), ("post_x", 0): (4,),
                          ("turn", 1): (5,), ("yhi", 1): (6,), ("rank", 2): (7,), ("c", 3): (8,)},
                      0: {("u", 0): (9,), ("g", 1): (10,), ("g", 3): (11,), ("turn", 0): (12,),
                          ("post_n", 0): (13,), ("b", 1): (14,)}}
        ENDING = [("u", 7, 0), ("u", 7, 1), ("g", 7, 0), ("silu", 7, 0), ("u", 7, 2), ("g", 7, 1),
                  ("silu", 7, 1), ("u", 7, 3), ("slots", 2, 1), ("g", 7, 2), ("silu", 7, 2), ("silu", 7, 3),
                  ("g", 7, 3), ("post_a", 6, 0), ("out_of", 6, 0), ("slots", 2, 2), ("b", 7, 0), ("c", 7, 0),
                  ("post_n", 6, 0), ("yhi", 7, 0), ("slots", 2, 3), ("post_x", 6, 0), ("slots", 2, 4),
                  ("b", 7, 1), ("post_h", 6, 0), ("c", 7, 1), ("slots", 2, 5), ("b", 7, 2), ("c", 7, 2),
                  ("spread", 6, 0), ("slots", 2, 6), ("rank", 6, 0), ("rank", 6, 1), ("yhi", 7, 1),
                  ("post_z", 6, 0), ("yhi", 7, 2), ("b", 7, 3), ("slots", 2, 7), ("c", 7, 3), ("slots", 2, 8),
                  ("rank", 6, 2), ("rank", 6, 3), ("yhi", 7, 3), ("rank", 6, 4), ("slots", 2, 9),
                  ("out_of", 7, 0), ("warm", 0, 3), ("slots", 2, 10), ("post_a", 7, 0), ("post_n", 7, 0),
                  ("post_x", 7, 0), ("slots", 2, 11), ("warm", 0, 11), ("post_h", 7, 0), ("slots", 2, 12),
                  ("spread", 7, 0), ("rank", 7, 0), ("post_z", 7, 0), ("rank", 7, 1), ("rank", 7, 2),
                  ("warm", 0, 9), ("rank", 7, 3), ("rank", 7, 4), ("warm", 0, 3), ("slots", 2, 13),
                  ("slots", 3, 1), ("warm", 0, 6), ("slots", 3, 2), ("slots", 2, 14), ("slots", 3, 3),
                  ("slots", 3, 4), ("slots", 3, 5), ("warm", 0, 11), ("slots", 3, 6), ("slots", 3, 7),
                  ("warm", 0, 4), ("slots", 3, 8), ("slots", 3, 9), ("warm", 0, 9), ("warm", 0, 2),
                  ("slots", 3, 10), ("slots", 3, 11), ("slots", 3, 12), ("slots", 3, 13)]
        NEXT = ("pre_s", "pre_n", "turn")
        BEFORE = ("out_of", "post_a", "post_n", "post_x", "post_h", "post_z", "spread", "rank")

        def run_row(do, t, q, r=None, first=False):
            for step in ROW:
                name, k = step
                if name in BEFORE:
                    if not first:
                        do(name, t - 1, 1 - q, k)
                elif name in NEXT:
                    do(name, t + 1, 1 - q, k)
                else:
                    do(name, t, q, k)
                if r is not None:
                    for n in SLOT_STEPS[q].get(step, ()):
                        do("slots", r, 0, n)

        def run_all(eng, do):
            do("pre_s", 0, 0, 0)
            do("pre_n", 0, 0, 0)
            do("turn", 0, 0, 0)
            do("turn", 0, 0, 1)
            run_row(do, 0, 0, first=True)
            run_row(do, 1, 1)
            run_row(do, 2, 0)
            with eng.Fori(1, PAIRS - 1) as p:
                run_row(do, p * 2 + 1, 1, r=p - 1)
                run_row(do, p * 2 + 2, 0, r=p - 1)
            for name, t, k in ENDING:
                do(name, t, t % 2, k)

        def idx_of(r, which):
            last = 1 if isinstance(r, int) and r == PAIRS - 1 else 0
            return idx[:, last, which:which + 1] if which is not None else idx[:, last, :]

        def is_row(t, n):
            return isinstance(t, int) and t == n

        @block.sync
        def _(sp):
            sp.dma_start(ident, consts[:, K_ID:K_ID + P]).then_inc(s_ident, 16)
            sp.dma_start(X[:, 0], x_rows[0]).then_inc(x_in, 16)
            sp.dma_start(rawin, W_in.rearrange("(k p) n -> p k n", p=P)).then_inc(s_win, 16)
            for v, r, n in ((b_in, R_BIN, 8), (b_bc, R_BBC, 8), (conv_b, R_CB, 4), (log_decay, R_LD, 4),
                            (ln1, R_LN1, 2), (ln2, R_LN2, 2)):
                sp.dma_start(rows[r:r + n, :], v.rearrange("(r p) -> r p", p=P)).then_inc(s_vec, 16)
            sp.dma_start(posi[0:16, :], pos[:, 0:NT].rearrange("b (i p) -> b i p", p=P)).then_inc(s_vec, 16)
            sp.dma_start(convw[:, :, :], conv_w.rearrange("(c p) o j -> p c (o j)", p=P)).then_inc(s_vec, 16)
            sp.dma_start(rw[:, :], router_w.rearrange("d o -> o d").to_broadcast([P, D])).then_inc(s_vec, 16)
            sp.dma_start(bout[:, :], b_out.rearrange("(o d) -> o d", o=1).to_broadcast([P, D])).then_inc(s_vec, 16)
            sp.dma_start(rb[:, :], router_b.rearrange("(o d) -> o d", o=1).to_broadcast([P, 1])).then_inc(s_vec, 16)
            sp.dma_start(K[:, P:], consts[:, P:]).then_inc(s_k, 16)
            sp.dma_start(rawbc, W_bc.rearrange("(k p) n -> p k n", p=P)).then_inc(s_wbc, 16)
            sp.dma_start(rawout, W_out.rearrange("(k p) n -> p k n", p=P)).then_inc(s_wout, 16)
            sp.wait_ge(pre.sem, pre.at(0, "st0"))
            sp.dma_start(X[:, 1], x_rows[1]).then_inc(x_in, 16)
            for j, w in enumerate((wq, wk, wv)):
                sp.dma_start(Wqkv[:, :, j * D:(j + 1) * D], w.rearrange("(k p) n -> p k n", p=P)).then_inc(s_wb, 16)
            sp.dma_start(Wo[:, :, :], wo.rearrange("(k p) n -> p k n", p=P)).then_inc(s_wb, 16)
            sp.dma_start(W1[:, :, :], w1.rearrange("(k p) n -> p k n", p=P)).then_inc(s_wb, 16)
            sp.dma_start(W2[:, :, :], w2.rearrange("(k p) n -> p k n", p=P)).then_inc(s_wb, 16)

            def residual(t):
                if began(t - 1):
                    sp.wait_ge(ranked.sem, ranked.at(t - 1))
                sp.dma_start(XR[:, :, :], x_rows[t]).then_inc(xr_in, 16)

            def next_x(t, q):
                if began(t - 2):
                    sp.wait_ge(turned.sem, turned.at(t - 2))
                sp.wait_ge(pre.sem, pre.at(t - 1, "st0"))
                sp.dma_start(X[:, q], x_rows[t]).then_inc(x_in, 16)

            def store(t):
                sp.wait_ge(x1_out.sem, x1_out.at(t))
                sp.dma_start(out_rows[t], A[:, :, :]).then_inc(out_stored, 16)

            residual(0)
            next_x(2, 0)
            store(0)
            residual(1)
            with sp.Fori(1, PAIRS - 1) as p:
                next_x(p * 2 + 1, 1)
                store(p * 2 - 1)
                residual(p * 2)
                next_x(p * 2 + 2, 0)
                store(p * 2)
                residual(p * 2 + 1)
            next_x(NB - 1, 1)
            store(NB - 3)
            residual(NB - 2)
            store(NB - 2)
            residual(NB - 1)
            store(NB - 1)
            sp.wait_ge(out_stored, 16 * NB)
            sp.wait_ge(scattered, 16 * PAIRS)

        @block.tensor
        def _(pe):
            def split_product(o, wh, wl, ah, al, n_k, w_cols, a_cols, done, weights_move, parts=None, t=None):
                n = 0
                for k in range(n_k):
                    if parts is not None:
                        hi, lo, event = parts
                        pe.wait_ge(hi.sem, hi.at(t, f"{event}{k}"))
                        pe.wait_ge(lo.sem, lo.at(t, f"{event}{k}"))
                    for w, a in ((wh, ah), (wh, al), (wl, ah)):
                        ws, as_ = w[:, k, w_cols], a[:, k, a_cols]
                        l, r = (as_, ws) if weights_move else (ws, as_)
                        mm = pe.matmul(o, l, r, start=(n == 0), stop=(n == 3 * n_k - 1))
                        n += 1
                mm.then_inc(done, 1)

            def keep_warm(n):
                for _ in range(n):
                    pe.matmul(bank[3][:, 0:P], ident, ident, start=True, stop=True)

            def turn_vectors():
                pe.wait_ge(s_vec, 16 * 11)
                pe.transpose(B5[:, 0:R_ALL], rows[0:R_ALL, :], ident[0:R_ALL, 0:R_ALL]).then_inc(set_pe.sem, 1)
                pe.wait_ge(set_dve.sem, set_dve.at(0, "pos"))
                pe.transpose(B5[:, 32:48], posf[0:16, :], ident[0:16, 0:16]).then_inc(set_pe.sem, 1)

            def turn(t, q, k):
                if k == 0:
                    if not is_row(t, 1):
                        if began(t - 3):
                            pe.wait_ge(ranked.sem, ranked.at(t - 3, "tie3"))
                    if began(t - 1):
                        pe.wait_ge(ln_lo.sem, ln_lo.at(t - 1))
                elif not is_row(t, 0):
                    pe.wait_ge(ln_hi.sem, ln_hi.at(t, "k0"))
                    pe.wait_ge(ln_lo.sem, ln_lo.at(t, "k0"))
                for i in T4:
                    if k == 0:
                        pe.wait_ge(x_norm.sem, x_norm.at(t, f"{i}"))
                    mm = pe.transpose(turn_bank(t, k)[:, i * P:(i + 1) * P], X[:, q, i, k * P:(k + 1) * P], ident)
                mm.then_inc(turned.sem, 1)

            def into(t, q, c, j):
                if c == 0 and j == 0 and is_row(t, 0):
                    pe.wait_ge(set_dve.sem, set_dve.at(0, "win"))
                n = INTO.index(("ug"[j], c))
                if n < 4:
                    if began(t - 1):
                        if n % 2 == 0:
                            pe.wait_ge(b_out_.sem, b_out_.at(t - 1, f"{2 + n // 2}"))
                        else:
                            pe.wait_ge(ssm.sem, ssm.at(t - 1, f"c{2 + n // 2}"))
                else:
                    before, c_before = INTO[n - 4]
                    if before == "u":
                        pe.wait_ge(u_out.sem, u_out.at(t, f"v{c_before}"))
                    else:
                        pe.wait_ge(g_out.sem, g_out.at(t, f"g{c_before}"))
                b = into_bank(c, q, "ug"[j])
                m = 4 * j + c
                split_product(bank[b][:, :], WinH, WinL, LNH, LNL, KD, slice(m * P, (m + 1) * P),
                              slice(0, NT), win.sem, False, (ln_hi, ln_lo, "k") if c == 0 and j == 0 else None, t)

            def out_of(t, q):
                b = 2 * out_pair(q)
                for i in T4:
                    if i % 2 == 0:
                        if is_row(t, NB - 1):
                            pe.wait_ge(ssm.sem, ssm.at(t, "c2"))
                        elif i == 0:
                            pe.wait_ge(g_out.sem, g_out.at(t + 1, "g1"))
                        else:
                            pe.wait_ge(u_out.sem, u_out.at(t + 1, "v3"))
                    split_product(bank[b + i // 2][:, (i % 2) * D:(i % 2 + 1) * D], WoutH, WoutL, YH, YL, KI,
                                  slice(0, D), slice(i * P, (i + 1) * P), wout.sem, True,
                                  (y_hi, y_lo, "") if i == 0 else None, t)

            def bc(t, q, c, j):
                if c == 0 and j == 0:
                    if is_row(t, 0):
                        pe.wait_ge(set_pool.sem, set_pool.at(0, "wbc"))
                        pe.wait_ge(set_dve.sem, set_dve.at(0, "wbcl"))
                if c == 0:
                    pe.wait_ge(g_out.sem, g_out.at(t, "g3" if j else "g2"))
                elif c == 1:
                    if began(t - 1):
                        pe.wait_ge(post.sem, post.at(t - 1, "a3" if j else "a1"))
                elif j == 0:
                    pe.wait_ge(b_out_.sem, b_out_.at(t, f"{c - 2}"))
                else:
                    pe.wait_ge(ssm.sem, ssm.at(t, f"c{c - 2}"))
                m = 4 * j + c
                split_product(bank[2 * b_pair(c, q) + j][:, :], WbcH, WbcL, SH, SL, KI, slice(m * P, (m + 1) * P),
                              slice(0, NT), wbc.sem, False, (s_hi, s_lo, "r") if c == 0 and j == 0 else None, t)

            def spread(t, q):
                pe.wait_ge(post.sem, post.at(t, "wb"))
                if is_row(t, NB - 1) or is_row(t, NB - 2):
                    if began(t - 1):
                        pe.wait_ge(ranked.sem, ranked.at(t - 1))
                else:
                    pe.wait_ge(ln_lo.sem, ln_lo.at(t + 2))
                for i in T4:
                    pe.transpose(TURN[:, i * P:(i + 1) * P],
                                 pay[:, q, i, C_W:C_W + 1].to_broadcast([P, P]), ident).then_inc(wrow.sem, 1)

            half_rows = [slice(0, 64), slice(64, 128)]

            def b1(r):
                for q in range(2):
                    pe.wait_ge(x1_out.sem, x1_out.at(r * 2 + q, "x13"))
                    pe.wait_ge(roots_post.sem, roots_post.at(r * 2 + q))
                    pe.wait_ge(ranked.sem, ranked.at(r * 2 + q))
                    for i in T4:
                        mm = pe.matmul(B5[half_rows[q], 0:PAY], onehot[:, q, i, :], pay[:, q, i, :],
                                       start=(i == 0), stop=(i == TT - 1))
                mm.then_inc(bpe.sem, 1)

            def b2(r):
                pe.wait_ge(bdve.sem, bdve.at(r, "hn"))
                for k in range(KD):
                    mm = pe.transpose(B6[:, k * P:(k + 1) * P], HN[:, k * P:(k + 1) * P], ident)
                mm.then_inc(bpe.sem, 1)

            def b3(r):
                pe.wait_ge(bact.sem, bact.at(r, "hnT"))
                for k in range(KD):
                    mm = pe.matmul(B5[:, :], HT[:, k, :], Wqkv[:, k, 0:2 * D], start=(k == 0), stop=(k == KD - 1))
                mm.then_inc(bpe.sem, 1)
                pe.wait_ge(bact.sem, bact.at(r, "hnTT1"))
                for q in range(2):
                    for k in range(KD):
                        mm = pe.matmul(B6[:, q * D:(q + 1) * D], HTT[:, k, q, :], Wqkv[:, k, 2 * D:3 * D],
                                       start=(k == 0), stop=(k == KD - 1))
                mm.then_inc(bpe.sem, 1)
                pe.wait_ge(mask_in, r * 16 + 16)
                for k in T4:
                    mm = pe.transpose(B7[:, k * P:(k + 1) * P], MR[:, k * P:(k + 1) * P], ident)
                mm.then_inc(bpe.sem, 1)

            def b4(r):
                pe.wait_ge(bdve.sem, bdve.at(r, "q2"))
                for k in range(4):
                    mm = pe.transpose(B5[:, k * P:(k + 1) * P], QK[:, k * P:(k + 1) * P], ident)
                mm.then_inc(bpe.sem, 1)
                pe.wait_ge(bact.sem, bact.at(r, "mt"))
                for q in range(2):
                    for k in T4:
                        mm = pe.matmul(B7[half_rows[q], 0:SLOTS], MT[:, k, half_rows[q]], onehot[:, q, k, :],
                                       start=(k == 0), stop=(k == TT - 1))
                mm.then_inc(bpe.sem, 1)

            def b5(r):
                pe.wait_ge(bact.sem, bact.at(r, "qT"))
                for g in range(2):
                    if g == 0:
                        pe.wait_ge(bact.sem, bact.at(r, "v11"))
                    else:
                        pe.wait_ge(bact.sem, bact.at(r, "ms"))
                    for q in range(2):
                        pe.wait_ge(bdve.sem, bdve.at(r, f"kb{g}{q}"))
                        kb = KB[g].rearrange("p (q n) -> p q n", q=2)
                        mm = pe.matmul(bank[6 + g][half_rows[q], :], QT[:, g, half_rows[q]], kb[:, q, :],
                                       start=True, stop=True)
                    mm.then_inc(bpe.sem, 1)

            def b6(r):
                for g in range(2):
                    pe.wait_ge(bact.sem, bact.at(r, f"exp{g}"))
                    for k in range(4):
                        hp = 4 * g + k
                        mm = pe.transpose(bank[6 + g][:, k * P:(k + 1) * P], SC[:, hp * P:(hp + 1) * P], ident)
                    mm.then_inc(bpe.sem, 1)

            def b7(r):
                for g in range(2):
                    if g == 0:
                        pe.wait_ge(bact.sem, bact.at(r, "at0"))
                    else:
                        pe.wait_ge(bdve.sem, bdve.at(r, "at1"))
                    for q, hp in ((q, 4 * g + k) for q in range(2) for k in range(4)):
                        mm = pe.matmul(B5[half_rows[q], hp * 2 * VW:(hp + 1) * 2 * VW], AT[:, hp, half_rows[q]],
                                       VB[:, q, hp, :], start=True, stop=True)
                mm.then_inc(bpe.sem, 1)

            def b8(r):
                pe.wait_ge(bdve.sem, bdve.at(r, "on"))
                for k in range(KD):
                    mm = pe.transpose(B6[:, k * P:(k + 1) * P], HN[:, k * P:(k + 1) * P], ident)
                mm.then_inc(bpe.sem, 1)

            def b9(r):
                pe.wait_ge(bact.sem, bact.at(r, "oT"))
                for k in range(KD):
                    mm = pe.matmul(B5[:, 0:D], HT[:, k, :], Wo[:, k, :], start=(k == 0), stop=(k == KD - 1))
                mm.then_inc(bpe.sem, 1)

            def b10(r):
                pe.wait_ge(bdve.sem, bdve.at(r, "hn2"))
                for k in range(KD):
                    mm = pe.transpose(B6[:, k * P:(k + 1) * P], HN[:, k * P:(k + 1) * P], ident)
                mm.then_inc(bpe.sem, 1)

            def b11(r):
                pe.wait_ge(bact.sem, bact.at(r, "hn2T"))
                for m in range(KF):
                    for k in range(KD):
                        mm = pe.matmul(bank[6 + m // 4][:, (m % 4) * P:(m % 4 + 1) * P], W1[:, k, m * P:(m + 1) * P],
                                       HT[:, k, :], start=(k == 0), stop=(k == KD - 1))
                    if m % 4 == 3:
                        mm.then_inc(bpe.sem, 1)

            def b12(r):
                for m in range(KF):
                    if m % 4 == 0:
                        pe.wait_ge(bact.sem, bact.at(r, f"ge{m // 4}"))
                    mm = pe.matmul(B5[:, 0:D], GE[:, m, :], W2[:, m, :], start=(m == 0), stop=(m == KF - 1))
                mm.then_inc(bpe.sem, 1)

            def b13(r):
                pe.wait_ge(bdve.sem, bdve.at(r, "x2"))

            B = [b1, b2, b3, b4, b5, b6, b7, b8, b9, b10, b11, b12, b13]

            def do(name, t, q, k):
                if name == "turn":
                    turn(t, q, k)
                    if is_row(t, 0) and k == 1:
                        turn_vectors()
                elif name in "ug":
                    into(t, q, k, "ug".index(name))
                elif name == "out_of":
                    out_of(t, q)
                elif name in "bc":
                    bc(t, q, k, "bc".index(name))
                elif name == "spread":
                    spread(t, q)
                elif name == "warm":
                    keep_warm(k)
                elif name == "slots" and k <= len(B):
                    B[k - 1](t)

            pe.wait_ge(s_ident, 16)
            run_all(pe, do)

        @block.scalar
        def _(act):
            act.wait_ge(s_win, 16)
            act.copy(WinH[:, 0, :], rawin[:, 0, :]).then_inc(set_act.sem, 1)
            flat = tokc[:, :, :, :].rearrange("p b i c -> p (b i) c")

            def setup_more():
                act.wait_ge(set_dve.sem, set_dve.at(0, "cols"))
                act.activation(decay[:, :], cols[:, R_LD:R_LD + KI], ACT.Exp).then_inc(set_act.sem, 1)
                act.mul(hbin[:, :], cols[:, R_BIN + KI:R_BIN + 2 * KI], 0.5).then_inc(set_act.sem, 1)
                act.wait_ge(s_wbc, 16)
                act.copy(WbcH[:, 0:2, :], rawbc[:, 0:2, :]).then_inc(set_act.sem, 1)

            def setup_wout():
                act.wait_ge(s_wout, 16)
                act.mul(WoutH[:, :, :], rawout, 0.5).then_inc(set_act.sem, 1)

            def trig():
                act.wait_ge(set_dve.sem, set_dve.at(0, "ang16"))
                act.activation(flat[:, :, HALF:2 * HALF], ang, ACT.Sin).then_inc(set_act.sem, 1)
                act.activation(flat[:, :, 0:HALF], red, ACT.Sin).then_inc(set_act.sem, 1)

            def scale_tiles(root, mean_root, dst, src, done):
                for i in T4:
                    act.activation(dst(i), src(i), ACT.Identity, bias=mean_root(i),
                                   scale=root(i)).then_inc(done.sem, 1)

            def pre_n(t, q):
                act.wait_ge(roots.sem, roots.at(t))
                scale_tiles(lambda i: rs[:, 0, i:i + 1], lambda i: negr[:, 0, i:i + 1],
                            lambda i: X[:, q, i, :], lambda i: X[:, q, i, :], x_norm)

            def post_n(t):
                act.wait_ge(roots_post.sem, roots_post.at(t, "ma"))
                scale_tiles(lambda i: rs[:, 1, i:i + 1], lambda i: negr[:, 1, i:i + 1],
                            lambda i: A[:, i, :], lambda i: A[:, i, :], scaled)

            def post_h(t, q):
                act.wait_ge(roots_post.sem, roots_post.at(t, "mx1"))
                scale_tiles(lambda i: pay[:, q, i, C_R:C_R + 1], lambda i: pay[:, q, i, C_MR:C_MR + 1],
                            lambda i: HB[:, i, :], lambda i: pay[:, q, i, 0:D], scaled)

            def post_z(t):
                act.wait_ge(roots_post.sem, roots_post.at(t, "h"))
                act.wait_ge(scaled.sem, scaled.at(t, "h3"))
                act.wait_ge(post.sem, post.at(t, "w3"))
                for i in T4:
                    act.activation(A[:, i, :], HB[:, i, :], ACT.Copy, scale=rs[:, 3, i:i + 1]).then_inc(scaled.sem, 1)

            def turn(t, k):
                act.wait_ge(turned.sem, turned.at(t, f"t{k}"))
                if began(t - 1):
                    act.wait_ge(win.sem, win.at(t - 1))
                act.copy(LNH[:, k, :], turn_bank(t, k)[:, :]).then_inc(ln_hi.sem, 1)

            def u(t, q, c):
                act.wait_ge(win.sem, win.at(t, f"u{c}"))
                if c < 2:
                    if began(t - 1):
                        act.wait_ge(s_hi.sem, s_hi.at(t - 1, f"r{c + 2}"))
                else:
                    act.wait_ge(s_hi.sem, s_hi.at(t, f"r{c - 2}"))
                if is_row(t, 0) and c == 0:
                    act.wait_ge(set_dve.sem, set_dve.at(0, "vbias"))
                act.activation(U[:, c % 2, TAPS - 1:], bank[into_bank(c, q, "u")][:, :], ACT.Identity,
                               bias=cols[:, R_BIN + c:R_BIN + c + 1]).then_inc(u_out.sem, 1)
                act.activation(V[:, c % 2, :], bank[into_bank(c, q, "u")][:, :], ACT.Identity, bias=vbias[:, c:c + 1],
                               scale=convw[:, c, TAPS - 1:TAPS]).then_inc(u_out.sem, 1)

            def silu(t, c):
                act.wait_ge(conv.sem, conv.at(t, f"{c}2"))
                if c >= 2:
                    act.wait_ge(s_lo.sem, s_lo.at(t, f"r{c - 2}"))
                elif began(t - 1):
                    act.wait_ge(s_lo.sem, s_lo.at(t - 1, f"r{c + 2}"))
                act.activation(S[:, c % 2, :], V[:, c % 2, :], ACT.Silu).then_inc(s_hi.sem, 1)
                if began(t - 1):
                    act.wait_ge(wbc.sem, wbc.at(t - 1))
                act.activation(SH[:, c, :], V[:, c % 2, :], ACT.Silu).then_inc(s_hi.sem, 1)

            def gate(t, q, c):
                act.wait_ge(win.sem, win.at(t, f"g{c}"))
                if is_row(t, 0) and c == 0:
                    act.wait_ge(set_act.sem, set_act.at(0, "hbin"))
                if began(t - 1):
                    act.wait_ge(ssm.sem, ssm.at(t - 1, f"y{c}"))
                act.activation(G[:, c, :], bank[into_bank(c, q, "g")][:, :], ACT.Tanh, bias=hbin[:, c:c + 1],
                               scale=0.5).then_inc(g_out.sem, 1)

            def bout_(t, q, c):
                act.wait_ge(wbc.sem, wbc.at(t, f"b{c}"))
                if c >= 2:
                    act.wait_ge(y_lo.sem, y_lo.at(t, f"{c - 2}"))
                else:
                    if began(t - 1):
                        act.wait_ge(y_lo.sem, y_lo.at(t - 1, f"{c + 2}"))
                act.activation(Y[:, c % 2, :], bank[2 * b_pair(c, q)][:, :], ACT.Identity,
                               bias=cols[:, R_BBC + c:R_BBC + c + 1]).then_inc(b_out_.sem, 1)

            def yhi(t, c):
                act.wait_ge(ssm.sem, ssm.at(t, f"y{c}"))
                if began(t - 1):
                    act.wait_ge(wout.sem, wout.at(t - 1))
                act.copy(YH[:, c, :], Y[:, c % 2, :]).then_inc(y_hi.sem, 1)

            def b1(r):
                act.wait_ge(bpe.sem, bpe.at(r, "gather"))
                act.copy(GS, B5[:, 0:PAY]).then_inc(bact.sem, 1)

            def b2(r):
                act.wait_ge(bpe.sem, bpe.at(r, "hnT"))
                act.copy(HT, B6[:, 0:D].rearrange("p (k n) -> p k n", k=KD)).then_inc(bact.sem, 1)

                for k in range(KD):
                    act.copy(HTT[:, k, :, :].rearrange("p q (e n) -> p q e n", e=2),
                             B6[:, k * P:(k + 1) * P].rearrange("p (q n) -> p q n", q=2).unsqueeze(2)
                             .to_broadcast([P, 2, 2, SLOTS])).then_inc(bact.sem, 1)

            def b3(r):
                act.wait_ge(bpe.sem, bpe.at(r, "v"))
                for q in range(2):
                    v = B6[:, q * D:(q + 1) * D].rearrange("p (h e d) -> p h e d", h=HP, e=2)
                    act.copy(VB[0:64, q, :, 0:HD], v[0:64, :, 0, :]).then_inc(bact.sem, 1)
                    act.copy(VB[64:128, q, :, VW:VW + HD], v[64:128, :, 1, :]).then_inc(bact.sem, 1)
                act.wait_ge(bpe.sem, bpe.at(r, "maskT"))
                act.copy(MT, B7[:, :].rearrange("p (k n) -> p k n", k=TT)).then_inc(bact.sem, 1)

            def b4(r):
                act.wait_ge(bpe.sem, bpe.at(r, "qkT"))
                act.copy(QT, B5[:, 0:D].rearrange("p (k n) -> p k n", k=KD)).then_inc(bact.sem, 1)
                act.wait_ge(bpe.sem, bpe.at(r, "mask"))
                act.copy(MS, B7[:, 0:SLOTS]).then_inc(bact.sem, 1)

            def b5(r):
                sc = SC.rearrange("p (h k) -> p h k", h=H)
                for g in range(2):
                    act.wait_ge(bdve.sem, bdve.at(r, f"sub{g}"))
                    sg = sc[:, 8 * g:8 * g + 8, 0:KC]
                    act.activation(sg, sg, ACT.Exp).then_inc(bact.sem, 1)

            def b6(r):
                act.wait_ge(bpe.sem, bpe.at(r, "at0"))
                act.copy(AT[:, 0:4, :], B6[:, :].rearrange("p (h n) -> p h n", h=4)).then_inc(bact.sem, 1)

            def b7(r):
                act.wait_ge(bpe.sem, bpe.at(r, "oT"))
                act.copy(HT, B6[:, 0:D].rearrange("p (k n) -> p k n", k=KD)).then_inc(bact.sem, 1)

            def b8(r):
                act.wait_ge(bpe.sem, bpe.at(r, "hn2T"))
                act.copy(HT, B6[:, 0:D].rearrange("p (k n) -> p k n", k=KD)).then_inc(bact.sem, 1)

            def b9(r):
                for g in range(2):
                    act.wait_ge(bpe.sem, bpe.at(r, "w1a" if g == 0 else "w1b"))
                    act.activation(GE[:, 4 * g:4 * g + 4, :], bank[6 + g][:, :].rearrange("p (h n) -> p h n", h=4),
                                   ACT.Gelu_apprx_tanh).then_inc(bact.sem, 1)

            def b13(r):
                act.wait_ge(bdve.sem, bdve.at(r))

            AT_STEP = {1: b1, 2: b2, 3: b3, 4: b4, 5: b5, 6: b6, 8: b7, 10: b8, 11: b9, 13: b13}

            def do(name, t, q, k):
                if name == "turn":
                    turn(t, k)
                    if is_row(t, 0) and k == 1:
                        setup_more()
                elif name == "u":
                    u(t, q, k)
                elif name == "g":
                    gate(t, q, k)
                elif name == "silu":
                    silu(t, k)
                    if is_row(t, 0) and k == 3:
                        setup_wout()
                elif name == "pre_n":
                    pre_n(t, q)
                elif name == "post_n":
                    post_n(t)
                elif name == "post_h":
                    post_h(t, q)
                elif name == "post_z":
                    post_z(t)
                elif name == "b":
                    bout_(t, q, k)
                elif name == "yhi":
                    yhi(t, k)
                    if is_row(t, 0) and k == 3:
                        trig()
                elif name == "slots" and k in AT_STEP:
                    AT_STEP[k](t)

            run_all(act, do)

        @block.gpsimd
        def _(pool):
            def root(out_, var, sig, rep, event, done, mean=None):
                pool.wait_ge(sig.sem, sig.at(rep, event))
                pool.tensor_tensor(out_, var, half[:, :], ALU.pow).then_inc(done.sem, 1)
                if mean is not None:
                    root_event, mean_event, mean_root, neg_mean = mean
                    pool.wait_ge(sig.sem, sig.at(rep, mean_event))
                    pool.wait_ge(done.sem, done.at(rep, root_event))
                    pool.tensor_tensor(mean_root, neg_mean, out_, ALU.mult).then_inc(done.sem, 1)

            def setup_pool():
                pool.wait_ge(set_act.sem, set_act.at(0, "wbc"))
                pool.tensor_tensor(WbcL[:, 0:2, :], rawbc[:, 0:2, :], WbcH[:, 0:2, :].bitcast(F32),
                                   ALU.subtract).then_inc(set_pool.sem, 1)

            def slo(t, c):
                pool.wait_ge(s_hi.sem, s_hi.at(t, f"r{c}"))
                pool.tensor_tensor(SL[:, c, :], S[:, c % 2, :], SH[:, c, :].bitcast(F32),
                                   ALU.subtract).then_inc(s_lo.sem, 1)

            def ylo(t, c):
                pool.wait_ge(y_hi.sem, y_hi.at(t, f"{c}"))
                pool.tensor_tensor(YL[:, c, :], Y[:, c % 2, :], YH[:, c, :].bitcast(F32),
                                   ALU.subtract).then_inc(y_lo.sem, 1)

            def post_a(t, q):
                if q == 0 and not is_row(t, 0):
                    if began((t // 2 if isinstance(t, int) else pair[0]) - 1):
                        pool.wait_ge(bpe.sem, bpe.at((t // 2 if isinstance(t, int) else pair[0]) - 1, "gather"))
                if is_row(t, 0):
                    pool.wait_ge(set_act.sem, set_act.at(0, "cos"))
                    pool.wait_ge(set_dve.sem, set_dve.at(0, "rows"))
                pool.tensor_copy(pay[:, q, :, C_COS:PAY], tokc[:, t, :, :]).then_inc(x1_out.sem, 1)
                root(rs[:, 1, :], ve[:, 1, :], post, t, "ave", roots_post,
                     mean=("a", "aneg", negr[:, 1, :], neg[:, 1, :]))

            def post_n(t, q):
                pool.wait_ge(xr_in, t * 16 + 16)
                for i in T4:
                    pool.wait_ge(scaled.sem, scaled.at(t, f"n{i}"))
                    pool.tensor_tensor(pay[:, q, i, 0:D], A[:, i, :], XR[:, i, :], ALU.add).then_inc(x1_out.sem, 1)

            def post_z(t, q):
                for i in T4:
                    pool.wait_ge(scaled.sem, scaled.at(t, f"z{i}"))
                    pool.tensor_tensor(A[:, i, :], A[:, i, :], pay[:, q, i, 0:D], ALU.add).then_inc(x1_out.sem, 1)

            pair = [None]

            def broot(r, event):
                pool.wait_ge(bdve.sem, bdve.at(r, event))
                pool.tensor_tensor(brs[:, :], bve[:, :], bhalf, ALU.pow).then_inc(bpool.sem, 1)

            def b1(r):
                pool.wait_ge(bdve.sem, bdve.at(r, "idx"))
                pool.tensor_tensor(spare[:, 2:3], bhalf, bhalf, ALU.mult)
                pool.indirect_dma_start(MR, None, mask_rows,
                                        bass.IndirectOffsetOnAxis(ap=idx_of(r, 0), axis=0)).then_inc(mask_in, 16)

            def b13(r):
                broot(r, "fve")
                pool.wait_ge(bdve.sem, bdve.at(r, "os"))
                pool.wait_ge(out_stored, (r * 2 + 1) * 16 + 16)
                pool.tensor_tensor(spare[:, 1:2], bhalf, bhalf, ALU.mult)
                pool.indirect_dma_start(out_flat, bass.IndirectOffsetOnAxis(ap=idx_of(r, 1), axis=0),
                                        OS, None).then_inc(scattered, 16)

            def do(name, t, q, k):
                if name == "pre_s":
                    root(rs[:, 0, :], ve[:, 0, :], pre, t, "ve", roots, mean=("x", "neg", negr[:, 0, :], neg[:, 0, :]))
                elif name == "turn" and k == 1 and is_row(t, 0):
                    setup_pool()
                elif name == "silu":
                    slo(t, k)
                elif name == "yhi":
                    ylo(t, k)
                elif name == "post_a":
                    post_a(t, q)
                elif name == "post_n":
                    post_n(t, q)
                elif name == "post_x":
                    root(pay[:, q, :, C_R], ve[:, 2, :], post, t, "xve", roots_post,
                         mean=("x1", "xneg", pay[:, q, :, C_MR], neg[:, 2, :]))
                    root(rs[:, 3, :], ve[:, 3, :], post, t, "hve", roots_post)
                    root(pay[:, q, :, C_R2], ve[:, 4, :], post, t, "rve", roots_post)
                elif name == "post_z":
                    post_z(t, q)
                elif name == "slots":
                    if k == 1:
                        pair[0] = t + 1
                        b1(t)
                    elif k == 9:
                        broot(t, "ss2ve")
                    elif k == 13:
                        b13(t)

            pool.wait_ge(set_dve.sem, set_dve.at(0, "half"))
            run_all(pool, do)

        @block.vector
        def _(dve):
            n_set = [0]

            def setup(ins):
                n_set[0] += 1
                ins.then_inc(set_dve.sem, 1)
                dve.wait_ge(set_dve.sem, n_set[0])

            setup(dve.memset(half[:, :], -0.5))

            def setup_win():
                dve.wait_ge(s_win, 16)
                setup(dve.tensor_copy(WinH[:, 1, :], rawin[:, 1, :]))
                dve.wait_ge(set_act.sem, set_act.at(0, "win"))
                setup(dve.tensor_tensor(WinL[:, :, :], rawin, WinH[:, :, :].bitcast(F32), ALU.subtract))
                dve.wait_ge(s_vec, 16 * 11)
                setup(dve.tensor_copy(posf[0:16, :], posi[0:16, :]))

            def setup_first():
                dve.wait_ge(set_pe.sem, set_pe.at(0))
                setup(dve.tensor_copy(cols[:, :], B5[:, 0:R_ALL]))
                setup(dve.tensor_copy(tpos[:, 0:NP_ROWS * TT], B5[:, 32:48]))
                setup(dve.memset(U[:, :, 0:TAPS - 1], 0.0))
                setup(dve.tensor_tensor(vbias[:, :], cols[:, R_BIN:R_BIN + KI], convw[:, :, TAPS - 1], ALU.mult))
                setup(dve.tensor_tensor(vbias[:, :], vbias[:, :], cols[:, R_CB:R_CB + KI], ALU.add))
                dve.wait_ge(s_wbc, 16)
                setup(dve.tensor_copy(WbcH[:, 2:, :], rawbc[:, 2:, :]))
                setup(dve.tensor_tensor(WbcL[:, 2:, :], rawbc[:, 2:, :], WbcH[:, 2:, :].bitcast(F32), ALU.subtract))

            def setup_more():
                dve.wait_ge(set_act.sem, set_act.at(0, "edecay"))
                setup(dve.tensor_scalar(decay[:, :], decay[:, :], 1.0, None, ALU.add))
                setup(dve.reciprocal(decay[:, :], decay[:, :]))
                dve.wait_ge(set_act.sem, set_act.at(0, "wout"))
                setup(dve.scalar_tensor_tensor(WoutL[:, :, :].rearrange("p k n -> p (k n)"),
                                               big[:, 6144:7168], 0.5,
                                               WoutH[:, :, :].rearrange("p k n -> p (k n)").bitcast(F32),
                                               ALU.mult, ALU.subtract))

            def setup_tokens():
                dve.wait_ge(s_k, 16)
                last_row = tpos[:, (NP_ROWS - 1) * TT:NP_ROWS * TT].unsqueeze(1)
                rest = tpos[:, NP_ROWS * TT:].rearrange("p (b i) -> p b i", i=TT)
                setup(dve.tensor_copy(rest, last_row.to_broadcast([P, NB - NP_ROWS, TT])))
                pb = tpos[:, :].unsqueeze(2).to_broadcast([P, NB * TT, HALF])
                fb = K[:, K_INV:K_INV + HALF].unsqueeze(1).to_broadcast([P, NB * TT, HALF])
                setup(dve.tensor_tensor(ang, pb, fb, ALU.mult))
                for shift, dst in ((0.25, red), (0.0, ang)):
                    setup(dve.tensor_scalar(trn, ang, 1.0 / TWO_PI, shift, ALU.mult, ALU.add))
                    setup(dve.tensor_scalar(trn, trn, MAGIC, None, ALU.add))
                    setup(dve.tensor_scalar(trn, trn, MAGIC, None, ALU.subtract))
                    src = ang
                    for part in (PI_A, PI_B, PI_C, PI_D):
                        setup(dve.scalar_tensor_tensor(dst, trn, -part, src, ALU.mult, ALU.add))
                        src = dst
                setup(dve.tensor_scalar(red, red, float(np.pi / 2), None, ALU.add))
                setup(dve.tensor_copy(tokc[:, :, :, C_MROW - C_COS],
                                      K[:, K_MROW:K_MROW + NB * TT].rearrange("p (b i) -> p b i", i=TT)))
                setup(dve.tensor_copy(tokc[:, :, :, C_OROW - C_COS],
                                      K[:, K_OROW:K_OROW + NB * TT].rearrange("p (b i) -> p b i", i=TT)))

            def setup_slots():
                dve.wait_ge(s_wb, 16 * 6)
                for k in range(KD):
                    setup(dve.tensor_scalar(Wqkv[:, k, :], Wqkv[:, k, :], cols[:, R_LN1 + k:R_LN1 + k + 1], None, ALU.mult))
                for k in range(KD):
                    setup(dve.tensor_scalar(W1[:, k, :], W1[:, k, :], cols[:, R_LN2 + k:R_LN2 + k + 1], None, ALU.mult))
                dve.wait_ge(set_pool.sem, set_pool.at(0))
                setup(dve.memset(VB, 0.0))
                setup(dve.memset(VB[0:64, :, :, HD:HD + 1], 1.0))
                setup(dve.memset(VB[64:128, :, :, VW + HD:VW + HD + 1], 1.0))
                setup(dve.memset(SC, 0.0))

            def carry():
                dve.memset(spare[:, 0:1], 0.0)

            def statistics(which, sig, t, tag, src, eps, name, x1=False):
                for i in T4:
                    if x1:
                        dve.wait_ge(x1_out.sem, x1_out.at(t, f"x1{i}"))
                    dve.bn_stats(stats[:, which, i, :], src(i)).then_inc(sig.sem, 1)
                moments(which, sig, t, tag, eps, name)

            def moments(which, sig, t, tag, eps, name):
                dve.wait_ge(sig.sem, sig.at(t, f"{tag[0]}3"))
                carry()
                for i in T4:
                    dve.bn_aggr(mv[:, which, i, :], stats[:, which, i, :]).then_inc(sig.sem, 1)
                dve.wait_ge(sig.sem, sig.at(t, f"{tag[1]}3"))
                dve.tensor_scalar(ve[:, which, :], mv[:, which, :, 1], eps, None, ALU.add).then_inc(sig.sem, 1)
                dve.tensor_scalar(neg[:, which, :], mv[:, which, :, 0], -1.0, None, ALU.mult).then_inc(sig.sem, 1)

            def pre_s(t, q):
                dve.wait_ge(x_in, t * 16 + 16)
                statistics(0, pre, t, ("st", "ag"), lambda i: X[:, q, i, :], 1e-5, "ve")

            def turn(t, k):
                dve.wait_ge(ln_hi.sem, ln_hi.at(t, f"k{k}"))
                dve.tensor_tensor(LNL[:, k, :], turn_bank(t, k)[:, :], LNH[:, k, :].bitcast(F32),
                                  ALU.subtract).then_inc(ln_lo.sem, 1)

            def convolve(t, c):
                for j in range(TAPS - 1):
                    if j == 0:
                        dve.wait_ge(u_out.sem, u_out.at(t, f"v{c}"))
                    else:
                        dve.wait_ge(conv.sem, conv.at(t, f"{c}{j - 1}"))
                    dve.scalar_tensor_tensor(V[:, c % 2, :], U[:, c % 2, j:j + NT], convw[:, c, j:j + 1],
                                             V[:, c % 2, :], ALU.mult, ALU.add).then_inc(conv.sem, 1)

            def scan(t, c):
                dve.wait_ge(b_out_.sem, b_out_.at(t, f"{c}"))
                dve.tensor_tensor_scan(Y[:, c % 2, :], decay[:, c:c + 1].to_broadcast([P, NT]), Y[:, c % 2, :], 0.0,
                                       ALU.mult, ALU.add).then_inc(ssm.sem, 1)

            def c_and_gate(t, q, c):
                dve.wait_ge(wbc.sem, wbc.at(t, f"c{c}"))
                dve.wait_ge(ssm.sem, ssm.at(t, f"scan{c}"))
                dve.scalar_tensor_tensor(Y[:, c % 2, :], bank[2 * b_pair(c, q) + 1][:, :],
                                         cols[:, R_BBC + KI + c:R_BBC + KI + c + 1], Y[:, c % 2, :],
                                         ALU.add, ALU.mult).then_inc(ssm.sem, 1)
                dve.wait_ge(g_out.sem, g_out.at(t, f"g{c}"))
                dve.wait_ge(ssm.sem, ssm.at(t, f"c{c}"))
                dve.scalar_tensor_tensor(Y[:, c % 2, :], G[:, c, :], 1.0, Y[:, c % 2, :],
                                         ALU.add, ALU.mult).then_inc(ssm.sem, 1)

            def post_a(t, q):
                if is_row(t, 0):
                    dve.wait_ge(set_act.sem, set_act.at(0, "cos"))
                if began(t - 1):
                    dve.wait_ge(out_stored, (t - 1) * 16 + 16)
                for i in T4:
                    if i % 2 == 0:
                        dve.wait_ge(wout.sem, wout.at(t, f"{i + 1}"))
                    dve.tensor_tensor(A[:, i, :], bank[2 * out_pair(q) + i // 2][:, (i % 2) * D:(i % 2 + 1) * D], bout[:, :],
                                      ALU.add).then_inc(post.sem, 1)
                    if i % 2 == 1:
                        dve.wait_ge(post.sem, post.at(t, f"a{i}"))
                        for k in (i - 1, i):
                            dve.bn_stats(stats[:, 1, k, :], A[:, k, :]).then_inc(post.sem, 1)
                moments(1, post, t, ("as", "aa"), 1e-5, "ave")

            def post_x(t, q):
                statistics(2, post, t, ("xs", "xg"), lambda i: pay[:, q, i, 0:D], 1e-5, "xve", x1=True)
                dve.wait_ge(roots_post.sem, roots_post.at(t, "x1"))
                dve.tensor_tensor(ve[:, 4, :], mv[:, 2, :, 1], pay[:, q, :, C_R], ALU.mult).then_inc(post.sem, 1)
                dve.wait_ge(post.sem, post.at(t, "v1"))
                dve.tensor_tensor(ve[:, 4, :], ve[:, 4, :], pay[:, q, :, C_R], ALU.mult).then_inc(post.sem, 1)
                dve.wait_ge(post.sem, post.at(t, "v2"))
                dve.tensor_scalar(ve[:, 3, :], ve[:, 4, :], 1e-5, None, ALU.add).then_inc(post.sem, 1)
                dve.wait_ge(post.sem, post.at(t, "hve"))
                dve.tensor_scalar(ve[:, 4, :], ve[:, 4, :], 1e-6, None, ALU.add).then_inc(post.sem, 1)

            def post_h(t, q):
                for i in T4:
                    dve.wait_ge(scaled.sem, scaled.at(t, f"h{i}"))
                    dve.tensor_tensor_reduce(out=A[:, i, :], in0=HB[:, i, :], in1=rw[:, :], scale=1.0, scalar=0.0,
                                             op0=ALU.mult, op1=ALU.add, accum_out=rank[:, i:i + 1]).then_inc(post.sem, 1)
                dve.wait_ge(post.sem, post.at(t, "w3"))
                dve.tensor_scalar(pay[:, q, :, C_W], rank[:, :], rb[:, 0:1], None, ALU.add).then_inc(post.sem, 1)

            def rank_(t, q, i):
                w = pay[:, q, i, C_W:C_W + 1] if i < TT else None
                if i == 0:
                    dve.wait_ge(wrow.sem, wrow.at(t))
                    dve.wait_ge(scaled.sem, scaled.at(t))
                if i < TT:
                    if i > 0:
                        dve.wait_ge(ranked.sem, ranked.at(t, f"nge{i - 1}"))
                    dve.tensor_scalar(junk[:, :], TURN[:, :], w, None, ALU.is_ge, ALU.add,
                                      accum_out=nge[:, i:i + 1]).then_inc(ranked.sem, 1)
                    n = NT - P * i
                    if i > 0:
                        dve.wait_ge(ranked.sem, ranked.at(t, f"tie{i - 1}"))
                    dve.scalar_tensor_tensor(junk_tie[:, 0:n], TURN[:, P * i:NT], w, K[:, K_TRI:K_TRI + n],
                                             ALU.is_equal, ALU.mult, accum_out=tie[:, i:i + 1]).then_inc(ranked.sem, 1)
                    return
                dve.wait_ge(ranked.sem, ranked.at(t, f"tie{TT - 1}"))
                dve.tensor_tensor(rank[:, :], nge[:, :], tie[:, :], ALU.subtract).then_inc(ranked.sem, 1)
                dve.tensor_scalar(pay[:, q, :, C_UNSEL], nge[:, :], float(KC), None, ALU.is_gt).then_inc(ranked.sem, 1)
                dve.wait_ge(ranked.sem, ranked.at(t, "rank"))
                for k in T4:
                    dve.tensor_scalar(onehot[:, q, k, :], K[:, K_IOTA:K_IOTA + SLOTS], rank[:, k:k + 1], None,
                                      ALU.is_equal).then_inc(ranked.sem, 1)

            def link(ins, r, event):
                ins.then_inc(bdve.sem, 1)
                dve.wait_ge(bdve.sem, bdve.at(r, event))

            def b1(r):
                dve.wait_ge(bact.sem, bact.at(r, "gs"))
                dve.tensor_scalar(HS, GS[:, 0:D], GS[:, C_R:C_R + 1], GS[:, C_MR:C_MR + 1], ALU.mult,
                                  ALU.add).then_inc(bdve.sem, 1)
                dve.tensor_copy(idx_of(r, None), GS[:, C_MROW:C_OROW + 1]).then_inc(bdve.sem, 1)
                dve.wait_ge(bdve.sem, bdve.at(r, "hs"))
                link(dve.tensor_scalar(HN, HS, GS[:, C_R2:C_R2 + 1], None, ALU.mult), r, "hn")

            def b3(r):
                dve.wait_ge(bpe.sem, bpe.at(r, "qk"))
                x4 = B5[:, :].rearrange("p (h e f) -> p h e f", e=2, f=HALF)
                o4 = QK.rearrange("p (h e f) -> p h e f", e=2, f=HALF)
                r4 = RT.rearrange("p (h e f) -> p h e f", e=2, f=HALF)
                cos = GS[:, C_COS:C_COS + HALF]
                sin = GS[:, C_SIN:C_SIN + HALF].unsqueeze(1).to_broadcast([P, 2 * H, HALF])
                cos4 = cos.unsqueeze(1).unsqueeze(1).to_broadcast([P, 2 * H, 2, HALF])
                dve.tensor_tensor(o4, x4, cos4, ALU.mult).then_inc(bdve.sem, 1)
                dve.tensor_tensor(r4[:, :, 0, :], x4[:, :, 1, :], sin, ALU.mult).then_inc(bdve.sem, 1)
                dve.tensor_tensor(r4[:, :, 1, :], x4[:, :, 0, :], sin, ALU.mult).then_inc(bdve.sem, 1)
                dve.wait_ge(bdve.sem, bdve.at(r, "r2"))
                dve.tensor_tensor(o4[:, :, 0, :], o4[:, :, 0, :], r4[:, :, 0, :], ALU.subtract).then_inc(bdve.sem, 1)
                dve.wait_ge(bdve.sem, bdve.at(r, "r3"))
                dve.tensor_tensor(o4[:, :, 1, :], o4[:, :, 1, :], r4[:, :, 1, :], ALU.add).then_inc(bdve.sem, 1)

            def b4(r):
                dve.wait_ge(bpe.sem, bpe.at(r, "qkT"))
                dve.wait_ge(bact.sem, bact.at(r, "qT"))
                head = K[:, K_HEAD:K_HEAD + 8].unsqueeze(2).to_broadcast([P, 8, SLOTS])
                for g, q in ((g, q) for g in range(2) for q in range(2)):
                    kt = B5[:, (2 + g) * P + q * SLOTS:(2 + g) * P + (q + 1) * SLOTS].unsqueeze(1) \
                        .to_broadcast([P, 8, SLOTS])
                    dve.tensor_tensor(KB[g].rearrange("p (q h n) -> p q h n", q=2, h=8)[:, q], kt, head,
                                      ALU.mult).then_inc(bdve.sem, 1)

            def b5(r):
                dve.wait_ge(bact.sem, bact.at(r, "ms"))
                m = MS[:, 0:KC].unsqueeze(1).to_broadcast([P, 8, KC])
                sc = [SC.rearrange("p (h k) -> p h k", h=H)[:, 8 * g:8 * g + 8, 0:KC] for g in range(2)]
                mg = [mx[:, 8 * g:8 * g + 8] for g in range(2)]

                def masked(g):
                    dve.wait_ge(bpe.sem, bpe.at(r, f"s{g}"))
                    s = bank[6 + g][:, :].rearrange("p (h k) -> p h k", h=8)[:, :, 0:KC]
                    dve.scalar_tensor_tensor(sc[g], s, HD ** -0.5, m, ALU.mult, ALU.add).then_inc(bdve.sem, 1)

                def maximum(g):
                    dve.wait_ge(bdve.sem, bdve.at(r, f"sc{g}"))
                    dve.tensor_reduce(mg[g], sc[g], AX.X, ALU.max).then_inc(bdve.sem, 1)

                def below_maximum(g):
                    dve.wait_ge(bdve.sem, bdve.at(r, f"max{g}"))
                    dve.tensor_tensor(sc[g], sc[g], mg[g].unsqueeze(2).to_broadcast([P, 8, KC]),
                                      ALU.subtract).then_inc(bdve.sem, 1)

                masked(0)
                maximum(0)
                masked(1)
                below_maximum(0)
                maximum(1)
                below_maximum(1)

            def b6(r):
                dve.wait_ge(bpe.sem, bpe.at(r, "at1"))
                dve.tensor_copy(AT[:, 4:8, :], B7[:, :].rearrange("p (h n) -> p h n", h=4)).then_inc(bdve.sem, 1)

            def b7(r):
                dve.wait_ge(bpe.sem, bpe.at(r, "pv"))
                o = B5[:, 0:H * VW].rearrange("p (h e) -> p h e", e=VW)
                link(dve.reciprocal(rden[:, :], o[:, :, HD]), r, "rden")
                link(dve.tensor_tensor(HN.rearrange("p (h e) -> p h e", e=HD), o[:, :, 0:HD],
                                       rden[:, :].unsqueeze(2).to_broadcast([P, H, HD]), ALU.mult), r, "on")

            def b9(r):
                dve.wait_ge(bpe.sem, bpe.at(r, "wo"))
                link(dve.tensor_tensor(X1S, B5[:, 0:D], HS, ALU.add), r, "x1s")
                link(dve.tensor_tensor_reduce(out=HN, in0=X1S, in1=X1S, scale=1.0, scalar=0.0, op0=ALU.mult,
                                              op1=ALU.add, accum_out=bss[:, :]), r, "ss2")
                link(dve.tensor_scalar(bve[:, :], bss[:, :], 1.0 / D, 1e-6, ALU.mult, ALU.add), r, "ss2ve")
                dve.wait_ge(bpool.sem, bpool.at(r, "hn2"))
                link(dve.tensor_scalar(HN, X1S, brs[:, 0:1], None, ALU.mult), r, "hn2")

            def b12(r):
                dve.tensor_tensor(bws[:, :], GS[:, C_W:C_W + 1], K[:, K_SEL:K_SEL + 1], ALU.mult).then_inc(bdve.sem, 1)
                dve.tensor_scalar(FS, HS, GS[:, C_UNSEL:C_UNSEL + 1], None, ALU.mult).then_inc(bdve.sem, 1)
                dve.wait_ge(bpe.sem, bpe.at(r, "w2"))
                link(dve.tensor_tensor(X1S, B5[:, 0:D], X1S, ALU.add), r, "x2")
                dve.scalar_tensor_tensor(FS, X1S, bws[:, 0:1], FS, ALU.mult, ALU.add).then_inc(bdve.sem, 1)

            def b13(r):
                dve.wait_ge(bdve.sem, bdve.at(r, "f"))
                dve.bn_stats(bst[:, :], FS).then_inc(bdve.sem, 1)
                dve.wait_ge(bdve.sem, bdve.at(r, "fst"))
                carry()
                link(dve.bn_aggr(bmv[:, :], bst[:, :]), r, "fag")
                link(dve.tensor_scalar(bve[:, :], bmv[:, 1:2], 1e-5, None, ALU.add), r, "fve")
                dve.wait_ge(bpool.sem, bpool.at(r, "f"))
                link(dve.tensor_scalar(FS, FS, bmv[:, 0:1], brs[:, 0:1], ALU.subtract, ALU.mult), r, "fn")
                dve.tensor_tensor(OS, FS, GS[:, 0:D], ALU.add).then_inc(bdve.sem, 1)

            def b14(r):
                dve.wait_ge(scattered, r * 16 + 16)

            AT_STEP = {1: b1, 3: b3, 4: b4, 5: b5, 6: b6, 7: b7, 9: b9, 12: b12, 13: b13, 14: b14}
            pair = [None]

            def do(name, t, q, k):
                if name == "pre_s":
                    pre_s(t, q)
                    if is_row(t, 0):
                        setup_win()
                elif name == "turn":
                    turn(t, k)
                    if is_row(t, 0) and k == 1:
                        setup_first()
                    if is_row(t, 1) and k == 1:
                        setup_tokens()
                elif name == "u":
                    convolve(t, k)
                elif name == "b":
                    if is_row(t, 0) and k == 0:
                        setup_more()
                    if is_row(t, 1) and k == 0:
                        setup_slots()
                    scan(t, k)
                elif name == "c":
                    c_and_gate(t, q, k)
                elif name == "post_a":
                    post_a(t, q)
                elif name == "post_x":
                    post_x(t, q)
                elif name == "post_h":
                    post_h(t, q)
                elif name == "rank":
                    rank_(t, q, k)
                elif name == "slots" and k in AT_STEP:
                    AT_STEP[k](t)

            run_all(dve, do)



_INS = ["L0_attn_x", "L0_attn_W_in", "L0_attn_b_in", "L0_attn_conv_w", "L0_attn_conv_b", "L0_attn_W_bc",
        "L0_attn_b_bc", "L0_attn_log_decay", "L0_attn_W_out", "L0_attn_b_out", "L0_ffn_attention_mask",
        "L0_ffn_position_ids", "L0_ffn_router_w", "L0_ffn_router_b", "L0_ffn_wq", "L0_ffn_wk", "L0_ffn_wv",
        "L0_ffn_wo", "L0_ffn_w1", "L0_ffn_w2", "L0_ffn_ln1", "L0_ffn_ln2"]


def kernel(**inputs):
    import concourse.bacc as bacc
    from concourse.bass_utils import run_bass_kernel_spmd

    nc = bacc.Bacc("TRN2", target_bir_lowering=False, num_devices=1)
    arrays = {f"in_{n}_dram": np.ascontiguousarray(inputs[n]) for n in _INS}
    arrays["in_shape_constants_dram"] = shape_constants()
    args = [nc.dram_tensor(n, a.shape, mybir.dt.from_np(a.dtype), kind="ExternalInput").ap()
            for n, a in arrays.items()]
    out = nc.dram_tensor("out_0_dram", (NB, NT, D), F32, kind="ExternalOutput").ap()
    build(nc, *args, out)
    r = run_bass_kernel_spmd(nc, [arrays], core_ids=[0])
    return r.results[0]["out_0_dram"]
```
